# Optimizing a Trainium2 kernel written in Bass

```python
import numpy as np
import jax
import jax.numpy as jnp

def _softmax(x, axis=-1):
    return jax.nn.softmax(x, axis=axis)

def _gelu(x):
    return jax.nn.gelu(x, approximate=True)

def _silu(x):
    return jax.nn.silu(x)

def _sigmoid(x):
    return jax.nn.sigmoid(x)

def _layernorm(x, axis=-1, eps=1e-05):
    m = jnp.mean(x, axis=axis, keepdims=True)
    v = jnp.var(x, axis=axis, keepdims=True)
    return (x - m) / jnp.sqrt(v + eps)

def _scatter_add(tgt, idx, src, axis=0):
    return tgt.at[idx].add(src)

def _segment_sum(src, seg, n):
    return jax.ops.segment_sum(src, seg, n)
kernel_name = 'mk_decoder_postln_d1_seqx_r4_850204'

def setup_inputs(seed: int=0):
    np.random.seed(seed)
    _w = jnp.asarray

    def _rec_inputs():
        import jax
        import jax.numpy as jnp
        _rk = jax.random.key(seed)
        x = -0.0002928 + 1 * jax.random.normal(jax.random.fold_in(_rk, 1), (2, 1024, 256), jnp.float32)
        _lenS = 1024 - jax.random.randint(jax.random.fold_in(_rk, 7), (2,), 0, max(1, 1024 // 4) + 1, jnp.int32)
        _lenS2 = 77 - jax.random.randint(jax.random.fold_in(_rk, 8), (2,), 0, max(1, 77 // 4) + 1, jnp.int32)
        _ctx_1024P = jax.random.normal(jax.random.fold_in(_rk, 11), (2, 16, 256), jnp.float32)
        _ctx_1024c = jax.random.dirichlet(jax.random.fold_in(_rk, 511), 0.3 * jnp.ones((16,), jnp.float32), (2, 77))
        _ctx_1024t = jnp.einsum('bsk,bkd->bsd', _ctx_1024c, _ctx_1024P)
        _ctx_1024t = _ctx_1024t * jax.lax.rsqrt(jnp.mean(jnp.square(_ctx_1024t)) + 1e-12) * 0.953939
        ctx_1024 = -1.39393e-06 + 0.999914 * (_ctx_1024t + 0.3 * jax.random.normal(jax.random.fold_in(_rk, 611), (2, 77, 256), jnp.float32))
        return (x, ctx_1024)
    x, ctx_1024 = _rec_inputs()

    def _L0_attn_setup():
        import jax, jax.numpy as jnp
        import numpy as np
        B, L, H, N = (4, 1024, 256, 64)
        LN_EPS = 1e-05

        def _s4d_kernel(log_A_real, A_imag, C_re, C_im, log_dt, length):
            A = -jnp.exp(log_A_real) + 1j * A_imag
            dt = jnp.exp(log_dt)[:, None]
            dtA = dt * A
            C = C_re + 1j * C_im
            Ct = C * (jnp.exp(dtA) - 1.0) / A
            l = jnp.arange(length, dtype=jnp.float32)
            V = jnp.exp(dtA[:, :, None] * l[None, None, :])
            K = 2.0 * jnp.real(jnp.einsum('hn,hnl->hl', Ct, V))
            return K
        key = jax.random.key(seed)
        ks = jax.random.split(key, 6)
        x = jax.random.normal(ks[0], (B, L, H), dtype=jnp.float32)
        log_A_real = jnp.log(0.5 * jnp.ones((H, N), dtype=jnp.float32))
        A_imag = jnp.broadcast_to(jnp.pi * jnp.arange(N, dtype=jnp.float32), (H, N))
        C_re = jax.random.normal(ks[1], (H, N), dtype=jnp.float32) * 0.5
        C_im = jax.random.normal(ks[2], (H, N), dtype=jnp.float32) * 0.5
        u = jax.random.uniform(ks[3], (H,), dtype=jnp.float32)
        log_dt = u * (jnp.log(0.1) - jnp.log(0.001)) + jnp.log(0.001)
        D = jax.random.normal(ks[4], (H,), dtype=jnp.float32)
        ln_w = jnp.ones((H,), dtype=jnp.float32)
        ln_b = jnp.zeros((H,), dtype=jnp.float32)
        return {'x': x, 'log_A_real': log_A_real, 'A_imag': A_imag, 'C_re': C_re, 'C_im': C_im, 'log_dt': log_dt, 'D': D, 'ln_w': ln_w, 'ln_b': ln_b}
    _L0_attn_all = _L0_attn_setup()
    _L0_attn_in = {k: v for k, v in _L0_attn_all.items() if k in ('log_A_real', 'A_imag', 'C_re', 'C_im', 'log_dt', 'D', 'ln_w', 'ln_b')}
    del _L0_attn_all

    def _L0_xattn_setup():
        import jax, jax.numpy as jnp
        import numpy as np
        DIM = 256
        NUM_HEADS = 16
        HEAD_DIM = DIM // NUM_HEADS
        key = jax.random.key(seed)
        ks = jax.random.split(key, 11)
        B, N, C = (2, 512, DIM)
        s = 1.0 / np.sqrt(C)
        inp = {'q': jax.random.normal(ks[0], (B, N, C), jnp.float32), 'k': jax.random.normal(ks[1], (B, N, C), jnp.float32), 'v': jax.random.normal(ks[2], (B, N, C), jnp.float32), 'Wq': jax.random.normal(ks[3], (C, C), jnp.float32) * s, 'bq': jnp.zeros((C,), jnp.float32), 'Wk': jax.random.normal(ks[4], (C, C), jnp.float32) * s, 'bk': jnp.zeros((C,), jnp.float32), 'Wv': jax.random.normal(ks[5], (C, C), jnp.float32) * s, 'bv': jnp.zeros((C,), jnp.float32), 'Wo': jax.random.normal(ks[6], (C, C), jnp.float32) * s, 'bo': jnp.zeros((C,), jnp.float32)}
        return inp
    _L0_xattn_all = _L0_xattn_setup()
    _L0_xattn_in = {k: v for k, v in _L0_xattn_all.items() if k in ('Wq', 'bq', 'Wk', 'bk', 'Wv', 'bv', 'Wo', 'bo')}
    del _L0_xattn_all

    def _L0_ffn_setup():
        import jax, jax.numpy as jnp
        import numpy as np
        B, T, D = (2, 512, 256)
        DCD = 1024
        RET = 128
        NEXP = 1024
        NKEYS = 64
        H = 4
        KPH = 8
        key = jax.random.key(seed)
        ks = jax.random.split(key, 10)
        s = lambda k, shape, scale: jax.random.normal(k, shape, jnp.float32) * scale
        return {'hidden_states': jax.random.normal(ks[0], (B, T, D), jnp.float32), 'Wg': s(ks[1], (D, DCD), 0.02), 'bg': jnp.zeros((DCD,), jnp.float32), 'Wu': s(ks[2], (D, DCD), 0.02), 'bu': jnp.zeros((DCD,), jnp.float32), 'Wd': s(ks[3], (DCD, D), 0.02), 'bd': jnp.zeros((D,), jnp.float32), 'Wq': s(ks[4], (D, RET * H), 0.02), 'keys': s(ks[5], (H, NKEYS, 2, RET // 2), 0.02), 'down_embed': s(ks[6], (NEXP, D), 0.02), 'up_embed': s(ks[7], (NEXP, D), 0.02)}
    _L0_ffn_all = _L0_ffn_setup()
    _L0_ffn_in = {k: v for k, v in _L0_ffn_all.items() if k in ('Wg', 'bg', 'Wu', 'bu', 'Wd', 'bd', 'Wq', 'keys', 'down_embed', 'up_embed')}
    del _L0_ffn_all
    return {'x': x, 'ctx_1024': ctx_1024, 'L0_attn_log_A_real': _L0_attn_in['log_A_real'], 'L0_attn_A_imag': _L0_attn_in['A_imag'], 'L0_attn_C_re': _L0_attn_in['C_re'], 'L0_attn_C_im': _L0_attn_in['C_im'], 'L0_attn_log_dt': _L0_attn_in['log_dt'], 'L0_attn_D': _L0_attn_in['D'], 'L0_attn_ln_w': _L0_attn_in['ln_w'], 'L0_attn_ln_b': _L0_attn_in['ln_b'], 'L0_xattn_Wq': _L0_xattn_in['Wq'], 'L0_xattn_bq': _L0_xattn_in['bq'], 'L0_xattn_Wk': _L0_xattn_in['Wk'], 'L0_xattn_bk': _L0_xattn_in['bk'], 'L0_xattn_Wv': _L0_xattn_in['Wv'], 'L0_xattn_bv': _L0_xattn_in['bv'], 'L0_xattn_Wo': _L0_xattn_in['Wo'], 'L0_xattn_bo': _L0_xattn_in['bo'], 'L0_ffn_Wg': _L0_ffn_in['Wg'], 'L0_ffn_bg': _L0_ffn_in['bg'], 'L0_ffn_Wu': _L0_ffn_in['Wu'], 'L0_ffn_bu': _L0_ffn_in['bu'], 'L0_ffn_Wd': _L0_ffn_in['Wd'], 'L0_ffn_bd': _L0_ffn_in['bd'], 'L0_ffn_Wq': _L0_ffn_in['Wq'], 'L0_ffn_keys': _L0_ffn_in['keys'], 'L0_ffn_down_embed': _L0_ffn_in['down_embed'], 'L0_ffn_up_embed': _L0_ffn_in['up_embed']}

def reference(x, ctx_1024, L0_attn_log_A_real, L0_attn_A_imag, L0_attn_C_re, L0_attn_C_im, L0_attn_log_dt, L0_attn_D, L0_attn_ln_w, L0_attn_ln_b, L0_xattn_Wq, L0_xattn_bq, L0_xattn_Wk, L0_xattn_bk, L0_xattn_Wv, L0_xattn_bv, L0_xattn_Wo, L0_xattn_bo, L0_ffn_Wg, L0_ffn_bg, L0_ffn_Wu, L0_ffn_bu, L0_ffn_Wd, L0_ffn_bd, L0_ffn_Wq, L0_ffn_keys, L0_ffn_down_embed, L0_ffn_up_embed):
    import jax
    import jax.numpy as jnp

    def _L0_attn_ref(x, log_A_real, A_imag, C_re, C_im, log_dt, D, ln_w, ln_b):
        import jax, jax.numpy as jnp
        import numpy as np
        B, L, H, N = (4, 1024, 256, 64)
        LN_EPS = 1e-05

        def _s4d_kernel(log_A_real, A_imag, C_re, C_im, log_dt, length):
            A = -jnp.exp(log_A_real) + 1j * A_imag
            dt = jnp.exp(log_dt)[:, None]
            dtA = dt * A
            C = C_re + 1j * C_im
            Ct = C * (jnp.exp(dtA) - 1.0) / A
            l = jnp.arange(length, dtype=jnp.float32)
            V = jnp.exp(dtA[:, :, None] * l[None, None, :])
            K = 2.0 * jnp.real(jnp.einsum('hn,hnl->hl', Ct, V))
            return K
        b, length, h = x.shape
        K = _s4d_kernel(log_A_real, A_imag, C_re, C_im, log_dt, length)
        n = 2 * length
        Xf = jnp.fft.rfft(x, n=n, axis=1)
        Kf = jnp.fft.rfft(K, n=n, axis=1)
        y = jnp.fft.irfft(Xf * Kf.T[None, :, :], n=n, axis=1)[:, :length, :]
        z = y + x * D[None, None, :]
        r = x + z
        mu = jnp.mean(r, axis=-1, keepdims=True)
        var = jnp.var(r, axis=-1, keepdims=True)
        out = (r - mu) * jax.lax.rsqrt(var + LN_EPS) * ln_w + ln_b
        return out

    def _L0_xattn_ref(q, k, v, Wq, bq, Wk, bk, Wv, bv, Wo, bo):
        import jax, jax.numpy as jnp
        import numpy as np
        DIM = 256
        NUM_HEADS = 16
        HEAD_DIM = DIM // NUM_HEADS
        B, Nq, C = q.shape
        Nkv = k.shape[1]
        H, D = (NUM_HEADS, HEAD_DIM)
        qh = (q @ Wq.T + bq).reshape(B, Nq, H, D).transpose(0, 2, 1, 3)
        kh = (k @ Wk.T + bk).reshape(B, Nkv, H, D).transpose(0, 2, 1, 3)
        vh = (v @ Wv.T + bv).reshape(B, Nkv, H, D).transpose(0, 2, 1, 3)
        scale = D ** (-0.5)
        attn = jax.nn.softmax(jnp.einsum('bhqd,bhkd->bhqk', qh, kh) * scale, axis=-1)
        out = jnp.einsum('bhqk,bhkd->bhqd', attn, vh)
        out = out.transpose(0, 2, 1, 3).reshape(B, Nq, C)
        return out @ Wo.T + bo

    def _L0_ffn_ref(hidden_states, Wg, bg, Wu, bu, Wd, bd, Wq, keys, down_embed, up_embed):
        import jax, jax.numpy as jnp
        import numpy as np
        B, T, D = (2, 512, 256)
        DCD = 1024
        RET = 128
        NEXP = 1024
        NKEYS = 64
        H = 4
        KPH = 8
        b, t, d = hidden_states.shape
        q = (hidden_states @ Wq).reshape(b, t, 2, H, RET // 2)
        sim = jnp.einsum('btphn,hkpn->pbthk', q, keys)
        sc, ix = jax.lax.top_k(sim, KPH)
        sx, sy = (sc[0], sc[1])
        ixx, ixy = (ix[0], ix[1])
        all_sc = (sx[..., :, None] + sy[..., None, :]).reshape(b, t, H, KPH * KPH)
        all_ix = (ixx[..., :, None] * NKEYS + ixy[..., None, :]).reshape(b, t, H, KPH * KPH)
        scores, pk = jax.lax.top_k(all_sc, KPH)
        idx = jnp.take_along_axis(all_ix, pk, axis=-1)
        de = down_embed[idx]
        ue = up_embed[idx]
        w = jnp.einsum('btd,bthkd->bthk', hidden_states, de)
        w = jax.nn.silu(w) * jax.nn.softmax(scores, axis=-1)
        experts_states = jnp.einsum('bthk,bthkd->btd', w, ue)
        mlp = jax.nn.silu(hidden_states @ Wg + bg) * (hidden_states @ Wu + bu) @ Wd + bd
        return mlp + experts_states
    x = _layernorm(x + _L0_attn_ref(x, L0_attn_log_A_real, L0_attn_A_imag, L0_attn_C_re, L0_attn_C_im, L0_attn_log_dt, L0_attn_D, L0_attn_ln_w, L0_attn_ln_b), axis=-1)
    x = _layernorm(x + _L0_xattn_ref(x, ctx_1024, ctx_1024, L0_xattn_Wq, L0_xattn_bq, L0_xattn_Wk, L0_xattn_bk, L0_xattn_Wv, L0_xattn_bv, L0_xattn_Wo, L0_xattn_bo), axis=-1)
    x = _layernorm(x + _L0_ffn_ref(x, L0_ffn_Wg, L0_ffn_bg, L0_ffn_Wu, L0_ffn_bu, L0_ffn_Wd, L0_ffn_bd, L0_ffn_Wq, L0_ffn_keys, L0_ffn_down_embed, L0_ffn_up_embed), axis=-1)
    return x

_drawn_inputs = setup_inputs


def setup_inputs(seed=0):
    import zlib

    import numpy as np

    out = dict(_drawn_inputs(seed))
    spreads = {'L0_attn_log_A_real': (-0.6931471824645996, 0.6),
     'L0_attn_ln_w': (1.0, 0.2),
     'L0_attn_ln_b': (0.0, 0.1),
     'L0_xattn_bq': (0.0, 0.347),
     'L0_xattn_bk': (0.0, 0.8),
     'L0_xattn_bv': (0.0, 0.1),
     'L0_xattn_bo': (0.0, 0.1),
     'L0_ffn_bg': (0.0, 0.7),
     'L0_ffn_bu': (0.0, 0.701),
     'L0_ffn_bd': (0.0, 0.1)}
    factors = {'L0_ffn_Wq': 8.0, 'L0_ffn_keys': 8.0, 'L0_ffn_down_embed': 6.628, 'L0_ffn_up_embed': 6.732}
    for name, (base, spread) in spreads.items():
        noise = np.random.default_rng([zlib.crc32(name.encode()), seed]).standard_normal(out[name].shape)
        drawn = base * np.exp(spread * noise) if base else spread * noise
        out[name] = jnp.asarray(drawn.astype(out[name].dtype))
    for name, factor in factors.items():
        out[name] = (out[name] * factor).astype(out[name].dtype)
    return out
```

```python
from contextlib import ExitStack

import numpy as np

import concourse.bass as bass
from concourse import mybir

ALU = mybir.AluOpType
ACT = mybir.ActivationFunctionType
AX_X = mybir.AxisListType.X
F32 = mybir.dt.float32
I32 = mybir.dt.int32

P = 128
B, L, D = 2, 1024, 256
NST = 64
NFFT = 2 * L
NC, NQ, NS = 8, 8, 16
KC = D // P
TILES = B * L // P
SUPER = 4
NSUP = TILES // SUPER
W = SUPER * P
NSLOT = 16
FREQ = 9
NKV, HEADS, HD = 77, 16, 16
GH = 4
FLAT = HEADS * NKV
PCH = (FLAT + P - 1) // P
FF = 1024
NEXP, NKEYS, FH, TOPK = 1024, 64, 4, 8
XR = NEXP // NKEYS
FC, EC = FF // P, NEXP // P
MAGIC = 1.5 * 2.0**23
TWO_PI = 6.283185
EPS = 1e-5
GRP = 64
NGRP = D // GRP
HALF = 32


def slot_of(k1, part):
    if k1 in (0, 8):
        return k1 // 8
    return 2 * k1 + part


def mat_of(k1, kind):
    if k1 == 0:
        return {0: 0, 2: 1}[kind]
    if k1 == 8:
        return {0: 2, 2: 3}[kind]
    return 4 + 3 * (k1 - 1) + kind


NMAT = 4 + 3 * 7


def heads_of(chunk):
    return chunk * P // NKV, min((chunk * P + P - 1) // NKV, HEADS - 1)


def fourier_constants():
    c, s = np.divmod(np.arange(P), NS)
    fwd = np.zeros((P, NSLOT, NS))
    inv = np.zeros((NSLOT, NS, P))
    for k1 in range(FREQ):
        ang = 2 * np.pi * k1 * c / NSLOT
        own = 1.0 if k1 in (0, 8) else 2.0
        fwd[np.arange(P), slot_of(k1, 0), s] = np.cos(ang)
        inv[slot_of(k1, 0), s, np.arange(P)] = own * np.cos(ang) / NFFT
        if k1 not in (0, 8):
            fwd[np.arange(P), slot_of(k1, 1), s] = -np.sin(ang)
            inv[slot_of(k1, 1), s, np.arange(P)] = -own * np.sin(ang) / NFFT
    fmat, imat = np.zeros((P, NMAT, P)), np.zeros((P, NMAT, P))
    pp, kk = np.meshgrid(np.arange(P), np.arange(P), indexing="ij")
    for k1 in range(FREQ):
        ang = 2 * np.pi * ((pp * (k1 + 16 * kk)) % NFFT) / NFFT
        for kind, m in ((0, np.cos(ang)), (1, np.sin(ang)), (2, -np.sin(ang))):
            if kind == 1 and k1 in (0, 8):
                continue
            fmat[:, mat_of(k1, kind)] = m
            imat[:, mat_of(k1, kind)] = m.T
    inv = inv.reshape(2, P, P).transpose(1, 0, 2)
    return [np.ascontiguousarray(a, dtype=np.float32) for a in (fwd.reshape(P, 2, P), inv, fmat, imat)]


def mask_constants():
    cols = np.zeros((P, 8), np.float32)
    cols[:64, 0] = -0.25
    cols[:64, 1] = np.pi / 2
    cols[:64, 2] = 2.0
    cols[64:, 3] = -2.0
    cols[:, 4] = np.pi / 2
    cols[:, 5] = -0.5
    ident = np.eye(P, dtype=np.float32)
    head_mask = np.zeros((P, P // HD), np.float32)
    head_mask[np.arange(P), np.arange(P) // HD] = 1.0
    shift = np.zeros((NKV, 3 * P), np.float32)
    shift[np.arange(NKV), np.arange(NKV) + P] = 1.0
    steps = np.tile(np.arange(HALF, dtype=np.float32), (P, 1))
    return [cols, ident, head_mask, shift, steps]


def build(nc, t):
    with ExitStack() as ctx:
        def sb(name, shape, dt=F32):
            return ctx.enter_context(nc.sbuf_tensor(name, shape, dt))

        def sem(name):
            return ctx.enter_context(nc.semaphore(name))

        bank = [ctx.enter_context(nc.psum_tensor(f"bank{i}", [P, 512], F32)) for i in range(8)]

        tok = sb("tok", [P, TILES, D])
        wq = sb("wq", [P, KC, D])
        wo = sb("wo", [P, KC, D])
        wsim = sb("wsim", [P, KC, 2 * FH * NKEYS])
        rows = sb("rows", [P, 5, D])
        lnw, lnb, bo, bd, bv = (rows[:, i, :] for i in range(5))
        pcol = sb("pcol", [P, 4 + 2 * FC])
        ident = sb("ident", [P, P])
        cols = sb("cols", [P, 8])
        head_mask = sb("head_mask", [P, P // HD])
        steps = sb("steps", [P, HALF])
        kbd = sb("kbd", [P, B, KC, 8 * NKV])
        vbd = sb("vbd", [P, B, PCH, 51])
        stats = sb("stats", [P, 2, 6])
        mv = sb("mv", [P, 4, TILES, 2])
        rstd = sb("rstd", [P, 4, TILES])
        mexp = sb("mexp", [P, 2, FH])
        skip = sb("skip", [1, D])

        WORDS = 41000
        arena = sb("arena", [P, WORDS])
        place = {}

        def part(name, start, *dims, rows_=P):
            n = int(np.prod(dims))
            assert start + n <= WORDS, (name, start, n)
            place[name] = (start, start + n)
            v = arena[0:rows_, start:start + n]
            if len(dims) == 1:
                return v
            names = "abcde"[:len(dims)]
            return v.rearrange(f"p ({' '.join(names)}) -> p {' '.join(names)}",
                               **{k: d for k, d in zip(names, dims)})

        o_a, o_b, o_tab = 0, 8192, 16384
        cA = part("cA", o_a, 2, NQ, 512)
        cB = part("cB", o_b, NSLOT, 512)
        zA = part("zA", o_a, NSLOT, 512)
        zB = part("zB", o_b, 2, NQ, 512)
        ktime = part("ktime", o_a, HALF, D, rows_=HALF)
        kB = part("kB", o_tab, NSLOT, D)
        kf = part("kf", o_tab + 4096, FREQ, 2, D)
        yf = part("yf", o_tab + 8704, 2, 2, 512)
        kQ = part("kQ", o_tab + 8704, NQ, D)
        prod = part("prod", o_tab + 10752, 2, 2, 1024)
        kA = part("kA", o_tab + 10752, 2, NQ, D)
        o_mat = o_tab + 14848
        fmat = part("fmat", o_mat, NMAT, P)
        imat = part("imat", o_mat + 3200, NMAT, P)
        fa = part("fa", o_mat + 6400, 2, P)
        fai = part("fai", o_mat + 6656, 2, P)
        assert o_mat + 6912 <= WORDS
        tq, tqm, tp, tpm, tpc, trd = (part(f"tab{i}", o_tab + 2048 * i, GRP, HALF) for i in range(6))
        wqf = part("wqf", o_tab + 12288, 2 * FH, D, rows_=NKEYS)
        keysT = part("keysT", o_tab + 14336, 2 * FH, NKEYS, rows_=NKEYS)
        wk = part("wk", o_b, KC, D)
        wv = part("wv", o_b + 512, KC, D)
        ctxT = part("ctxT", o_b + 1024, KC, B * NKV)
        kT = part("kT", o_b + 1332, KC, B * NKV)
        vaug = part("vaug", o_b + 1640, B, HEADS, HD + 1, rows_=NKV)
        shift = part("shift", o_b + 2184, 3 * P, rows_=NKV)
        ssm = part("ssm", o_b + 2568, 5, D)
        wk_ = [part(f"w{i}", o_b + 4104 + D * i, D) for i in range(15)]

        wg, wu, dn = (part(n, o_tab + 2048 * i, KC, FF) for i, n in ((0, "wg"), (1, "wu"), (3, "dn")))
        wd, up = (part(n, o_tab + 2048 * i, FC, D) for i, n in ((2, "wd"), (4, "up")))
        o_w = o_tab + 10240
        silg = part("silg", o_w, EC, W)
        hid = part("hid", o_w + 4096, FC, W)
        x2T = part("x2T", o_w + 8192, KC, W)
        sim = part("sim", o_w + 9216, 2, 2 * FH, NKEYS)
        ebuf = [part("ebuf0", o_w + 10240, XR, NKEYS)]
        assert o_w + 11264 <= o_mat + 6656
        o_l = o_mat + 6912
        ebuf.append(part("ebuf1", o_l, XR, NKEYS))
        sxb = [part("sx0", o_l + 1024, XR, NKEYS)]
        best = part("best", o_l + 2048, 2 * FH, TOPK)
        pairs = part("pairs", o_l + 2112, FH, TOPK * TOPK)
        top = part("top", o_l + 2368, 2, FH, TOPK)
        zexp = part("zexp", o_l + 2432, FH, TOPK)
        zinv = part("zinv", o_l + 2464, FH)
        negm = part("negm", o_l + 2468, 2, FH)
        rsum = part("rsum", o_l + 2476, 2)
        bgh = part("bgh", o_l + 2480, FC)
        smax = part("smax", o_l + 2488, 8)
        rec = part("rec", o_l + 2496, HEADS)
        vare = part("vare", o_l + 2512, 4)
        gtmp = part("gtmp", o_l, B, D)
        x1T = part("x1T", o_a, KC, W)
        qT = part("qT", o_a + 1024, KC, W)
        prob = part("prob", o_a + 2048, 2, FLAT)
        pT = part("pT", o_a + 4512, PCH, P)
        ob = part("ob", o_a + 5792, 2, D)
        oT = part("oT", o_a + 6304, 2, KC, P)
        sxb.append(part("sx1", o_a + 6816, XR, NKEYS))
        rw = part("rw", o_b, SUPER, NEXP)
        aT = part("aT", o_b + 4096, EC, P)
        tg = part("tg", o_b + 5120, 2, 2, W)
        gate = part("gate", o_b + 7168, W)

        s_ssm, s_cst, s_ctx, s_wsim_in, s_ffn_in = (sem(n) for n in (
            "ssm_loaded", "const_loaded", "ctx_loaded", "simw_loaded", "ffn_loaded"))
        s_x = [sem(f"x{q}_loaded") for q in range(NQ)]
        s_mat = sem("mat_loaded")
        s_dve, s_pool, s_actc = sem("dve_steps"), sem("pool_steps"), sem("act_steps")
        s_small_ready = sem("small_ready")
        s_small_act = sem("small_act")
        s_base = sem("table_base_ready")
        s_outer = sem("decay_outer_ready")
        s_phase = sem("table_phase_ready")
        s_trig = sem("table_trig_ready")
        s_bsin = sem("table_bsin_ready")
        s_tab = sem("table_ready")
        s_ktm = sem("ktime_mm")
        s_kev = sem("ktime_evac")
        s_kdone = sem("ktime_done")
        s_kq = sem("kq_moved")
        s_kw = sem("kt_written")
        s_xa, s_xae, s_xaw, s_xb = sem("xa_mm"), sem("xa_evac"), sem("xa_written"), sem("xb_loaded")
        s_ka, s_kae, s_kaw, s_kb = sem("ka_mm"), sem("ka_evac"), sem("ka_written"), sem("kb_loaded")
        s_kfm, s_kfe = sem("kf_mm"), sem("kf_evac")
        s_xf, s_pr, s_yf = sem("xf_mm"), sem("xk_products"), sem("y_ready")
        s_z, s_ze, s_zw, s_zr = sem("z_mm"), sem("z_evac"), sem("z_written"), sem("z_loaded")
        s_r = sem("conv_mm")
        s_rfree = sem("conv_read")
        s_cm, s_kt, s_ce = sem("ctx_mm"), sem("ctx_keys"), sem("ctx_evac")
        s_kbd = sem("kbd_ready")
        s_kbz = sem("vaug_ready")

        s_xbr = sem("x_plus_bias")
        s_x1, s_x2, s_out = sem("x1_ready"), sem("x2_ready"), sem("out_ready")
        s_outw = sem("out_written")
        s_stat = [sem(f"norm{n}_stats") for n in range(4)]
        s_rstd = [sem(f"norm{n}_rstd") for n in range(4)]
        s_u = [sem("attn_residual")]
        s_bo, s_bd = sem("bo_added"), sem("bd_added")
        s_tmm, s_tev = sem("turned_mm"), sem("turned_evac")
        s_wmm, s_wact, s_wdve = sem("wide_mm"), sem("wide_read_act"), sem("wide_read_dve")
        s_smm, s_ssub, s_exp = sem("score_mm"), sem("score_shifted"), sem("score_exp")
        s_pv, s_on, s_wo = sem("pv_mm"), sem("attn_normed"), sem("wo_mm")
        s_best, s_zarg, s_zexp = sem("pair_top"), sem("pair_args"), sem("pair_exp")
        s_sx, s_e, s_rfr, s_rr = sem("pair_sums"), sem("pair_exps"), sem("pair_used"), sem("weights_ready")
        s_tg, s_tgf = sem("tanh_ready"), sem("tanh_used")
        s_7mm, s_7f = sem("bank7_mm"), sem("bank7_read")

        T_AT, n = {}, 0
        for s in range(NSUP + 1):
            units = []
            if s < NSUP:
                units += [("x1", s, j) for j in range(2)]
            if s >= 1:
                units += [("x2", s - 1, j) for j in range(2)]
            if s < NSUP:
                for i in range(SUPER):
                    units += [("p", SUPER * s + i, j) for j in range(3)] + [("o", SUPER * s + i, 0)]
            for u in units:
                T_AT[u], n = n, n + 1
        W_AT, W_FREE, nw, na, nd = {}, [], 0, 0, 0
        for s in range(NSUP + 1):
            units = []
            if s < NSUP:
                units += [("q", s, j) for j in range(KC)]
            if s >= 1:
                for i in range(SUPER):
                    units += [("sim", s - 1, i), ("e", s - 1, 2 * i), ("e", s - 1, 2 * i + 1)]
                    for j in (2 * i, 2 * i + 1):
                        units += [("g", s - 1, j), ("u", s - 1, j)]
            for u in units:
                W_AT[u], nw = nw, nw + 1
                if u[0] == "u":
                    nd += 1
                    W_FREE.append((s_wdve, nd))
                else:
                    na += 1
                    W_FREE.append((s_wact, na))

        scr_x = t["scr_x"]
        scr_k = t["scr_k"]
        scr_t = t["scr_t"]
        scr_z = t["scr_z"]

        class Steps:

            def __init__(self, eng, s):
                self.eng, self.s, self.n = eng, s, 0
                self.counts = {}

            def mark(self, ins):
                self.n += 1
                ins.then_inc(self.s, 1)
                return self.n

            def need(self, k):
                self.eng.wait_ge(self.s, k)

            def link(self, ins):
                self.need(self.mark(ins))

            def done(self, s):
                self.counts[id(s)] = self.counts.get(id(s), 0) + 1
                self.eng.wait_ge(s, self.counts[id(s)])

        block = ctx.enter_context(nc.Block())

        @block.sync
        def _(sp):
            sp.dma_start(ssm, t["ssm"]).then_inc(s_ssm, 16)
            sp.dma_start(cols[:, :], t["cols"]).then_inc(s_ssm, 16)
            sp.dma_start(steps[:, :], t["steps"]).then_inc(s_ssm, 16)
            sp.dma_start(skip[:, :], t["skip"]).then_inc(s_ssm, 16)
            sp.dma_start(fa, t["fa"]).then_inc(s_cst, 16)
            for q in range(NQ):
                sp.dma_start(tok[:, 2 * q:2 * q + 2, :], t["x"][:, 2 * q:2 * q + 2, :]).then_inc(s_x[q], 16)
            for dst, n in ((ctxT, "ctxT"), (wk, "wk"), (wv, "wv"), (pcol[:, :], "pcol"), (shift, "shift"),
                           (head_mask[:, :], "head_mask"), (rows[:, :, :], "rows")):
                sp.dma_start(dst, t[n]).then_inc(s_ctx, 16)
            sp.dma_start(wqf, t["wqf"]).then_inc(s_wsim_in, 16)
            sp.dma_start(keysT, t["keysT"]).then_inc(s_wsim_in, 16)
            for dst, n in ((fmat, "fmat"), (imat, "imat"), (fai, "fai"), (wq[:, :, :], "wq"), (wo[:, :, :], "wo"),
                           (ident[:, :], "ident")):
                sp.dma_start(dst, t[n]).then_inc(s_mat, 16)
            for q in range(NQ):
                sp.wait_ge(s_xae, 2 * (q + 1))
                for h in range(2):
                    sp.dma_start(scr_x[q, 8 * h:8 * h + 8].rearrange("r s n -> (r s) n"),
                                 cA[:, h, q, :]).then_inc(s_xaw, 16)
            sp.wait_ge(s_xaw, 16 * 2 * NQ)
            sp.wait_ge(s_kbd, 1)
            sp.wait_ge(s_ce, 4)
            sp.wait_ge(s_tab, NGRP)
            for q in range(NQ):
                sp.dma_start(cB[16 * q:16 * q + 16, :, :],
                             scr_x[q].rearrange("r s n -> s r n")).then_inc(s_xb, 16)
            sp.wait_ge(s_kdone, 1)
            for g in range(4):
                sp.dma_start(scr_t[:, 8 * g:8 * g + 8, :], ktime[:, 8 * g:8 * g + 8, :]).then_inc(s_kw, 16)
            sp.wait_ge(s_kw, 64)
            taps = scr_t.rearrange("i j n -> (i j) n").rearrange("(c q s) n -> c s q n", c=NC, q=NQ)
            for c in range(NC):
                sp.dma_start(kQ[16 * c:16 * c + 16, :, :], taps[c]).then_inc(s_kq, 16)
            for qp in range(NQ // 2):
                sp.wait_ge(s_kae, 2 * (qp + 1))
                for q in (2 * qp, 2 * qp + 1):
                    for h in range(2):
                        sp.dma_start(scr_k[q, 8 * h:8 * h + 8].rearrange("r s n -> (r s) n"),
                                     kA[:, h, q, :]).then_inc(s_kaw, 16)
            sp.wait_ge(s_kaw, 16 * 2 * NQ)
            for q in range(NQ):
                sp.dma_start(kB[16 * q:16 * q + 16, :, :],
                             scr_k[q].rearrange("r s n -> s r n")).then_inc(s_kb, 16)
            for k1 in range(FREQ):
                sp.wait_ge(s_ze, k1 + 1)
                for part_ in range(1 if k1 in (0, 8) else 2):
                    r = slot_of(k1, part_)
                    sp.dma_start(scr_z[r], zA[:, r, :]).then_inc(s_zw, 16)
            sp.wait_ge(s_zw, 16 * NSLOT)
            sp.wait_ge(s_xf, FREQ)
            for r in range(NSLOT):
                h, rr = divmod(r, 8)
                sp.dma_start(zB[16 * rr:16 * rr + 16, h, :, :],
                             scr_z[r].rearrange("(q s) n -> s q n", s=NS)).then_inc(s_zr, 16)
            sp.wait_ge(s_z, FREQ)
            for dst, n in ((dn, "dn"), (wg, "wg"), (wu, "wu"), (wd, "wd"), (up, "up")):
                sp.dma_start(dst, t[n]).then_inc(s_ffn_in, 16)
            for tl in range(TILES):
                sp.wait_ge(s_out, tl + 1)
                sp.dma_start(t["out"][:, tl, :], tok[:, tl, :]).then_inc(s_outw, 16)
            sp.wait_ge(s_outw, 16 * TILES)

        @block.tensor
        def _(pe):
            mm = nc.tensor.matmul
            pe.wait_ge(s_cst, 16)
            for q in range(NQ):
                pe.wait_ge(s_x[q], 16)
                for h in range(2):
                    i = 2 * q + h
                    if i >= 4:
                        pe.wait_ge(s_xae, i - 3)
                    mm(bank[i % 4][:, :], fa[:, h, :],
                       tok[:, 2 * q:2 * q + 2, :].rearrange("p a b -> p (a b)"),
                       start=True, stop=True).then_inc(s_xa, 1)
            pe.wait_ge(s_ctx, 16 * 7)
            for oc in range(KC):
                for ic in range(KC):
                    ins = mm(bank[4 + oc][:, 0:B * NKV], wk[:, ic, P * oc:P * oc + P], ctxT[:, ic, :],
                             start=(ic == 0), stop=(ic == KC - 1))
                ins.then_inc(s_cm, 1)
            for b in range(B):
                for ic in range(KC):
                    ins = mm(bank[6 + b][0:NKV, 0:D], ctxT[:, ic, NKV * b:NKV * b + NKV], wv[:, ic, :],
                             start=(ic == 0), stop=(ic == KC - 1))
                ins.then_inc(s_cm, 1)
            pe.wait_ge(s_wsim_in, 32)
            pe.wait_ge(s_kt, 2)
            for oc in range(KC):
                for m in range(2 * FH):
                    ins = mm(bank[4 + oc][:, NKEYS * m:NKEYS * m + NKEYS], wqf[:, m, P * oc:P * oc + P],
                             keysT[:, m, :], start=True, stop=True, skip_group_check=True)
                ins.then_inc(s_cm, 1)
            pe.wait_ge(s_kbz, 1)
            for b in range(B):
                for ch in range(PCH):
                    h0, h1 = heads_of(ch)
                    for h in range(h0, h1 + 1):
                        at = P + P * ch - NKV * h
                        ins = mm(bank[6 + b][:, 51 * ch + 17 * (h - h0):51 * ch + 17 * (h - h0) + 17],
                                 shift[:, at:at + P], vaug[:, b, h, :], start=True, stop=True,
                                 skip_group_check=True)
                ins.then_inc(s_cm, 1)
            pe.wait_ge(s_ce, 4)
            for g in range(NGRP):
                pe.wait_ge(s_tab, g + 1)
                for m in range(GRP // 16):
                    i = (GRP // 16) * g + m
                    if i >= 4:
                        pe.wait_ge(s_kev, i - 3)
                    for hh in range(16):
                        ch = 16 * m + hh
                        ins = mm(bank[4 + i % 4][0:HALF, HALF * hh:HALF * hh + HALF], tpm[:, ch, :], tqm[:, ch, :],
                                 start=True, stop=True, skip_group_check=True)
                    ins.then_inc(s_ktm, 1)
            pe.wait_ge(s_kq, 16 * NC)
            pe.wait_ge(s_xae, 2 * NQ)
            for qp in range(NQ // 2):
                for h in range(2):
                    i = 2 * qp + h
                    if i >= 4:
                        pe.wait_ge(s_kae, i - 3)
                    mm(bank[i % 4][:, :], fa[:, h, :], kQ[:, 2 * qp:2 * qp + 2, :].rearrange("p a b -> p (a b)"),
                       start=True, stop=True).then_inc(s_ka, 1)

            def second_stage(k1, re, im, src):
                r, i = slot_of(k1, 0), slot_of(k1, 1)
                two = k1 not in (0, 8)
                mm(re, fmat[:, mat_of(k1, 0), :], src(r), start=True, stop=not two)
                if two:
                    mm(re, fmat[:, mat_of(k1, 1), :], src(i), start=False, stop=True)
                ins = mm(im, fmat[:, mat_of(k1, 2), :], src(r), start=True, stop=not two)
                if two:
                    ins = mm(im, fmat[:, mat_of(k1, 0), :], src(i), start=False, stop=True)
                return ins

            pe.wait_ge(s_mat, 16 * 6)
            pe.wait_ge(s_kb, 16 * NQ)
            pe.wait_ge(s_kev, 16)
            for k1 in range(FREQ):
                bk = bank[4 + k1 % 4]
                if k1 >= 4:
                    pe.wait_ge(s_kfe, k1 - 3)
                second_stage(k1, bk[:, 0:D], bk[:, D:2 * D], lambda r: kB[:, r, :]).then_inc(s_kfm, 1)
            pe.wait_ge(s_xb, 16 * NQ)
            pe.wait_ge(s_kae, NQ)
            pe.wait_ge(s_kfe, FREQ)
            for k1 in range(FREQ + 1):
                if k1 < FREQ:
                    if k1 >= 2:
                        pe.wait_ge(s_pr, k1 - 1)
                    bb = 2 * (k1 % 2)
                    second_stage(k1, bank[bb][:, :], bank[bb + 1][:, :], lambda r: cB[:, r, :]).then_inc(s_xf, 1)
                if k1 >= 1:
                    k = k1 - 1
                    pe.wait_ge(s_yf, k + 1)
                    if k >= 2:
                        pe.wait_ge(s_ze, k - 1)
                    bb = 4 + 2 * (k % 2)
                    y = yf[:, k % 2]
                    mm(bank[bb][:, :], imat[:, mat_of(k, 0), :], y[:, 0, :], start=True, stop=False)
                    ins = mm(bank[bb][:, :], imat[:, mat_of(k, 2), :], y[:, 1, :], start=False, stop=True)
                    if k not in (0, 8):
                        mm(bank[bb + 1][:, :], imat[:, mat_of(k, 1), :], y[:, 0, :], start=True, stop=False)
                        ins = mm(bank[bb + 1][:, :], imat[:, mat_of(k, 0), :], y[:, 1, :], start=False, stop=True)
                    ins.then_inc(s_z, 1)
            pe.wait_ge(s_zr, 16 * NSLOT)
            pe.wait_ge(s_pr, FREQ)
            for q in range(NQ):
                if q >= 4:
                    pe.wait_ge(s_rfree, q - 3)
                for h in range(2):
                    ins = mm(bank[q % 4][:, :], fai[:, h, :], zB[:, h, q, :], start=(h == 0), stop=(h == 1))
                ins.then_inc(s_r, 1)

            def t_unit(key):
                u = T_AT[key]
                if u >= 2:
                    pe.wait_ge(s_tev, u - 1)
                return bank[2 + u % 2]

            def w_unit(key):
                u = W_AT[key]
                if u >= 2:
                    pe.wait_ge(*W_FREE[u - 2])
                return bank[5 + u % 2]

            def turn_tokens(name, s):
                for j in range(2):
                    bk = t_unit((name, s, j))
                    for i in range(2):
                        for k in range(KC):
                            ins = nc.tensor.transpose(bk[:, P * (2 * i + k):P * (2 * i + k) + P],
                                                      tok[:, SUPER * s + 2 * j + i, P * k:P * k + P], ident[:, :])
                    ins.then_inc(s_tmm, 1)

            def wide(key, w, m, src):
                bk = w_unit(key)
                for k in range(KC):
                    ins = mm(bk[:, :], w[:, k, P * m:P * m + P], src[:, k, :], start=(k == 0), stop=(k == KC - 1))
                ins.then_inc(s_wmm, 1)

            def scores(tl):
                i, b = tl % SUPER, tl % B
                for hh in range(KC):
                    if tl or hh:
                        pe.wait_ge(s_ssub, 2 * tl + hh)
                    for g in range(2):
                        ins = mm(bank[g][:, 0:GH * NKV], qT[:, hh, P * i:P * i + P],
                                 kbd[:, b, hh, GH * NKV * g:GH * NKV * (g + 1)], start=True, stop=True)
                    ins.then_inc(s_smm, 1)

            def attend(tl):
                b = tl % B
                pe.wait_ge(s_exp, 2 * tl + 2)
                for j in range(3):
                    bk = t_unit(("p", tl, j))
                    for c in range(4 * j, min(4 * j + 4, PCH)):
                        n = min(P, FLAT - P * c)
                        ins = nc.tensor.transpose(bk[0:n, P * (c % 4):P * (c % 4) + P],
                                                  prob[:, tl % 2, P * c:P * c + n], ident[:, :])
                    ins.then_inc(s_tmm, 1)
                if tl:
                    pe.wait_ge(s_u[0], tl)
                for c in range(PCH):
                    if c % 4 == 0:
                        pe.wait_ge(s_tev, T_AT[("p", tl, c // 4)] + 1)
                    h0, h1 = heads_of(c)
                    n = min(P, FLAT - P * c)
                    k = (HD + 1) * (h1 - h0 + 1)
                    ins = mm(bank[4][:, (HD + 1) * h0:(HD + 1) * h0 + k], pT[0:n, c, :], vbd[0:n, b, c, 0:k],
                             start=(c == 0), stop=(c == PCH - 1), skip_group_check=True)
                ins.then_inc(s_pv, 1)

            def project(tl):
                pe.wait_ge(s_on, tl + 1)
                bk = t_unit(("o", tl, 0))
                for k in range(KC):
                    ins = nc.tensor.transpose(bk[:, P * k:P * k + P], ob[:, tl % 2, P * k:P * k + P], ident[:, :])
                ins.then_inc(s_tmm, 1)
                pe.wait_ge(s_tev, T_AT[("o", tl, 0)] + 1)
                for k in range(KC):
                    ins = mm(bank[4][:, 0:D], oT[:, tl % 2, k, :], wo[:, k, :], start=(k == 0), stop=(k == KC - 1))
                ins.then_inc(s_wo, 1)

            def inner(f, i):
                pe.wait_ge(s_tev, T_AT[("x2", f, i // 2)] + 1)
                bk = w_unit(("sim", f, i))
                for k in range(KC):
                    ins = mm(bk[:, :], x2T[:, k, P * i:P * i + P], wsim[:, k, :], start=(k == 0), stop=(k == KC - 1))
                ins.then_inc(s_wmm, 1)
                pe.wait_ge(s_tev, T_AT[("x2", f, 1)] + 1)
                for j in (2 * i, 2 * i + 1):
                    wide(("e", f, j), dn, j, x2T)
                for j in (2 * i, 2 * i + 1):
                    wide(("g", f, j), wg, j, x2T)
                    wide(("u", f, j), wu, j, x2T)

            def outer(f, i):
                rt = SUPER * f + i
                pe.wait_ge(s_rr, rt + 1)
                for j in range(2):
                    if rt or j:
                        pe.wait_ge(s_7f, 3 * rt + j)
                    for c in range(4):
                        ins = nc.tensor.transpose(bank[7][:, P * c:P * c + P],
                                                  rw[:, i, P * (4 * j + c):P * (4 * j + c) + P], ident[:, :])
                    ins.then_inc(s_7mm, 1)
                pe.wait_ge(s_wdve, FC * (f + 1))
                pe.wait_ge(s_7f, 3 * rt + 2)
                for c in range(FC):
                    mm(bank[7][:, 0:D], hid[:, c, P * i:P * i + P], wd[:, c, :], start=(c == 0), stop=False)
                for c in range(EC):
                    ins = mm(bank[7][:, 0:D], aT[:, c, :], up[:, c, :], start=False, stop=(c == EC - 1))
                ins.then_inc(s_7mm, 1)

            for s in range(NSUP + 1):
                if s < NSUP:
                    pe.wait_ge(s_x1, SUPER * (s + 1) // 2)
                    if s == 0:
                        pe.wait_ge(s_x1, NQ)
                    turn_tokens("x1", s)
                    pe.wait_ge(s_tev, T_AT[("x1", s, 1)] + 1)
                    for j in range(KC):
                        wide(("q", s, j), wq, j, x1T)
                if s >= 1:
                    pe.wait_ge(s_x2, SUPER * s)
                    if s == 1:
                        pe.wait_ge(s_ffn_in, 16 * 5)
                    turn_tokens("x2", s - 1)
                for i in range(SUPER):
                    if s < NSUP:
                        pe.wait_ge(s_wact, W_FREE[W_AT[("q", s, KC - 1)]][1])
                        if s == 0 and i == 0:
                            pe.wait_ge(s_kbd, 1)
                        scores(SUPER * s + i)
                    if s >= 1:
                        inner(s - 1, i)
                    if s < NSUP:
                        attend(SUPER * s + i)
                        project(SUPER * s + i)
                if s >= 1:
                    for i in range(SUPER):
                        outer(s - 1, i)

        def evac_taps(act, own, i):
            if i == 0:
                act.wait_ge(s_xaw, 16 * 2 * NQ)
            src = bank[4 + i % 4][0:HALF, :].rearrange("p (h j) -> p j h", j=HALF)
            nc.scalar.copy(ktime[:, :, 16 * i:16 * i + 16], src).then_inc(s_kev, 1)
            own.done(s_kev)

        @block.scalar
        def _(act):
            fn = nc.scalar.activation
            own = Steps(act, s_actc)
            for i in range(2 * NQ):
                act.wait_ge(s_xa, i + 1)
                nc.scalar.copy(cA[:, i % 2, i // 2, :], bank[i % 4][:, :]).then_inc(s_xae, 1)
                own.done(s_xae)
                if i == 3:
                    act.wait_ge(s_small_ready, 1)
                    fn(wk_[3], wk_[2], ACT.Sin, scale=-TWO_PI).then_inc(s_small_act, 1)
                    own.done(s_small_act)
                    fn(wk_[4], wk_[2], ACT.Sin, scale=-TWO_PI / 2).then_inc(s_small_act, 1)
                    own.done(s_small_act)
                    act.wait_ge(s_small_ready, 2)
                    fn(wk_[5], wk_[1], ACT.Tanh, scale=0.5).then_inc(s_small_act, 1)
                    own.done(s_small_act)
                    fn(wk_[6], wk_[1], ACT.Exp).then_inc(s_small_act, 1)
                    own.done(s_small_act)
            act.wait_ge(s_cm, 5)
            nc.scalar.copy(wsim[:, 0, :], bank[4][:, :]).then_inc(s_ce, 1)
            own.done(s_ce)
            act.wait_ge(s_cm, 6)
            nc.scalar.copy(wsim[:, 1, :], bank[5][:, :]).then_inc(s_ce, 1)
            own.done(s_ce)
            for b in range(B):
                act.wait_ge(s_cm, 7 + b)
                for ch in range(PCH):
                    h0, h1 = heads_of(ch)
                    k = 17 * (h1 - h0 + 1)
                    ins = nc.scalar.copy(vbd[:, b, ch, 0:k], bank[6 + b][:, 51 * ch:51 * ch + k])
                ins.then_inc(s_ce, 1)
                own.done(s_ce)
            for g in range(NGRP):
                act.wait_ge(s_phase, 2 * g + 1)
                own.link(fn(tq, tq, ACT.Sin, scale=TWO_PI, bias=cols[:, 1:2]))
                act.wait_ge(s_phase, 2 * g + 2)
                own.link(fn(tpc, trd, ACT.Sin, scale=-TWO_PI, bias=cols[:, 4:5]))
                own.link(fn(tp, tp, ACT.Sin, scale=-TWO_PI))
                act.wait_ge(s_outer, 2 * g + 2)
                own.link(fn(tqm, tqm, ACT.Exp))
                fn(tpm, tpm, ACT.Exp).then_inc(s_trig, 1)
                own.done(s_trig)
                if g >= 1:
                    for m in range(4):
                        i = 4 * (g - 1) + m
                        act.wait_ge(s_ktm, i + 1)
                        evac_taps(act, own, i)
            for m in range(4):
                i = 4 * (NGRP - 1) + m
                act.wait_ge(s_ktm, i + 1)
                evac_taps(act, own, i)
            for k1 in range(FREQ):
                act.wait_ge(s_kfm, k1 + 1)
                nc.scalar.copy(kf[:, k1].rearrange("p a b -> p (a b)"), bank[4 + k1 % 4][:, :]).then_inc(s_kfe, 1)
                own.done(s_kfe)
            for k1 in range(FREQ):
                act.wait_ge(s_z, k1 + 1)
                bb = 4 + 2 * (k1 % 2)
                ins = nc.scalar.copy(zA[:, slot_of(k1, 0), :], bank[bb][:, :])
                if k1 not in (0, 8):
                    own.link(ins)
                    ins = nc.scalar.copy(zA[:, slot_of(k1, 1), :], bank[bb + 1][:, :])
                ins.then_inc(s_ze, 1)
                own.done(s_ze)

            def turned(key, out, view):
                u = T_AT[key]
                act.wait_ge(s_tmm, u + 1)
                nc.scalar.copy(out, view(bank[2 + u % 2])).then_inc(s_tev, 1)
                own.done(s_tev)

            def turned_tokens(name, s, dst):
                for j in range(2):
                    turned((name, s, j), dst[:, :, 2 * P * j:2 * P * j + 2 * P].rearrange("p k (i n) -> p k i n", n=P),
                           lambda bk: bk[:, :].rearrange("p (i k n) -> p k i n", i=2, k=KC))

            def wide_ready(key):
                u = W_AT[key]
                act.wait_ge(s_wmm, u + 1)
                return bank[5 + u % 2][:, :]

            for s in range(NSUP + 1):
                f = s - 1
                if s < NSUP:
                    if s:
                        act.wait_ge(s_wmm, W_AT[("q", s - 1, KC - 1)] + 1)
                    turned_tokens("x1", s, x1T)
                    for j in range(KC):
                        src = wide_ready(("q", s, j))
                        if s:
                            act.wait_ge(s_smm, 2 * SUPER * s)
                        fn(qT[:, j, :], src, ACT.Identity, bias=pcol[:, j:j + 1]).then_inc(s_wact, 1)
                        own.done(s_wact)
                if s >= 1:
                    if f:
                        act.wait_ge(s_wmm, W_AT[("u", f - 1, FC - 1)] + 1)
                    turned_tokens("x2", f, x2T)
                for i in range(SUPER):
                    tl, rt = SUPER * s + i, SUPER * f + i
                    if s < NSUP:
                        for hh in range(KC):
                            act.wait_ge(s_ssub, 2 * tl + hh + 1)
                            half = prob[:, tl % 2, 8 * NKV * hh:8 * NKV * (hh + 1)]
                            fn(half, half, ACT.Exp).then_inc(s_exp, 1)
                            own.done(s_exp)
                    if s >= 1:
                        src = wide_ready(("sim", f, i))
                        if rt >= 2:
                            act.wait_ge(s_sx, FH * (rt - 1))
                            act.wait_ge(s_best, rt - 1)
                        nc.scalar.copy(sim[:, rt % 2].rearrange("p a b -> p (a b)"), src).then_inc(s_wact, 1)
                        own.done(s_wact)
                        for k, key in enumerate((("e", f, 2 * i), ("e", f, 2 * i + 1), ("g", f, 2 * i), ("g", f, 2 * i + 1))):
                            src, n = wide_ready(key), 16 * f + 4 * i + k
                            if n >= 2:
                                act.wait_ge(s_tgf, n - 1)
                            bias = bgh[:, key[2]:key[2] + 1] if key[0] == "g" else 0.0
                            fn(tg[:, n % 2, 0, :], src, ACT.Tanh, scale=0.5, bias=bias).then_inc(s_tg, 1)
                            own.done(s_tg)
                            fn(tg[:, n % 2, 1, :], src, ACT.Identity, scale=0.5, bias=bias).then_inc(s_wact, 1)
                            own.done(s_wact)
                        act.wait_ge(s_zarg, rt + 1)
                        fn(zexp, zexp, ACT.Exp).then_inc(s_zexp, 1)
                        own.done(s_zexp)
                        act.wait_ge(s_best, rt + 1)
                        for h in range(FH):
                            n = FH * rt + h
                            act.wait_ge(s_sx, n + 1)
                            if n >= 2:
                                act.wait_ge(s_rfr, n - 1)
                            fn(ebuf[n % 2], sxb[n % 2], ACT.Exp, bias=negm[:, rt % 2, h:h + 1]).then_inc(s_e, 1)
                            own.done(s_e)
                    if s < NSUP:
                        for j in range(3):
                            if tl:
                                act.wait_ge(s_pv, tl)
                            c0, c1 = 4 * j, min(4 * j + 4, PCH)
                            if j < 2:
                                turned(("p", tl, j), pT[:, c0:c1, :], lambda bk: bk[:, :].rearrange("p (c n) -> p c n", n=P))
                            else:
                                u = T_AT[("p", tl, j)]
                                act.wait_ge(s_tmm, u + 1)
                                own.link(nc.scalar.copy(pT[:, 8, :], bank[2 + u % 2][:, 0:P]))
                                r_ = FLAT - 9 * P
                                nc.scalar.copy(pT[0:r_, 9, :], bank[2 + u % 2][0:r_, P:2 * P]).then_inc(s_tev, 1)
                                own.done(s_tev)
                        if tl >= 2:
                            act.wait_ge(s_wo, tl - 1)
                        turned(("o", tl, 0), oT[:, tl % 2], lambda bk: bk[:, 0:D].rearrange("p (k n) -> p k n", n=P))

        @block.gpsimd
        def _(pool):
            own = Steps(pool, s_pool)
            tt = nc.gpsimd.tensor_tensor
            pool.wait_ge(s_base, 1)
            for g in range(NGRP):
                ch = slice(GRP * g, GRP * g + GRP)
                if g >= 1:
                    pool.wait_ge(s_ktm, 4 * g)
                for dst, a in ((tqm, wk_[1]), (tpm, wk_[7])):
                    tt(dst, a[:, ch].unsqueeze(2).broadcast_to((P, GRP, HALF)),
                       steps[:, :].unsqueeze(1).broadcast_to((P, GRP, HALF)), ALU.mult).then_inc(s_outer, 1)
                    own.done(s_outer)
                pool.wait_ge(s_trig, g + 1)
                pool.wait_ge(s_base, 2)
                tt(tp, tp, wk_[9][:, ch].unsqueeze(2).broadcast_to((P, GRP, HALF)), ALU.mult).then_inc(s_bsin, 1)
                own.done(s_bsin)
                if g == 0:
                    pool.wait_ge(s_kt, 2)
                    for b in range(B):
                        for oc in range(KC):
                            ins = tt(kbd[:, b, oc, :].rearrange("p (h k) -> p h k", k=NKV),
                                     kT[:, oc, NKV * b:NKV * b + NKV].unsqueeze(1).broadcast_to((P, 8, NKV)),
                                     head_mask[:, :].unsqueeze(2).broadcast_to((P, 8, NKV)), ALU.mult)
                            if (b, oc) == (B - 1, KC - 1):
                                ins.then_inc(s_kbd, 1)
                                own.done(s_kbd)
                            else:
                                own.link(ins)
            pool.wait_ge(s_xa, 2 * NQ)
            pool.wait_ge(s_ctx, 16 * 7)
            for tl in range(TILES):
                tt(tok[:, tl, :], tok[:, tl, :], lnb, ALU.add).then_inc(s_xbr, 1)
                own.done(s_xbr)

            def deviation(k, tl, n):
                own.link(nc.gpsimd.tensor_scalar(vare[:, 0:n], mv[:, k, tl:tl + n, 1], EPS, None, ALU.add))
                tt(rstd[:, k, tl:tl + n], vare[:, 0:n], cols[:, 5:6].broadcast_to((P, n)), ALU.pow).then_inc(s_rstd[k], 1)
                own.done(s_rstd[k])

            for q in range(NQ + 1):
                if q < NQ:
                    pool.wait_ge(s_stat[0], q + 1)
                    deviation(0, 2 * q, 2)
                if q >= 1:
                    pool.wait_ge(s_stat[1], q)
                    deviation(1, 2 * q - 2, 2)
            for s in range(NSUP + 1):
                f = s - 1
                if s < NSUP:
                    pool.wait_ge(s_tmm, T_AT[("x1", s, 1)] + 1)
                    for i in range(SUPER):
                        tl = SUPER * s + i
                        tt(tok[:, tl, :], tok[:, tl, :], bo, ALU.add).then_inc(s_bo, 1)
                        own.done(s_bo)
                if s >= 1:
                    pool.wait_ge(s_tmm, T_AT[("x2", f, 1)] + 1)
                    for i in range(SUPER):
                        tl = SUPER * f + i
                        tt(tok[:, tl, :], tok[:, tl, :], bd, ALU.add).then_inc(s_bd, 1)
                        own.done(s_bd)
                for i in range(SUPER):
                    rt = SUPER * f + i
                    if s >= 1:
                        pool.wait_ge(s_wact, W_FREE[W_AT[("sim", f, i)]][1])
                        for h in range(FH):
                            n = FH * rt + h
                            if n >= 2:
                                pool.wait_ge(s_rfr, n - 1)
                            tt(sxb[n % 2], sim[:, rt % 2, h, 0:XR].unsqueeze(2).broadcast_to((P, XR, NKEYS)),
                               sim[:, rt % 2, FH + h, :].unsqueeze(1).broadcast_to((P, XR, NKEYS)), ALU.add).then_inc(s_sx, 1)
                            own.done(s_sx)
                    if s < NSUP:
                        pool.wait_ge(s_stat[2], SUPER * s + i + 1)
                        deviation(2, SUPER * s + i, 1)
                if s >= 1:
                    for i in range(SUPER):
                        pool.wait_ge(s_stat[3], SUPER * f + i + 1)
                        deviation(3, SUPER * f + i, 1)

        @block.vector
        def _(dve):
            own = Steps(dve, s_dve)
            link, mark, need = own.link, own.mark, own.need
            V = nc.vector
            tt, ts, stt = V.tensor_tensor, V.tensor_scalar, V.scalar_tensor_tensor
            w = wk_

            def exact_exp(out, x, a, b, c):
                link(ts(a, x, 1.4426950408889634, MAGIC, ALU.mult, ALU.add))
                link(ts(a, a, MAGIC, None, ALU.subtract))
                link(stt(b, a, -0.693359375, x, ALU.mult, ALU.add))
                link(stt(b, a, 2.12194440e-4, b, ALU.mult, ALU.add))
                link(ts(c, b, 1.0 / 40320, None, ALU.mult))
                for k in (5040, 720, 120, 24, 6, 2, 1):
                    link(stt(c, c, 1.0 / k, b, ALU.add, ALU.mult))
                link(ts(a.bitcast(I32), a, 127.0, 8388608.0, ALU.add, ALU.mult))
                link(stt(out, c, 1.0, a, ALU.add, ALU.mult))

            dve.wait_ge(s_ssm, 64)
            logdt, loga, aim, cre, cim = (ssm[:, i, :] for i in range(5))
            exact_exp(w[0], logdt, w[10], w[11], w[12])
            link(tt(w[2], w[0], aim, ALU.mult))
            link(ts(w[2], w[2], 0.15915494309189535, None, ALU.mult))
            link(ts(w[10], w[2], MAGIC, None, ALU.add))
            stt(w[2], w[10], MAGIC, w[2], ALU.subtract, ALU.subtract).then_inc(s_small_ready, 1)
            own.done(s_small_ready)
            exact_exp(w[13], loga, w[10], w[11], w[12])
            link(ts(w[13], w[13], -1.0, None, ALU.mult))
            tt(w[1], w[13], w[0], ALU.mult).then_inc(s_small_ready, 1)
            own.done(s_small_ready)
            link(ts(w[7], w[1], float(HALF), None, ALU.mult))
            link(ts(w[8], w[2], float(HALF), None, ALU.mult))
            link(ts(w[10], w[8], MAGIC, None, ALU.add))
            stt(w[8], w[10], MAGIC, w[8], ALU.subtract, ALU.subtract).then_inc(s_base, 1)
            own.done(s_base)

            def context():
                for oc in range(KC):
                    dve.wait_ge(s_cm, oc + 1)
                    dve.wait_ge(s_ctx, 16 * 7)
                    ts(kT[:, oc, :], bank[4 + oc][:, 0:B * NKV], pcol[:, 2 + oc:3 + oc], HD ** -0.5,
                       ALU.add, ALU.mult).then_inc(s_kt, 1)
                    own.done(s_kt)
                link(V.memset(vaug, 1.0))
                for b in range(B):
                    dve.wait_ge(s_cm, 3 + b)
                    ins = tt(vaug[:, b, :, 0:HD], bank[6 + b][0:NKV, 0:D].rearrange("p (h d) -> p h d", d=HD),
                             bv[0:NKV].rearrange("p (h d) -> p h d", d=HD), ALU.add)
                    if b == 0:
                        link(ins)
                    else:
                        ins.then_inc(s_kbz, 1)
                        own.done(s_kbz)

            def expand(v):
                return v.unsqueeze(2).broadcast_to((P, GRP, HALF))

            st3 = steps[:, :].unsqueeze(1).broadcast_to((P, GRP, HALF))

            def phases(g):
                ch = slice(GRP * g, GRP * g + GRP)
                link(tt(tq, expand(w[2][:, ch]), st3, ALU.mult))
                link(ts(trd, tq, cols[:, 0:1], MAGIC, ALU.add, ALU.add))
                stt(tq, trd, MAGIC, tq, ALU.subtract, ALU.subtract).then_inc(s_phase, 1)
                own.done(s_phase)
                link(tt(tp, expand(w[8][:, ch]), st3, ALU.mult))
                link(ts(trd, tp, MAGIC, None, ALU.add))
                link(stt(tp, trd, MAGIC, tp, ALU.subtract, ALU.subtract))
                stt(trd, tp, -1.0, tp, ALU.mult, ALU.max).then_inc(s_phase, 1)
                own.done(s_phase)

            def mode_weights():
                dve.wait_ge(s_small_act, 4)
                sb_, sh, th, ea = w[3], w[4], w[5], w[6]
                link(tt(sh, sh, sh, ALU.mult))
                link(tt(sh, sh, ea, ALU.mult))
                link(ts(w[10], th, -1.0, 1.0, ALU.mult, ALU.add))
                link(V.reciprocal(w[10], w[10]))
                link(tt(w[10], w[10], th, ALU.mult))
                link(tt(w[10], w[10], sh, ALU.subtract))
                link(ts(w[10], w[10], 2.0, None, ALU.mult))
                link(tt(w[11], sb_, ea, ALU.mult))
                link(tt(w[3], w[13], w[13], ALU.mult))
                link(tt(w[4], aim, aim, ALU.mult))
                link(tt(w[3], w[3], w[4], ALU.add))
                link(V.reciprocal(w[3], w[3]))
                link(tt(w[4], w[10], w[13], ALU.mult))
                link(tt(w[5], w[11], aim, ALU.mult))
                link(tt(w[4], w[4], w[5], ALU.add))
                link(tt(w[5], w[11], w[13], ALU.mult))
                link(tt(w[6], w[10], aim, ALU.mult))
                link(tt(w[5], w[5], w[6], ALU.subtract))
                link(tt(w[4], w[4], w[3], ALU.mult))
                link(tt(w[5], w[5], w[3], ALU.mult))
                link(tt(w[10], cre, w[4], ALU.mult))
                link(tt(w[11], cim, w[5], ALU.mult))
                link(tt(w[10], w[10], w[11], ALU.subtract))
                link(tt(w[11], cre, w[5], ALU.mult))
                link(tt(w[12], cim, w[4], ALU.mult))
                link(tt(w[11], w[11], w[12], ALU.add))
                link(ts(w[12], w[11], cols[:, 3:4], None, ALU.mult))
                link(stt(w[14], w[10], cols[:, 2:3], w[12], ALU.mult, ALU.add))
                link(ts(w[12], w[11], cols[:, 2:3], None, ALU.mult))
                stt(w[9], w[10], cols[:, 3:4], w[12], ALU.mult, ALU.subtract).then_inc(s_base, 1)
                own.done(s_base)

            def tables(g):
                ch = slice(GRP * g, GRP * g + GRP)
                dve.wait_ge(s_trig, g + 1)
                link(tt(tqm, tqm, tq, ALU.mult))
                link(tt(tpc, tpc, expand(w[14][:, ch]), ALU.mult))
                dve.wait_ge(s_bsin, g + 1)
                link(tt(tpc, tpc, tp, ALU.add))
                tt(tpm, tpm, tpc, ALU.mult).then_inc(s_tab, 1)
                own.done(s_tab)

            phases(0)
            mode_weights()
            context()
            tables(0)
            for g in range(1, NGRP):
                phases(g)
                tables(g)
            dve.wait_ge(s_base, 2)
            dve.wait_ge(s_kev, 16)
            stt(ktime[0:1, 0, :], skip[0:1, :], 1.0, ktime[0:1, 0, :], ALU.add, ALU.add).then_inc(s_kdone, 1)
            own.done(s_kdone)
            for i in range(NQ):
                dve.wait_ge(s_ka, i + 1)
                qp, h = divmod(i, 2)
                V.tensor_copy(kA[:, h, 2 * qp:2 * qp + 2, :].rearrange("p a b -> p (a b)"),
                              bank[i % 4][:, :]).then_inc(s_kae, 1)
                own.done(s_kae)
            for k1 in range(FREQ):
                dve.wait_ge(s_xf, k1 + 1)
                dve.wait_ge(s_kfe, k1 + 1)
                if k1 == 0:
                    dve.wait_ge(s_kaw, 16 * 2 * NQ)
                bb = 2 * (k1 % 2)
                pr = prod[:, k1 % 2]
                for out, kk in ((0, 0), (1, 1)):
                    for c in range(2):
                        dst = pr[:, out, 512 * c:512 * c + 512].rearrange("p (b n) -> p b n", b=B)
                        ins = tt(dst, bank[bb + c][:, :].rearrange("p (b n) -> p b n", b=B),
                                 kf[:, k1, kk, :].unsqueeze(1).broadcast_to((P, B, D)), ALU.mult)
                ins.then_inc(s_pr, 1)
                own.done(s_pr)
                if k1 >= 2:
                    dve.wait_ge(s_z, k1 - 1)
                y = yf[:, k1 % 2]
                link(tt(y[:, 0, :], pr[:, 0, 0:512], pr[:, 1, 512:1024], ALU.subtract))
                tt(y[:, 1, :], pr[:, 0, 512:1024], pr[:, 1, 0:512], ALU.add).then_inc(s_yf, 1)
                own.done(s_yf)

            def statistics(k, tl, src, last):
                link(V.bn_stats(stats[:, tl % 2, :], src))
                ins = V.bn_aggr(mv[:, k, tl, :], stats[:, tl % 2, :])
                if last:
                    ins.then_inc(s_stat[k], 1)
                    own.done(s_stat[k])
                else:
                    link(ins)

            def normalise(k, tl, s_done, last=True):
                ins = ts(tok[:, tl, :], tok[:, tl, :], mv[:, k, tl, 0:1], rstd[:, k, tl:tl + 1], ALU.subtract, ALU.mult)
                if last:
                    ins.then_inc(s_done, 1)
                    own.done(s_done)
                else:
                    link(ins)

            for q in range(NQ + 2):
                if q < NQ:
                    dve.wait_ge(s_r, q + 1)
                    for b in range(B):
                        statistics(0, 2 * q + b, bank[q % 4][:, D * b:D * b + D], b == 1)
                if 1 <= q <= NQ:
                    z = q - 1
                    dve.wait_ge(s_rstd[0], z + 1)
                    dve.wait_ge(s_xbr, 2 * z + 2)
                    for b in range(B):
                        tl = 2 * z + b
                        ins = stt(gtmp[:, b, :], bank[z % 4][:, D * b:D * b + D], mv[:, 0, tl, 0:1], lnw, ALU.subtract, ALU.mult)
                        if b:
                            ins.then_inc(s_rfree, 1)
                            own.done(s_rfree)
                        else:
                            link(ins)
                    for b in range(B):
                        tl = 2 * z + b
                        link(stt(tok[:, tl, :], gtmp[:, b, :], rstd[:, 0, tl:tl + 1], tok[:, tl, :], ALU.mult, ALU.add))
                        statistics(1, tl, tok[:, tl, :], b == 1)
                if q >= 2:
                    z = q - 2
                    dve.wait_ge(s_rstd[1], z + 1)
                    for b in range(B):
                        normalise(1, 2 * z + b, s_x1, b == 1)
            link(ts(bgh, pcol[:, 4:4 + FC], 0.5, None, ALU.mult))

            def shift_scores(tl):
                for hh in range(KC):
                    dve.wait_ge(s_smm, 2 * tl + hh + 1)
                    if tl >= 2:
                        dve.wait_ge(s_tmm, T_AT[("p", tl - 2, 2)] + 1)
                    m = smax[:, 0:8].rearrange("p (a h) -> p a h", a=2)
                    dst = prob[:, tl % 2, 8 * NKV * hh:8 * NKV * (hh + 1)].rearrange("p (a n) -> p a n", a=2)
                    for g in range(2):
                        src = bank[g][:, 0:GH * NKV].rearrange("p (h k) -> p h k", k=NKV)
                        link(V.tensor_reduce(m[:, g, :], src, AX_X, ALU.max))
                    for g in range(2):
                        src = bank[g][:, 0:GH * NKV].rearrange("p (h k) -> p h k", k=NKV)
                        ins = tt(dst[:, g, :].rearrange("p (h k) -> p h k", k=NKV), src,
                                 m[:, g, :].unsqueeze(2).broadcast_to((P, GH, NKV)), ALU.subtract)
                        if g:
                            ins.then_inc(s_ssub, 1)
                            own.done(s_ssub)
                        else:
                            link(ins)

            def best_pairs(rt):
                dve.wait_ge(s_wact, W_FREE[W_AT[("sim", rt // SUPER, rt % SUPER)]][1])
                for m in range(2 * FH):
                    link(V.max(best[:, m, :], sim[:, rt % 2, m, :]))
                link(tt(pairs.rearrange("p h (a b) -> p h a b", a=TOPK),
                        best[:, 0:FH, :].unsqueeze(3).broadcast_to((P, FH, TOPK, TOPK)),
                        best[:, FH:2 * FH, :].unsqueeze(2).broadcast_to((P, FH, TOPK, TOPK)), ALU.add))
                tp_ = top[:, rt % 2]
                for h in range(FH):
                    link(V.max(tp_[:, h, :], pairs[:, h, :]))
                ts(negm[:, rt % 2, :], tp_[:, :, 0], -1.0, None, ALU.mult).then_inc(s_best, 1)
                own.done(s_best)
                tt(zexp, tp_, tp_[:, :, 0:1].broadcast_to((P, FH, TOPK)), ALU.subtract).then_inc(s_zarg, 1)
                own.done(s_zarg)

            def silus(f, i):
                for k in range(2):
                    n, c = 16 * f + 4 * i + k, 2 * i + k
                    dve.wait_ge(s_wact, W_FREE[W_AT[("e", f, c)]][1])
                    stt(silg[:, c, :], tg[:, n % 2, 0, :], 1.0, tg[:, n % 2, 1, :], ALU.add, ALU.mult).then_inc(s_tgf, 1)
                    own.done(s_tgf)
                for k in range(2):
                    n, c = 16 * f + 4 * i + 2 + k, 2 * i + k
                    dve.wait_ge(s_wact, W_FREE[W_AT[("g", f, c)]][1])
                    stt(gate, tg[:, n % 2, 0, :], 1.0, tg[:, n % 2, 1, :], ALU.add, ALU.mult).then_inc(s_tgf, 1)
                    own.done(s_tgf)
                    u = W_AT[("u", f, c)]
                    dve.wait_ge(s_wmm, u + 1)
                    if f:
                        dve.wait_ge(s_7mm, 3 * SUPER * f)
                    stt(hid[:, c, :], bank[5 + u % 2][:, :], pcol[:, 4 + FC + c:5 + FC + c], gate,
                        ALU.add, ALU.mult).then_inc(s_wdve, 1)
                    own.done(s_wdve)

            def expert_weights(rt):
                dve.wait_ge(s_zexp, rt + 1)
                link(V.tensor_reduce(zinv, zexp, AX_X, ALU.add))
                link(V.reciprocal(zinv, zinv))
                r_ = rw[:, rt % SUPER, :]
                if rt >= SUPER:
                    dve.wait_ge(s_7mm, 3 * (rt - SUPER) + 2)
                for h in range(FH):
                    n = FH * rt + h
                    e = ebuf[n % 2].rearrange("p a b -> p (a b)")
                    dve.wait_ge(s_e, n + 1)
                    link(stt(e, sxb[n % 2].rearrange("p a b -> p (a b)"), top[:, rt % 2, h, TOPK - 1:TOPK], e,
                             ALU.is_ge, ALU.mult))
                    if h == 0:
                        ts(r_, e, zinv[:, h:h + 1], None, ALU.mult).then_inc(s_rfr, 1)
                    else:
                        stt(r_, e, zinv[:, h:h + 1], r_, ALU.mult, ALU.add,
                            accum_out=rsum[:, 0:1] if h == FH - 1 else None).then_inc(s_rfr, 1)
                    own.done(s_rfr)
                link(ts(rsum[:, 1:2], rsum[:, 0:1], -1.0, float(FH), ALU.mult, ALU.add))
                tt(r_[:, NEXP - 1:NEXP], r_[:, NEXP - 1:NEXP], rsum[:, 1:2], ALU.add).then_inc(s_rr, 1)
                own.done(s_rr)

            def attention_out(tl):
                dve.wait_ge(s_pv, tl + 1)
                o3 = bank[4][:, 0:HEADS * (HD + 1)].rearrange("p (h d) -> p h d", d=HD + 1)
                link(V.reciprocal(rec.unsqueeze(2), o3[:, :, HD:HD + 1]))
                if tl >= 2:
                    dve.wait_ge(s_tmm, T_AT[("o", tl - 2, 0)] + 1)
                tt(ob[:, tl % 2, :].rearrange("p (h d) -> p h d", d=HD), o3[:, :, 0:HD],
                   rec.unsqueeze(2).broadcast_to((P, HEADS, HD)), ALU.mult).then_inc(s_on, 1)
                own.done(s_on)

            def residual(k, tl, src):
                tt(tok[:, tl, :], src, tok[:, tl, :], ALU.add).then_inc(s_u[k - 2], 1)
                own.done(s_u[k - 2])
                statistics(k, tl, tok[:, tl, :], True)
                dve.wait_ge(s_rstd[k], tl + 1)
                normalise(k, tl, s_x2 if k == 2 else s_out)

            for s in range(NSUP + 1):
                f = s - 1
                for i in range(SUPER):
                    tl, rt = SUPER * s + i, SUPER * f + i
                    if s < NSUP:
                        shift_scores(tl)
                    if s >= 1:
                        best_pairs(rt)
                        silus(f, i)
                        expert_weights(rt)
                    if s < NSUP:
                        attention_out(tl)
                        dve.wait_ge(s_wo, tl + 1)
                        dve.wait_ge(s_bo, tl + 1)
                        residual(2, tl, bank[4][:, 0:D])
                if s >= 1:
                    for i in range(SUPER):
                        rt = SUPER * f + i
                        for j in range(2):
                            dve.wait_ge(s_7mm, 3 * rt + j + 1)
                            tt(aT[:, 4 * j:4 * j + 4, :], bank[7][:, :].rearrange("p (c n) -> p c n", n=P),
                               silg[:, 4 * j:4 * j + 4, P * i:P * i + P], ALU.mult).then_inc(s_7f, 1)
                            own.done(s_7f)
                        dve.wait_ge(s_7mm, 3 * rt + 3)
                        dve.wait_ge(s_bd, rt + 1)
                        tt(tok[:, rt, :], bank[7][:, 0:D], tok[:, rt, :], ALU.add).then_inc(s_7f, 1)
                        own.done(s_7f)
                        statistics(3, rt, tok[:, rt, :], True)
                        dve.wait_ge(s_rstd[3], rt + 1)
                        normalise(3, rt, s_out)


SHAPES = {}


def kernel(**inputs):
    import concourse.bacc as bacc
    from concourse.bass_utils import run_bass_kernel_spmd

    g = {k: np.asarray(v) for k, v in inputs.items()}

    def by_chunk(a):
        return np.ascontiguousarray(a.reshape(-1, P, a.shape[-1]).transpose(1, 0, 2))

    def both(a):
        return np.concatenate([a.T, a.T], axis=0)

    def every(a):
        return np.tile(a[None, :], (P, 1))

    fa, fai, fmat, imat = fourier_constants()
    cols, ident, head_mask, shift, steps = mask_constants()
    x = g["x"].reshape(B, NC, NQ, NS, D).transpose(1, 3, 2, 0, 4).reshape(P, TILES, D)
    ctx = g["ctx_1024"].reshape(B * NKV, D)
    keys = g["L0_ffn_keys"].transpose(3, 2, 0, 1).reshape(NKEYS, 2 * FH, NKEYS)
    arrays = {
        "ssm": np.stack([every(g["L0_attn_log_dt"]), both(g["L0_attn_log_A_real"]), both(g["L0_attn_A_imag"]),
                         both(g["L0_attn_C_re"]), both(g["L0_attn_C_im"])], axis=1),
        "skip": g["L0_attn_D"][None, :],
        "cols": cols, "steps": steps, "fa": fa, "fai": fai, "fmat": fmat, "imat": imat, "x": x,
        "ctxT": by_chunk(ctx.T), "wk": by_chunk(g["L0_xattn_Wk"].T), "wv": by_chunk(g["L0_xattn_Wv"].T),
        "wq": by_chunk(g["L0_xattn_Wq"].T), "wo": by_chunk(g["L0_xattn_Wo"].T),
        "pcol": np.concatenate([v.reshape(-1, P).T for v in (
            g["L0_xattn_bq"], g["L0_xattn_bk"], g["L0_ffn_bg"], g["L0_ffn_bu"])], axis=1),
        "rows": np.stack([every(g[n]) for n in (
            "L0_attn_ln_w", "L0_attn_ln_b", "L0_xattn_bo", "L0_ffn_bd", "L0_xattn_bv")], axis=1),
        "shift": shift, "head_mask": head_mask, "ident": ident,
        "wqf": g["L0_ffn_Wq"].T.reshape(2 * FH, NKEYS, D).transpose(1, 0, 2), "keysT": keys,
        "wg": by_chunk(g["L0_ffn_Wg"]), "wu": by_chunk(g["L0_ffn_Wu"]), "wd": by_chunk(g["L0_ffn_Wd"]),
        "dn": by_chunk(g["L0_ffn_down_embed"].T), "up": by_chunk(g["L0_ffn_up_embed"]),
    }
    arrays = {f"in_{k}": np.ascontiguousarray(v) for k, v in arrays.items()}
    nc = bacc.Bacc("TRN2", target_bir_lowering=False, num_devices=1)
    t = {k[3:]: nc.dram_tensor(k, v.shape, F32, kind="ExternalInput").ap() for k, v in arrays.items()}
    for name, shape in (("scr_x", (NQ, NSLOT, NS, B * D)), ("scr_k", (NQ, NSLOT, NS, D)),
                        ("scr_t", (HALF, HALF, D)), ("scr_z", (NSLOT, P, B * D))):
        t[name] = nc.dram_tensor(name, shape, F32, kind="Internal").ap()
    t["out"] = nc.dram_tensor("out", (P, TILES, D), F32, kind="ExternalOutput").ap()
    build(nc, t)
    r = run_bass_kernel_spmd(nc, [arrays], core_ids=[0])
    out = r.results[0]["out"].reshape(NC, NS, NQ, B, D)
    return np.ascontiguousarray(out.transpose(3, 0, 2, 1, 4).reshape(B, L, D))
```

```python
from contextlib import ExitStack

import numpy as np

import concourse.bass as bass
from concourse import mybir

ALU = mybir.AluOpType
ACT = mybir.ActivationFunctionType
AX_X = mybir.AxisListType.X
F32 = mybir.dt.float32
I32 = mybir.dt.int32

P = 128
B, L, D = 2, 1024, 256
NST = 64
NFFT = 2 * L
NC, NQ, NS = 8, 8, 16
KC = D // P
TILES = B * L // P
SUPER = 4
NSUP = TILES // SUPER
W = SUPER * P
NSLOT = 16
FREQ = 9
NKV, HEADS, HD = 77, 16, 16
GH = 4
FLAT = HEADS * NKV
PCH = (FLAT + P - 1) // P
FF = 1024
NEXP, NKEYS, FH, TOPK = 1024, 64, 4, 8
XR = NEXP // NKEYS
FC, EC = FF // P, NEXP // P
MAGIC = 1.5 * 2.0**23
TWO_PI = 6.283185
EPS = 1e-5
GRP = 32
NGRP = D // GRP
HC = D // 2
GH_ = NGRP // 2
ZRING = 4
HALF = 32


def slot_of(k1, part):
    if k1 in (0, 8):
        return k1 // 8
    return 2 * k1 + part


def mat_of(k1, kind):
    if k1 == 0:
        return {0: 0, 2: 1}[kind]
    if k1 == 8:
        return {0: 2, 2: 3}[kind]
    return 4 + 3 * (k1 - 1) + kind


NMAT = 4 + 3 * 7

PLACE = {"probs": (0.02, 0.12, 0.22), "score": (0.45, 0.65), "attend": (0.55,), "turno": (0.85,), "project": (1.3,),
         "project_last": (0.95,), "turn1": (0.02, 0.05), "query": (0.2, 0.25), "turn2": (0.06, 0.07),
         "sim": (0.3,), "sim_first": (0.08,), "best": (0.7,), "best_first": (0.09,),
         "pair": (0.15, 0.35, 0.57, 0.8), "total": (0.9,), "sums": (-0.3,), "exps": (-0.15,), "late": (0.0, 0.01, 0.02),
         "conv": (-1.8, -1.6, -0.9, -0.65, 0.3, 0.7, 1.3, 1.7), "conv_steps": (0.0, 0.02, 0.15, 0.17, 0.3),
         "phases": (-1.5,), "exponents": (-1.2,), "sines": (-1.0,), "decays": (-0.8, -1.2), "weigh": (-0.7,),
         "tables": (-0.4,), "taps": (0.0,), "x_second": (1.3, 0.55), "skip": (0.3,), "k_first": (4.6, 8.4),
         "simw": (-0.3,), "values": (0.4,), "diagonal": (-0.6,),
         "k_second": (6.3, 0.05, 9.5, 0.05), "spectra": (7.7, 0.12, 10.0, 0.12),
         "inverse": (7.8, 0.12, 10.1, 0.12),
         "dev2": (0.04,), "norm2": (0.08,), "dev3": (0.05,), "norm3": (0.1,)}
LAG = {("act", "x_second"): 0.2, ("act", "taps"): 0.3, ("act", "k_first"): 0.1, ("act", "k_second"): 0.1,
       ("act", "inverse"): 0.1,
       ("dve", "score"): 0.02, ("act", "score"): 0.08, 
       ("act", "best"): 0.03, ("dve", "attend"): 0.02, ("dve", "expert"): 0.15, ("dve", "inner"): 0.15,
       ("dve", "outer"): 0.05, ("dve", "spread"): 0.03, ("dve", "project"): 0.03}


def image_of(k1):
    return NSLOT + k1 // 8 if k1 in (0, 8) else slot_of(k1, 1)


def conv_bank(q):
    return 4 if q in (0, 2) else 7


def heads_of(chunk):
    return chunk * P // NKV, min((chunk * P + P - 1) // NKV, HEADS - 1)


def plan():
    steps = []

    def put(start, kind, n, *rest, key=None, j=0):
        steps.append((start + PLACE[key or kind][j], (kind, n) + rest))
        return steps[-1][0]

    def queries(start, s):
        for kind in ("turn1", "query"):
            for j in range(2):
                put(start, kind, s, j, j=j)

    def normed(at, tl, k):
        put(at, f"dev{k}", tl)
        put(at, f"norm{k}", tl)

    def products(f, i):
        r = SUPER * f
        if i == 0:
            return [("expert", f, c) for c in range(6)]
        if i == 1:
            return [("expert", f, 6), ("expert", f, 7)] + [("inner", f, c) for c in range(4)]
        if i == 2:
            return [("inner", f, c) for c in range(4, 8)] + [("spread", r, 0), ("spread", r, 1)]
        return [("outer", r), ("spread", r + 1, 0), ("spread", r + 1, 1), ("outer", r + 1),
                ("spread", r + 2, 0), ("spread", r + 2, 1), ("outer", r + 2)]

    for q in range(NQ):
        at = PLACE["conv"][q]
        for k, kind in enumerate(("conv", "dev0", "residual", "dev1", "norm1")):
            steps.append((at + PLACE["conv_steps"][k], (kind, q)))
    queries(-1, 0)
    for h in range(2):
        put(-1, "score", 0, h, j=h)
    for tl in range(TILES):
        s, i = divmod(tl, SUPER)
        start = tl
        for j in range(3):
            put(start, "probs", tl, j, j=j)
        put(start, "attend", tl)
        put(start, "turno", tl)
        normed(put(start, "project", tl, key="project_last" if i == SUPER - 1 else "project"), tl, 2)
        if i == SUPER - 1 and s + 1 < NSUP:
            queries(start, s + 1)
        if tl + 1 < TILES:
            for h in range(2):
                put(start, "score", tl + 1, h, j=h)
        start = tl + SUPER
        if i == 0:
            for j in range(2):
                put(start, "turn2", s, j, j=j)
            put(start, "sim", tl, key="sim_first")
            put(start, "best", tl, key="best_first")
        work = products(s, i)
        for k, y in enumerate(work):
            at = start + (k + 0.5) / len(work)
            steps.append((at, y))
            if y[0] == "outer":
                normed(at, y[1], 3)
        for h in range(FH):
            at = put(start, "pair", tl, h, j=h)
            for kind in ("sums", "exps"):
                steps.append((max(at + PLACE[kind][0], start + PLACE["best_first"][0] + 0.01 if i == 0 else at - 1.0),
                              (kind, tl, h)))
        put(start, "total", tl)
        if i < SUPER - 1:
            put(start, "sim", tl + 1)
            put(start, "best", tl + 1)
        else:
            for j in range(2):
                put(start + 1, "spread", tl, j, key="late", j=j)
            normed(put(start + 1, "outer", tl, key="late", j=2), tl, 3)
    return steps


def head():
    steps = []
    steps += [(PLACE["simw"][0], ("simw", 0)), (PLACE["values"][0], ("values", 0)),
              (PLACE["diagonal"][0], ("diagonal", 0))]
    for g in range(NGRP):
        for kind in ("phases", "exponents", "sines", "weigh", "tables", "taps"):
            steps.append((g + PLACE[kind][0], (kind, g)))
        steps.append((g + PLACE["decays"][g % 2], ("decays", g)))
    for k in range(FREQ):
        steps.append((PLACE["x_second"][0] + PLACE["x_second"][1] * k, ("x_second", k)))
    for hf in range(2):
        steps.append((GH_ * (hf + 1) - 1 + PLACE["skip"][0], ("skip", hf)))
        steps.append((PLACE["k_first"][hf], ("k_first", hf)))
        for kind in ("k_second", "spectra", "inverse"):
            for k in range(FREQ):
                steps.append((PLACE[kind][2 * hf] + PLACE[kind][2 * hf + 1] * k, (kind, FREQ * hf + k)))
    return steps


def order(steps, engine):
    return [y for _, y in sorted(steps, key=lambda v: v[0] + LAG.get((engine, v[1][0]), 0.0))]


def fourier_constants():
    c, s = np.divmod(np.arange(P), NS)
    fwd = np.zeros((P, NSLOT, NS))
    inv = np.zeros((NSLOT, NS, P))
    for k1 in range(FREQ):
        ang = 2 * np.pi * k1 * c / NSLOT
        own = 1.0 if k1 in (0, 8) else 2.0
        fwd[np.arange(P), slot_of(k1, 0), s] = np.cos(ang)
        inv[slot_of(k1, 0), s, np.arange(P)] = own * np.cos(ang) / NFFT
        if k1 not in (0, 8):
            fwd[np.arange(P), slot_of(k1, 1), s] = -np.sin(ang)
            inv[slot_of(k1, 1), s, np.arange(P)] = -own * np.sin(ang) / NFFT
    fmat, imat = np.zeros((P, NMAT, P)), np.zeros((P, NMAT, P))
    pp, kk = np.meshgrid(np.arange(P), np.arange(P), indexing="ij")
    for k1 in range(FREQ):
        ang = 2 * np.pi * ((pp * (k1 + 16 * kk)) % NFFT) / NFFT
        for kind, m in ((0, np.cos(ang)), (1, np.sin(ang)), (2, -np.sin(ang))):
            if kind == 1 and k1 in (0, 8):
                continue
            fmat[:, mat_of(k1, kind)] = m
            imat[:, mat_of(k1, kind)] = m.T
    inv = inv.reshape(2, P, P).transpose(1, 0, 2)
    return [np.ascontiguousarray(a, dtype=np.float32) for a in (fwd.reshape(P, 2, P), inv, fmat, imat)]


def mask_constants():
    cols = np.zeros((P, 8), np.float32)
    cols[:64, 0] = -0.25
    cols[:64, 1] = np.pi / 2
    cols[:64, 2] = 2.0
    cols[64:, 3] = -2.0
    cols[:, 4] = np.pi / 2
    cols[:, 5] = -0.5
    ident = np.eye(P, dtype=np.float32)
    head_mask = np.zeros((P, P // HD), np.float32)
    head_mask[np.arange(P), np.arange(P) // HD] = 1.0
    shift = np.zeros((NKV, 3 * P), np.float32)
    shift[np.arange(NKV), np.arange(NKV) + P] = 1.0
    steps = np.tile(np.arange(HALF, dtype=np.float32), (P, 1))
    return [cols, ident, head_mask, shift, steps]


def build(nc, t):
    with ExitStack() as ctx:
        def sb(name, shape, dt=F32):
            return ctx.enter_context(nc.sbuf_tensor(name, shape, dt))

        def sem(name):
            return ctx.enter_context(nc.semaphore(name))

        bank = [ctx.enter_context(nc.psum_tensor(f"bank{i}", [P, 512], F32)) for i in range(8)]

        tok = sb("tok", [P, TILES, D])
        wq = sb("wq", [P, KC, D])
        wo = sb("wo", [P, KC, D])
        wsim = sb("wsim", [P, KC, 2 * FH * NKEYS])
        rows = sb("rows", [P, 5, D])
        lnw, lnb, bo, bd, bv = (rows[:, i, :] for i in range(5))
        pcol = sb("pcol", [P, 4 + 2 * FC])
        ident = sb("ident", [P, P])
        cols = sb("cols", [P, 8])
        head_mask = sb("head_mask", [P, P // HD])
        steps = sb("steps", [P, HALF])
        kbd = sb("kbd", [P, B, KC, 8 * NKV])
        vbd = sb("vbd", [P, B, PCH, 51])
        stats = sb("stats", [P, 2, 6])
        mv = sb("mv", [P, 4, TILES, 2])
        rstd = sb("rstd", [P, 4, TILES])
        mexp = sb("mexp", [P, 2, FH])
        skip = sb("skip", [1, D])

        WORDS = 41600
        arena = sb("arena", [P, WORDS])
        place = {}

        def part(name, start, *dims, rows_=P):
            n = int(np.prod(dims))
            assert start + n <= WORDS, (name, start, n)
            place[name] = (start, start + n)
            v = arena[0:rows_, start:start + n]
            if len(dims) == 1:
                return v
            names = "abcde"[:len(dims)]
            return v.rearrange(f"p ({' '.join(names)}) -> p {' '.join(names)}",
                               **{k: d for k, d in zip(names, dims)})

        o_a, o_b, o_tab, o_par, o_mat, o_u = 0, 8192, 17408, 28672, 33792, 37504
        cA = part("cA", o_a, 2, NQ, 512)
        ktime = part("ktime", o_a, HALF, HC, rows_=HALF)
        kQ = part("kQ", o_a + 4096, NQ, HC)
        kS = [part("kS0", o_a + 5120, NSLOT + 2, HC), part("kS1", o_tab + 8192, NSLOT + 2, HC)]
        kA = [part("kA0", o_a + 5120, 2, NQ, HC), part("kA1", o_tab + 8192, 2, NQ, HC)]
        xS = part("xS", o_b, NSLOT + 2, 512)
        prod = part("prod", o_u, 2, 2, B, HC)
        yf = part("yf", o_u + 1024, 2, 2, 2 * HC)
        zring = part("zring", o_u + 2048, ZRING, 2, 2 * HC)
        zB = part("zB", o_tab, 2, 2, NQ, 2 * HC)
        tq, tqm, tp, tpm, tpc = ([part(f"tab{i}{d}", o_tab + 2048 * i + 1024 * d, GRP, HALF) for d in range(2)]
                                 for i in range(5))
        trd = part("trd", o_tab + 10240, GRP, HALF)
        wqf = part("wqf", o_u, 2 * FH, D, rows_=NKEYS)
        keysT = part("keysT", o_u + 2048, 2 * FH, NKEYS, rows_=NKEYS)
        wk = part("wk", o_b, KC, D)
        wv = part("wv", o_b + 512, KC, D)
        ctxT = part("ctxT", o_b + 1024, KC, B * NKV)
        kT = part("kT", o_u + 2560, KC, B * NKV)
        vaug = part("vaug", o_u + 2868, B, HEADS, HD + 1, rows_=NKV)
        shift = part("shift", o_u + 3412, 3 * P, rows_=NKV)
        wk_ = [None] * 15
        for j, i in enumerate((1, 2, 7, 8, 9, 14, 0, 3, 4, 5, 6, 10, 11, 12, 13)):
            wk_[i] = part(f"w{i}", o_par + D * j, D)
        ssm = part("ssm", o_par + 15 * D, 5, D)
        imat = part("imat", o_par + 6 * D, NMAT, P)
        fmat = part("fmat", o_mat, NMAT, P)
        fa = part("fa", o_mat + 3200, 2, P)
        fai = part("fai", o_mat + 3456, 2, P)

        o_wt = 16384
        wg, wu, dn = (part(n, o_wt + 2048 * i, KC, FF) for i, n in ((0, "wg"), (1, "wu"), (3, "dn")))
        wd, up = (part(n, o_wt + 2048 * i, FC, D) for i, n in ((2, "wd"), (4, "up")))
        o_w = o_wt + 10240
        silg = part("silg", o_w, EC, W)
        hid = part("hid", o_w + 4096, FC, W)
        x2T = part("x2T", o_w + 8192, KC, W)
        sim = part("sim", o_w + 9216, 2, 2 * FH, NKEYS)
        ebuf = [part("ebuf0", o_w + 10240, XR, NKEYS)]
        o_l = o_w + 11264
        ebuf.append(part("ebuf1", o_l, XR, NKEYS))
        sxb = [part("sx0", o_l + 1024, XR, NKEYS)]
        best = part("best", o_l + 2048, 2 * FH, TOPK)
        pairs = part("pairs", o_l + 2112, FH, TOPK * TOPK)
        top = part("top", o_l + 2368, 2, FH, TOPK)
        zexp = part("zexp", o_l + 2432, FH, TOPK)
        zinv = part("zinv", o_l + 2464, FH)
        negm = part("negm", o_l + 2468, 2, FH)
        rsum = part("rsum", o_l + 2476, 2)
        smax = part("smax", o_l + 2488, 8)
        rec = part("rec", o_l + 2496, HEADS)
        vare = part("vare", o_l + 2512, 4)
        gtmp = part("gtmp", o_l, B, D)
        x1T = part("x1T", o_a, KC, W)
        qT = part("qT", o_a + 1024, KC, W)
        prob = part("prob", o_a + 2048, 2, FLAT)
        pT = part("pT", o_a + 4512, PCH, P)
        ob = part("ob", o_a + 5792, 2, D)
        oT = part("oT", o_a + 6304, 2, KC, P)
        sxb.append(part("sx1", o_a + 6816, XR, NKEYS))
        rw = part("rw", o_b, SUPER, NEXP)
        aT = part("aT", o_b + 4096, EC, P)
        gate = part("gate", o_b + 5120, 2, W)
        thb = part("thb", o_b + 6144, 2, W)
        upb = part("upb", o_b + 7168, 2, W)

        s_ssm, s_cst, s_ctx, s_wsim_in, s_ffn_in = (sem(n) for n in (
            "ssm_loaded", "const_loaded", "ctx_loaded", "simw_loaded", "ffn_loaded"))
        s_x = [sem(f"x{q}_loaded") for q in range(NQ)]
        s_mat = sem("mat_loaded")
        s_dve, s_pool, s_actc = sem("dve_steps"), sem("pool_steps"), sem("act_steps")
        s_small_ready = sem("small_ready")
        s_small_act = sem("small_act")
        s_base = sem("table_base_ready")
        s_outer = sem("decay_outer_ready")
        s_phase = sem("table_phase_ready")
        s_sin = sem("table_sines_ready")
        s_dec = sem("table_decays_ready")
        s_wtd = sem("table_sines_weighted")
        s_tab = sem("table_ready")
        s_ktm = sem("ktime_mm")
        s_kev = sem("ktime_evac")
        s_kdone = sem("ktime_done")
        s_kw, s_kq, s_kaw, s_kb, s_zr = ([sem(f"{n}{h}") for h in range(2)] for n in (
            "taps_written", "taps_moved", "ka_written", "kb_loaded", "z_loaded"))
        s_xa, s_xae, s_xaw, s_xb = sem("xa_mm"), sem("xa_evac"), sem("xa_written"), sem("xb_loaded")
        s_imat = sem("imat_loaded")
        s_ka, s_kae = sem("ka_mm"), sem("ka_evac")
        s_kfm, s_kfe = sem("kf_mm"), sem("kf_evac")
        s_xf, s_xfe, s_yf = sem("xf_mm"), sem("xf_evac"), sem("y_ready")
        s_z, s_ze = sem("z_mm"), sem("z_evac")
        s_zw = [sem(f"z_written{d}") for d in range(ZRING)]
        s_r = sem("conv_mm")
        s_rfree = sem("conv_read")
        s_cm, s_kt, s_ce = sem("ctx_mm"), sem("ctx_keys"), sem("ctx_evac")
        s_kbd = sem("kbd_ready")
        s_kbz = sem("vaug_ready")

        s_xbr = sem("x_plus_bias")
        s_x1, s_x2, s_out = sem("x1_ready"), sem("x2_ready"), sem("out_ready")
        s_outw = sem("out_written")
        s_stat = [sem(f"norm{n}_stats") for n in range(4)]
        s_rstd = [sem(f"norm{n}_rstd") for n in range(4)]
        s_u = [sem("attn_residual")]
        s_bo, s_bd = sem("bo_added"), sem("bd_added")
        s_tmm, s_tev = sem("turned_mm"), sem("turned_evac")
        s_wmm, s_wact, s_wdve = sem("wide_mm"), sem("wide_read_act"), sem("wide_read_dve")
        s_smm, s_ssub, s_exp = sem("score_mm"), sem("score_shifted"), sem("score_exp")
        s_pv, s_on, s_wo = sem("pv_mm"), sem("attn_normed"), sem("wo_mm")
        s_best, s_zarg, s_zexp = sem("pair_top"), sem("pair_args"), sem("pair_exp")
        s_sx, s_e, s_rfr, s_rr = sem("pair_sums"), sem("pair_exps"), sem("pair_used"), sem("weights_ready")
        s_7mm, s_7f = sem("outer_mm"), sem("outer_read")
        s_half = sem("gate_bias_halved")
        s_hid = sem("hidden_ready")
        s_silu = sem("silu_ready")

        HEAD = head()
        SCHEDULE = plan()
        PLAN = order(SCHEDULE, "pe")
        T_AT, W_AT, W_FREE, na, nd = {}, {}, [], 0, 0
        SILU_AT = {step: u for u, step in enumerate(y for y in PLAN if y[0] in ("expert", "inner"))}
        for step in PLAN:
            if step[0] in ("turn1", "turn2", "probs", "turno"):
                T_AT[step] = len(T_AT)
            for part_ in {"query": "a", "sim": "a", "expert": "a", "inner": "aA", "spread": "d"}.get(step[0], ""):
                W_AT[step + (part_,)] = len(W_FREE)
                if part_ == "d":
                    nd += 1
                    W_FREE.append((s_wdve, nd))
                else:
                    na += 1
                    W_FREE.append((s_wact, na))

        scr_x = t["scr_x"]
        scr_k = t["scr_k"]
        scr_t = t["scr_t"]
        scr_z = t["scr_z"]

        def z_writes(upto, d):
            return len(range(d, upto, ZRING))

        class Steps:

            def __init__(self, eng, s):
                self.eng, self.s, self.n = eng, s, 0
                self.counts = {}

            def mark(self, ins):
                self.n += 1
                ins.then_inc(self.s, 1)
                return self.n

            def need(self, k):
                self.eng.wait_ge(self.s, k)

            def link(self, ins):
                self.need(self.mark(ins))

            def done(self, s):
                self.counts[id(s)] = self.counts.get(id(s), 0) + 1
                self.eng.wait_ge(s, self.counts[id(s)])

        block = ctx.enter_context(nc.Block())

        @block.sync
        def _(sp):
            sp.dma_start(ssm, t["ssm"]).then_inc(s_ssm, 16)
            sp.dma_start(cols[:, :], t["cols"]).then_inc(s_ssm, 16)
            sp.dma_start(steps[:, :], t["steps"]).then_inc(s_ssm, 16)
            sp.dma_start(skip[:, :], t["skip"]).then_inc(s_ssm, 16)
            sp.dma_start(fa, t["fa"]).then_inc(s_cst, 16)
            for q in range(NQ):
                sp.dma_start(tok[:, 2 * q:2 * q + 2, :], t["x"][:, 2 * q:2 * q + 2, :]).then_inc(s_x[q], 16)
            for dst, n in ((ctxT, "ctxT"), (wk, "wk"), (wv, "wv"), (pcol[:, :], "pcol"), (shift, "shift"),
                           (head_mask[:, :], "head_mask"), (rows[:, :, :], "rows")):
                sp.dma_start(dst, t[n]).then_inc(s_ctx, 16)
            sp.dma_start(wqf, t["wqf"]).then_inc(s_wsim_in, 16)
            sp.dma_start(keysT, t["keysT"]).then_inc(s_wsim_in, 16)
            for dst, n in ((fmat, "fmat"), (fai, "fai"), (wq[:, :, :], "wq"), (wo[:, :, :], "wo"),
                           (ident[:, :], "ident")):
                sp.dma_start(dst, t[n]).then_inc(s_mat, 16)
            for q in range(NQ):
                sp.wait_ge(s_xae, 2 * (q + 1))
                for h in range(2):
                    sp.dma_start(scr_x[q, 8 * h:8 * h + 8].rearrange("r s n -> (r s) n"),
                                 cA[:, h, q, :]).then_inc(s_xaw, 16)
            sp.wait_ge(s_base, 2)
            sp.dma_start(imat, t["imat"]).then_inc(s_imat, 16)
            sp.wait_ge(s_xaw, 16 * 2 * NQ)
            sp.wait_ge(s_cm, 4)
            for q in range(NQ):
                sp.dma_start(xS[16 * q:16 * q + 16, 0:NSLOT, :],
                             scr_x[q].rearrange("r s n -> s r n")).then_inc(s_xb, 16)
            for hf in range(2):
                sp.wait_ge(s_kdone, hf + 1)
                for g in range(4):
                    sp.dma_start(scr_t[hf, :, 8 * g:8 * g + 8, :], ktime[:, 8 * g:8 * g + 8, :]).then_inc(s_kw[hf], 16)
                sp.wait_ge(s_kw[hf], 64)
                taps = scr_t[hf].rearrange("i j n -> (i j) n").rearrange("(c q s) n -> c s q n", c=NC, q=NQ)
                if hf:
                    sp.wait_ge(s_ka, 4)
                for c in range(NC):
                    sp.dma_start(kQ[16 * c:16 * c + 16, :, :], taps[c]).then_inc(s_kq[hf], 16)
                for h in range(2):
                    sp.wait_ge(s_kae, 4 * hf + 2 * h + 2)
                    for q in range(NQ):
                        sp.dma_start(scr_k[hf, q, 8 * h:8 * h + 8].rearrange("r s n -> (r s) n"),
                                     kA[hf][:, h, q, :]).then_inc(s_kaw[hf], 16)
                sp.wait_ge(s_kaw[hf], 16 * 2 * NQ)
                for q in range(NQ):
                    sp.dma_start(kS[hf][16 * q:16 * q + 16, 0:NSLOT, :],
                                 scr_k[hf, q].rearrange("r s n -> s r n")).then_inc(s_kb[hf], 16)
            for hf in range(2):
                sp.wait_ge(s_ktm, 2 * NGRP)
                for d in range(ZRING):
                    sp.wait_ge(s_zw[d], 16 * z_writes(FREQ * (hf + 1), d))
                for r in range(NSLOT):
                    h, rr = divmod(r, 8)
                    sp.dma_start(zB[16 * rr:16 * rr + 16, hf, h, :, :],
                                 scr_z[hf, r].rearrange("(q s) n -> s q n", s=NS)).then_inc(s_zr[hf], 16)
            sp.wait_ge(s_r, NQ)
            for dst, n in ((dn, "dn"), (wg, "wg"), (wu, "wu"), (wd, "wd"), (up, "up")):
                sp.dma_start(dst, t[n]).then_inc(s_ffn_in, 16)
            for tl in range(TILES):
                sp.wait_ge(s_out, tl + 1)
                sp.dma_start(t["out"][:, tl, :], tok[:, tl, :]).then_inc(s_outw, 16)
            sp.wait_ge(s_outw, 16 * TILES)

        @block.tensor
        def _(pe):
            mm = nc.tensor.matmul
            pe.wait_ge(s_cst, 16)
            for q in range(NQ):
                pe.wait_ge(s_x[q], 16)
                for h in range(2):
                    i = 2 * q + h
                    if i >= 4:
                        pe.wait_ge(s_xae, i - 3)
                    mm(bank[i % 4][:, :], fa[:, h, :],
                       tok[:, 2 * q:2 * q + 2, :].rearrange("p a b -> p (a b)"),
                       start=True, stop=True).then_inc(s_xa, 1)
            pe.wait_ge(s_ctx, 16 * 7)
            for oc in range(KC):
                for ic in range(KC):
                    ins = mm(bank[4 + oc][:, 0:B * NKV], wk[:, ic, P * oc:P * oc + P], ctxT[:, ic, :],
                             start=(ic == 0), stop=(ic == KC - 1))
                ins.then_inc(s_cm, 1)
            for b in range(B):
                for ic in range(KC):
                    ins = mm(bank[6 + b][0:NKV, 0:D], ctxT[:, ic, NKV * b:NKV * b + NKV], wv[:, ic, :],
                             start=(ic == 0), stop=(ic == KC - 1))
                ins.then_inc(s_cm, 1)
            pe.wait_ge(s_wsim_in, 32)
            pe.wait_ge(s_kt, 2)
            for oc in range(KC):
                for m in range(2 * FH):
                    ins = mm(bank[4 + oc][:, NKEYS * m:NKEYS * m + NKEYS], wqf[:, m, P * oc:P * oc + P],
                             keysT[:, m, :], start=True, stop=True, skip_group_check=True)
                ins.then_inc(s_cm, 1)
            def spread_values():
                pe.wait_ge(s_kbz, 1)
                for b in range(B):
                    for ch in range(PCH):
                        h0, h1 = heads_of(ch)
                        for h in range(h0, h1 + 1):
                            at = P + P * ch - NKV * h
                            ins = mm(bank[6 + b][:, 51 * ch + 17 * (h - h0):51 * ch + 17 * (h - h0) + 17],
                                     shift[:, at:at + P], vaug[:, b, h, :], start=True, stop=True,
                                     skip_group_check=True)
                    ins.then_inc(s_cm, 1)

            def taps(g):
                pe.wait_ge(s_tab, g + 1)
                for m in range(2):
                    i = 2 * g + m
                    if i >= 2:
                        pe.wait_ge(s_kev, i - 1)
                    for hh in range(16):
                        ch = 16 * m + hh
                        ins = mm(bank[4 + i % 2][0:HALF, HALF * hh:HALF * hh + HALF], tpm[g % 2][:, ch, :],
                                 tqm[g % 2][:, ch, :], start=True, stop=True, skip_group_check=True)
                    ins.then_inc(s_ktm, 1)

            def second_stage(k1, re, im, src):
                r, i = slot_of(k1, 0), slot_of(k1, 1)
                two = k1 not in (0, 8)
                mm(re, fmat[:, mat_of(k1, 0), :], src(r), start=True, stop=not two, skip_group_check=True)
                if two:
                    mm(re, fmat[:, mat_of(k1, 1), :], src(i), start=False, stop=True, skip_group_check=True)
                ins = mm(im, fmat[:, mat_of(k1, 2), :], src(r), start=True, stop=not two, skip_group_check=True)
                if two:
                    ins = mm(im, fmat[:, mat_of(k1, 0), :], src(i), start=False, stop=True, skip_group_check=True)
                return ins

            def x_second(k1):
                pe.wait_ge(s_mat, 16 * 5)
                pe.wait_ge(s_xb, 16 * NQ)
                if k1 >= 2:
                    pe.wait_ge(s_xfe, k1 - 1)
                bb = 2 * (k1 % 2)
                second_stage(k1, bank[bb][:, :], bank[bb + 1][:, :], lambda r: xS[:, r, :]).then_inc(s_xf, 1)

            def k_first(hf):
                pe.wait_ge(s_kq[hf], 16 * NC)
                if hf:
                    pe.wait_ge(s_kfe, FREQ)
                else:
                    pe.wait_ge(s_ce, 4)
                for i in range(4):
                    h, qh = divmod(i, 2)
                    if i >= 2 or hf:
                        pe.wait_ge(s_kae, 4 * hf + max(i - 1, 0))
                    mm(bank[6 + i % 2][:, :], fa[:, h, :], kQ[:, 4 * qh:4 * qh + 4, :].rearrange("p a b -> p (a b)"),
                       start=True, stop=True).then_inc(s_ka, 1)

            def k_second(hf, k1):
                pe.wait_ge(s_kb[hf], 16 * NQ)
                if k1 >= 2:
                    pe.wait_ge(s_kfe, FREQ * hf + k1 - 1)
                else:
                    pe.wait_ge(s_kae, 4 * hf + 4)
                bk = bank[6 + k1 % 2]
                second_stage(k1, bk[:, 0:HC], bk[:, HC:2 * HC], lambda r: kS[hf][:, r, :]).then_inc(s_kfm, 1)

            def inverse(hf, k):
                m = FREQ * hf + k
                pe.wait_ge(s_imat, 16)
                pe.wait_ge(s_xfe, FREQ)
                pe.wait_ge(s_yf, m + 1)
                if m >= 4:
                    pe.wait_ge(s_ze, m - 3)
                bk, y = bank[m % 4], yf[:, m % 2]
                mm(bk[:, 0:2 * HC], imat[:, mat_of(k, 0), :], y[:, 0, :], start=True, stop=False, skip_group_check=True)
                ins = mm(bk[:, 0:2 * HC], imat[:, mat_of(k, 2), :], y[:, 1, :], start=False, stop=True,
                         skip_group_check=True)
                if k not in (0, 8):
                    mm(bk[:, 2 * HC:4 * HC], imat[:, mat_of(k, 1), :], y[:, 0, :], start=True, stop=False,
                       skip_group_check=True)
                    ins = mm(bk[:, 2 * HC:4 * HC], imat[:, mat_of(k, 0), :], y[:, 1, :], start=False, stop=True,
                             skip_group_check=True)
                ins.then_inc(s_z, 1)

            for kind, n in order(HEAD, "pe"):
                if kind == "taps":
                    if n == 0:
                        pe.wait_ge(s_ce, 2)
                    taps(n)
                elif kind == "values":
                    spread_values()
                elif kind == "x_second":
                    x_second(n)
                elif kind == "k_first":
                    k_first(n)
                elif kind == "k_second":
                    k_second(*divmod(n, FREQ))
                elif kind == "inverse":
                    inverse(*divmod(n, FREQ))

            def conv(q):
                for hf in range(2):
                    pe.wait_ge(s_zr[hf], 16 * NSLOT)
                pe.wait_ge(s_kev, 2 * NGRP)
                pe.wait_ge(s_kfe, 2 * FREQ)
                if q >= 2:
                    pe.wait_ge(s_rfree, q - 1 if q < 4 else q)
                bk = bank[conv_bank(q)][:, :].rearrange("p (b f n) -> p f b n", b=B, f=2)
                for hf in range(2):
                    for h in range(2):
                        ins = mm(bk[:, hf], fai[:, h, :], zB[:, hf, h, q, :].rearrange("p (b n) -> p b n", b=B),
                                 start=(h == 0), stop=(h == 1), skip_group_check=True)
                ins.then_inc(s_r, 1)

            def t_unit(key):
                u = T_AT[key]
                if u >= 2:
                    pe.wait_ge(s_tev, u - 1)
                return bank[2 + u % 2]

            def w_unit(key):
                u = W_AT[key]
                if u >= 2:
                    pe.wait_ge(*W_FREE[u - 2])
                return bank[5 + u % 2]

            def turn_tokens(key, s, j):
                bk = t_unit(key)
                for i in range(2):
                    for k in range(KC):
                        ins = nc.tensor.transpose(bk[:, P * (2 * i + k):P * (2 * i + k) + P],
                                                  tok[:, SUPER * s + 2 * j + i, P * k:P * k + P], ident[:, :])
                ins.then_inc(s_tmm, 1)

            def wide(key, w, m, src):
                bk = w_unit(key)
                for k in range(KC):
                    ins = mm(bk[:, :], w[:, k, P * m:P * m + P], src[:, k, :], start=(k == 0), stop=(k == KC - 1))
                ins.then_inc(s_wmm, 1)

            for step in order(SCHEDULE, "pe"):
                kind, n = step[0], step[1]
                if kind == "conv":
                    conv(n)
                elif kind == "turn1":
                    pe.wait_ge(s_x1, 2 * n + step[2] + 1)
                    turn_tokens(step, n, step[2])
                elif kind == "query":
                    pe.wait_ge(s_tev, T_AT[("turn1", n, 1)] + 1)
                    wide(step + ("a",), wq, step[2], x1T)
                elif kind == "score":
                    hh, i, b = step[2], n % SUPER, n % B
                    pe.wait_ge(s_wact, W_FREE[W_AT[("query", n // SUPER, hh, "a")]][1])
                    if n == 0:
                        pe.wait_ge(s_kbd, 1)
                    if n or hh:
                        pe.wait_ge(s_ssub, 2 * n + hh)
                    for g in range(2):
                        ins = mm(bank[g][:, 0:GH * NKV], qT[:, hh, P * i:P * i + P],
                                 kbd[:, b, hh, GH * NKV * g:GH * NKV * (g + 1)], start=True, stop=True)
                    ins.then_inc(s_smm, 1)
                elif kind == "probs":
                    j = step[2]
                    pe.wait_ge(s_exp, 2 * n + 2)
                    bk = t_unit(step)
                    for c in range(4 * j, min(4 * j + 4, PCH)):
                        m = min(P, FLAT - P * c)
                        ins = nc.tensor.transpose(bk[0:m, P * (c % 4):P * (c % 4) + P],
                                                  prob[:, n % 2, P * c:P * c + m], ident[:, :])
                    ins.then_inc(s_tmm, 1)
                elif kind == "attend":
                    if n:
                        pe.wait_ge(s_u[0], n)
                    else:
                        pe.wait_ge(s_rfree, 3)
                    for c in range(PCH):
                        if c % 4 == 0:
                            pe.wait_ge(s_tev, T_AT[("probs", n, c // 4)] + 1)
                        h0, h1 = heads_of(c)
                        m = min(P, FLAT - P * c)
                        k = (HD + 1) * (h1 - h0 + 1)
                        ins = mm(bank[4][:, (HD + 1) * h0:(HD + 1) * h0 + k], pT[0:m, c, :], vbd[0:m, n % B, c, 0:k],
                                 start=(c == 0), stop=(c == PCH - 1), skip_group_check=True)
                    ins.then_inc(s_pv, 1)
                elif kind == "turno":
                    pe.wait_ge(s_on, n + 1)
                    bk = t_unit(step)
                    for k in range(KC):
                        ins = nc.tensor.transpose(bk[:, P * k:P * k + P], ob[:, n % 2, P * k:P * k + P], ident[:, :])
                    ins.then_inc(s_tmm, 1)
                elif kind == "project":
                    pe.wait_ge(s_tev, T_AT[("turno", n)] + 1)
                    for k in range(KC):
                        ins = mm(bank[4][:, 0:D], oT[:, n % 2, k, :], wo[:, k, :], start=(k == 0), stop=(k == KC - 1))
                    ins.then_inc(s_wo, 1)
                elif kind == "turn2":
                    pe.wait_ge(s_x2, SUPER * n + 2 * step[2] + 2)
                    turn_tokens(step, n, step[2])
                elif kind == "sim":
                    f, i = divmod(n, SUPER)
                    pe.wait_ge(s_tev, T_AT[("turn2", f, i // 2)] + 1)
                    bk = w_unit(step + ("a",))
                    for k in range(KC):
                        ins = mm(bk[:, :], x2T[:, k, P * i:P * i + P], wsim[:, k, :], start=(k == 0), stop=(k == KC - 1))
                    ins.then_inc(s_wmm, 1)
                elif kind == "expert":
                    if step[2] == 0:
                        pe.wait_ge(s_ffn_in, 16 * 5)
                        pe.wait_ge(s_tev, T_AT[("turn2", n, 1)] + 1)
                    wide(step + ("a",), dn, step[2], x2T)
                elif kind == "inner":
                    wide(step + ("a",), wg, step[2], x2T)
                    wide(step + ("A",), wu, step[2], x2T)
                elif kind == "spread":
                    j = step[2]
                    pe.wait_ge(s_rr, n + 1)
                    bk = w_unit(step + ("d",))
                    for c in range(4):
                        ins = nc.tensor.transpose(bk[:, P * c:P * c + P],
                                                  rw[:, n % SUPER, P * (4 * j + c):P * (4 * j + c) + P], ident[:, :])
                    ins.then_inc(s_wmm, 1)
                elif kind == "outer":
                    i = n % SUPER
                    pe.wait_ge(s_hid, FC * (n // SUPER + 1))
                    if n:
                        pe.wait_ge(s_7f, n)
                    for c in range(FC):
                        mm(bank[7][:, 0:D], hid[:, c, P * i:P * i + P], wd[:, c, :], start=(c == 0), stop=False)
                    pe.wait_ge(s_wdve, W_FREE[W_AT[("spread", n, 1, "d")]][1])
                    for c in range(EC):
                        ins = mm(bank[7][:, 0:D], aT[:, c, :], up[:, c, :], start=False, stop=(c == EC - 1))
                    ins.then_inc(s_7mm, 1)

        def evac_taps(act, own, i):
            if i == 0:
                act.wait_ge(s_xaw, 16 * 2 * NQ)
            act.wait_ge(s_ktm, i + 1)
            if i == NGRP:
                act.wait_ge(s_kw[0], 64)
            src = bank[4 + i % 2][0:HALF, :].rearrange("p (h j) -> p j h", j=HALF)
            i = i % NGRP
            nc.scalar.copy(ktime[:, :, 16 * i:16 * i + 16], src).then_inc(s_kev, 1)
            own.done(s_kev)

        @block.scalar
        def _(act):
            fn = nc.scalar.activation
            own = Steps(act, s_actc)
            for i in range(2 * NQ):
                act.wait_ge(s_xa, i + 1)
                nc.scalar.copy(cA[:, i % 2, i // 2, :], bank[i % 4][:, :]).then_inc(s_xae, 1)
                own.done(s_xae)
                if i == 3:
                    act.wait_ge(s_small_ready, 1)
                    fn(wk_[3], wk_[2], ACT.Sin, scale=-TWO_PI).then_inc(s_small_act, 1)
                    own.done(s_small_act)
                    fn(wk_[4], wk_[2], ACT.Sin, scale=-TWO_PI / 2).then_inc(s_small_act, 1)
                    own.done(s_small_act)
                    act.wait_ge(s_small_ready, 2)
                    fn(wk_[5], wk_[1], ACT.Tanh, scale=0.5).then_inc(s_small_act, 1)
                    own.done(s_small_act)
                    fn(wk_[6], wk_[1], ACT.Exp).then_inc(s_small_act, 1)
                    own.done(s_small_act)
            def sines(g):
                d = g % 2
                act.wait_ge(s_phase, 2 * g + 1)
                own.link(fn(tq[d], tq[d], ACT.Sin, scale=TWO_PI, bias=cols[:, 1:2]))
                act.wait_ge(s_phase, 2 * g + 2)
                own.link(fn(tpc[d], tp[d], ACT.Abs))
                own.link(fn(tpc[d], tpc[d], ACT.Sin, scale=-TWO_PI, bias=cols[:, 4:5]))
                fn(tp[d], tp[d], ACT.Sin, scale=-TWO_PI).then_inc(s_sin, 1)
                own.done(s_sin)

            def decays(g):
                d = g % 2
                act.wait_ge(s_outer, 2 * g + 2)
                own.link(fn(tqm[d], tqm[d], ACT.Exp))
                fn(tpm[d], tpm[d], ACT.Exp).then_inc(s_dec, 1)
                own.done(s_dec)

            for kind, n in order(HEAD, "act"):
                if kind == "simw":
                    for k in range(KC):
                        act.wait_ge(s_cm, 5 + k)
                        nc.scalar.copy(wsim[:, k, :], bank[4 + k][:, :]).then_inc(s_ce, 1)
                        own.done(s_ce)
                elif kind == "values":
                    for b in range(B):
                        act.wait_ge(s_cm, 7 + b)
                        for ch in range(PCH):
                            h0, h1 = heads_of(ch)
                            k = 17 * (h1 - h0 + 1)
                            ins = nc.scalar.copy(vbd[:, b, ch, 0:k], bank[6 + b][:, 51 * ch:51 * ch + k])
                        ins.then_inc(s_ce, 1)
                        own.done(s_ce)
                elif kind == "sines":
                    sines(n)
                elif kind == "decays":
                    decays(n)
                elif kind == "taps":
                    for i in (2 * n, 2 * n + 1):
                        evac_taps(act, own, i)
                elif kind == "x_second":
                    act.wait_ge(s_xf, n + 1)
                    r = slot_of(n, 0)
                    own.link(nc.scalar.copy(xS[:, r, :], bank[2 * (n % 2)][:, :]))
                    nc.scalar.copy(xS[:, image_of(n), :], bank[2 * (n % 2) + 1][:, :]).then_inc(s_xfe, 1)
                    own.done(s_xfe)
                elif kind == "k_first":
                    for i in range(4):
                        h, qh = divmod(i, 2)
                        act.wait_ge(s_ka, 4 * n + i + 1)
                        nc.scalar.copy(kA[n][:, h, 4 * qh:4 * qh + 4, :].rearrange("p a b -> p (a b)"),
                                       bank[6 + i % 2][:, :]).then_inc(s_kae, 1)
                        own.done(s_kae)
                elif kind == "k_second":
                    hf, k1 = divmod(n, FREQ)
                    act.wait_ge(s_kfm, n + 1)
                    r, m = slot_of(k1, 0), image_of(k1)
                    nc.scalar.copy(kS[hf][:, r:m + 1:m - r, :],
                                   bank[6 + k1 % 2][:, 0:2 * HC].rearrange("p (a b) -> p a b", a=2)).then_inc(s_kfe, 1)
                    own.done(s_kfe)
                elif kind == "inverse":
                    hf, k = divmod(n, FREQ)
                    d, planes = n % ZRING, 1 if k in (0, 8) else 2
                    act.wait_ge(s_z, n + 1)
                    if n >= ZRING:
                        act.wait_ge(s_zw[d], 16 * z_writes(n, d))
                    nc.scalar.copy(zring[:, d, 0:planes].rearrange("p a b -> p (a b)"),
                                   bank[n % 4][:, 0:2 * HC * planes]).then_inc(s_ze, 1)
                    own.done(s_ze)
                    r = slot_of(k, 0)
                    act.dma_start(scr_z[hf, r:r + planes].rearrange("r p n -> p r n"),
                                  zring[:, d, 0:planes]).then_inc(s_zw[d], 16)

            def turned(key, out, view):
                u = T_AT[key]
                act.wait_ge(s_tmm, u + 1)
                nc.scalar.copy(out, view(bank[2 + u % 2])).then_inc(s_tev, 1)
                own.done(s_tev)

            def turned_tokens(key, j, dst):
                turned(key, dst[:, :, 2 * P * j:2 * P * j + 2 * P].rearrange("p k (i n) -> p k i n", n=P),
                       lambda bk: bk[:, :].rearrange("p (i k n) -> p k i n", i=2, k=KC))

            def wide_ready(key):
                u = W_AT[key]
                act.wait_ge(s_wmm, u + 1)
                return bank[5 + u % 2][:, :]

            def silu(key, half, src, **bias):
                u = SILU_AT[key]
                if u == 0:
                    act.wait_ge(s_half, 1)
                if u >= 2:
                    act.wait_ge(s_silu, u - 1)
                fn(half, src, ACT.Identity, scale=0.5, **bias)
                fn(thb[:, u % 2, :], src, ACT.Tanh, scale=0.5, **bias).then_inc(s_wact, 1)
                own.done(s_wact)

            for step in order(SCHEDULE, "act"):
                kind, n = step[0], step[1]
                if kind == "turn1":
                    if n:
                        act.wait_ge(s_wmm, W_AT[("query", n - 1, KC - 1, "a")] + 1)
                    turned_tokens(step, step[2], x1T)
                elif kind == "query":
                    j = step[2]
                    src = wide_ready(step + ("a",))
                    if n:
                        act.wait_ge(s_smm, 2 * SUPER * n)
                    fn(qT[:, j, :], src, ACT.Identity, bias=pcol[:, j:j + 1]).then_inc(s_wact, 1)
                    own.done(s_wact)
                elif kind == "score":
                    act.wait_ge(s_ssub, 2 * n + step[2] + 1)
                    half = prob[:, n % 2, 8 * NKV * step[2]:8 * NKV * (step[2] + 1)]
                    fn(half, half, ACT.Exp).then_inc(s_exp, 1)
                    own.done(s_exp)
                elif kind == "probs":
                    j, u = step[2], T_AT[step]
                    if n:
                        act.wait_ge(s_pv, n)
                    if j < 2:
                        turned(step, pT[:, 4 * j:4 * j + 4, :], lambda bk: bk[:, :].rearrange("p (c n) -> p c n", n=P))
                    else:
                        act.wait_ge(s_tmm, u + 1)
                        own.link(nc.scalar.copy(pT[:, 8, :], bank[2 + u % 2][:, 0:P]))
                        m = FLAT - 9 * P
                        nc.scalar.copy(pT[0:m, 9, :], bank[2 + u % 2][0:m, P:2 * P]).then_inc(s_tev, 1)
                        own.done(s_tev)
                elif kind == "turno":
                    if n >= 2:
                        act.wait_ge(s_wo, n - 1)
                    turned(step, oT[:, n % 2], lambda bk: bk[:, 0:D].rearrange("p (k n) -> p k n", n=P))
                elif kind == "turn2":
                    if n:
                        act.wait_ge(s_wmm, max(W_AT[("inner", n - 1, FC - 1, "A")], W_AT[("sim", SUPER * n - 1, "a")]) + 1)
                    turned_tokens(step, step[2], x2T)
                elif kind == "sim":
                    src = wide_ready(step + ("a",))
                    if n >= 2:
                        act.wait_ge(s_sx, FH * (n - 1))
                        act.wait_ge(s_best, n - 1)
                    nc.scalar.copy(sim[:, n % 2].rearrange("p a b -> p (a b)"), src).then_inc(s_wact, 1)
                    own.done(s_wact)
                elif kind == "expert":
                    c = step[2]
                    src = wide_ready(step + ("a",))
                    if n:
                        act.wait_ge(s_wdve, W_FREE[W_AT[("spread", SUPER * n - 1, 1, "d")]][1])
                    silu(step, silg[:, c, :], src)
                elif kind == "inner":
                    c, m = step[2], FC * n + step[2]
                    src = wide_ready(step + ("a",))
                    if m >= 2:
                        act.wait_ge(s_hid, m - 1)
                    silu(step, gate[:, m % 2, :], src, bias=pcol[:, 4 + c:5 + c])
                    src = wide_ready(step + ("A",))
                    fn(upb[:, m % 2, :], src, ACT.Identity, bias=pcol[:, 4 + FC + c:5 + FC + c]).then_inc(s_wact, 1)
                    own.done(s_wact)
                elif kind == "best":
                    act.wait_ge(s_zarg, n + 1)
                    fn(zexp, zexp, ACT.Exp).then_inc(s_zexp, 1)
                    own.done(s_zexp)
                elif kind == "exps":
                    m = FH * n + step[2]
                    act.wait_ge(s_best, n + 1)
                    act.wait_ge(s_sx, m + 1)
                    if m >= 2:
                        act.wait_ge(s_rfr, m - 1)
                    fn(ebuf[m % 2], sxb[m % 2], ACT.Exp, bias=negm[:, n % 2, step[2]:step[2] + 1]).then_inc(s_e, 1)
                    own.done(s_e)

        @block.gpsimd
        def _(pool):
            own = Steps(pool, s_pool)
            tt = nc.gpsimd.tensor_tensor
            pool.wait_ge(s_base, 1)

            def exponents(g):
                d, ch = g % 2, slice(GRP * g, GRP * g + GRP)
                if g >= 2:
                    pool.wait_ge(s_ktm, 2 * (g - 1))
                for dst, a in ((tqm[d], wk_[1]), (tpm[d], wk_[7])):
                    tt(dst, a[:, ch].unsqueeze(2).broadcast_to((P, GRP, HALF)),
                       steps[:, :].unsqueeze(1).broadcast_to((P, GRP, HALF)), ALU.mult).then_inc(s_outer, 1)
                    own.done(s_outer)

            def weigh(g):
                d, ch = g % 2, slice(GRP * g, GRP * g + GRP)
                pool.wait_ge(s_sin, g + 1)
                pool.wait_ge(s_base, 2)
                for dst, a in ((tpc[d], wk_[14]), (tp[d], wk_[9])):
                    tt(dst, dst, a[:, ch].unsqueeze(2).broadcast_to((P, GRP, HALF)), ALU.mult).then_inc(s_wtd, 1)
                    own.done(s_wtd)

            def skip_terms(hf):
                pool.wait_ge(s_kev, NGRP * (hf + 1))
                tt(ktime[0:1, 0, :], skip[0:1, HC * hf:HC * hf + HC], ktime[0:1, 0, :], ALU.add).then_inc(s_kdone, 1)
                own.done(s_kdone)

            def keys_diagonal():
                pool.wait_ge(s_kt, 2)
                for b in range(B):
                    for oc in range(KC):
                        ins = tt(kbd[:, b, oc, :].rearrange("p (h k) -> p h k", k=NKV),
                                 kT[:, oc, NKV * b:NKV * b + NKV].unsqueeze(1).broadcast_to((P, 8, NKV)),
                                 head_mask[:, :].unsqueeze(2).broadcast_to((P, 8, NKV)), ALU.mult)
                        if (b, oc) == (B - 1, KC - 1):
                            ins.then_inc(s_kbd, 1)
                            own.done(s_kbd)
                        else:
                            own.link(ins)

            for k, (kind, n) in enumerate(order(HEAD, "pool")):
                if kind == "exponents":
                    exponents(n)
                elif kind == "weigh":
                    weigh(n)
                elif kind == "diagonal":
                    own.link(nc.gpsimd.tensor_scalar(skip[:, :], skip[:, :], 1.0, None, ALU.add))
                    keys_diagonal()
                elif kind == "skip":
                    skip_terms(n)
            pool.wait_ge(s_xa, 2 * NQ)
            pool.wait_ge(s_ctx, 16 * 7)
            nc.gpsimd.tensor_scalar(pcol[:, 4:4 + FC], pcol[:, 4:4 + FC], 0.5, None, ALU.mult).then_inc(s_half, 1)
            for tl in range(TILES):
                tt(tok[:, tl, :], tok[:, tl, :], lnb, ALU.add).then_inc(s_xbr, 1)
                own.done(s_xbr)

            def deviation(k, tl, n):
                own.link(nc.gpsimd.tensor_scalar(vare[:, 0:n], mv[:, k, tl:tl + n, 1], EPS, None, ALU.add))
                tt(rstd[:, k, tl:tl + n], vare[:, 0:n], cols[:, 5:6].broadcast_to((P, n)), ALU.pow).then_inc(s_rstd[k], 1)
                own.done(s_rstd[k])

            for step in order(SCHEDULE, "pool"):
                kind, n = step[0], step[1]
                if kind in ("turn1", "turn2"):
                    pool.wait_ge(s_tmm, T_AT[step] + 1)
                    bias, s_added = (bo, s_bo) if kind == "turn1" else (bd, s_bd)
                    for i in range(2):
                        tl = SUPER * n + 2 * step[2] + i
                        tt(tok[:, tl, :], tok[:, tl, :], bias, ALU.add).then_inc(s_added, 1)
                        own.done(s_added)
                elif kind == "sums":
                    h, m = step[2], FH * n + step[2]
                    pool.wait_ge(s_wact, W_FREE[W_AT[("sim", n, "a")]][1])
                    if m >= 2:
                        pool.wait_ge(s_rfr, m - 1)
                    tt(sxb[m % 2], sim[:, n % 2, h, 0:XR].unsqueeze(2).broadcast_to((P, XR, NKEYS)),
                       sim[:, n % 2, FH + h, :].unsqueeze(1).broadcast_to((P, XR, NKEYS)), ALU.add).then_inc(s_sx, 1)
                    own.done(s_sx)
                elif kind in ("dev0", "dev1"):
                    k = int(kind[-1])
                    pool.wait_ge(s_stat[k], n + 1)
                    deviation(k, 2 * n, 2)
                elif kind in ("dev2", "dev3"):
                    k = int(kind[-1])
                    pool.wait_ge(s_stat[k], n + 1)
                    deviation(k, n, 1)

        @block.vector
        def _(dve):
            own = Steps(dve, s_dve)
            link, mark, need = own.link, own.mark, own.need
            V = nc.vector
            tt, ts, stt = V.tensor_tensor, V.tensor_scalar, V.scalar_tensor_tensor
            w = wk_

            def exact_exp(out, x, a, b, c):
                link(ts(a, x, 1.4426950408889634, MAGIC, ALU.mult, ALU.add))
                link(ts(a, a, MAGIC, None, ALU.subtract))
                link(stt(b, a, -0.693359375, x, ALU.mult, ALU.add))
                link(stt(b, a, 2.12194440e-4, b, ALU.mult, ALU.add))
                link(ts(c, b, 1.0 / 40320, None, ALU.mult))
                for k in (5040, 720, 120, 24, 6, 2, 1):
                    link(stt(c, c, 1.0 / k, b, ALU.add, ALU.mult))
                link(ts(a.bitcast(I32), a, 127.0, 8388608.0, ALU.add, ALU.mult))
                link(stt(out, c, 1.0, a, ALU.add, ALU.mult))

            dve.wait_ge(s_ssm, 64)
            logdt, loga, aim, cre, cim = (ssm[:, i, :] for i in range(5))
            exact_exp(w[0], logdt, w[10], w[11], w[12])
            link(tt(w[2], w[0], aim, ALU.mult))
            link(ts(w[2], w[2], 0.15915494309189535, None, ALU.mult))
            link(ts(w[10], w[2], MAGIC, None, ALU.add))
            stt(w[2], w[10], MAGIC, w[2], ALU.subtract, ALU.subtract).then_inc(s_small_ready, 1)
            own.done(s_small_ready)
            exact_exp(w[13], loga, w[10], w[11], w[12])
            link(ts(w[13], w[13], -1.0, None, ALU.mult))
            tt(w[1], w[13], w[0], ALU.mult).then_inc(s_small_ready, 1)
            own.done(s_small_ready)
            link(ts(w[7], w[1], float(HALF), None, ALU.mult))
            link(ts(w[8], w[2], float(HALF), None, ALU.mult))
            link(ts(w[10], w[8], MAGIC, None, ALU.add))
            stt(w[8], w[10], MAGIC, w[8], ALU.subtract, ALU.subtract).then_inc(s_base, 1)
            own.done(s_base)

            def context():
                for oc in range(KC):
                    dve.wait_ge(s_cm, oc + 1)
                    dve.wait_ge(s_ctx, 16 * 7)
                    ts(kT[:, oc, :], bank[4 + oc][:, 0:B * NKV], pcol[:, 2 + oc:3 + oc], HD ** -0.5,
                       ALU.add, ALU.mult).then_inc(s_kt, 1)
                    own.done(s_kt)
                link(V.memset(vaug, 1.0))
                for b in range(B):
                    dve.wait_ge(s_cm, 3 + b)
                    ins = tt(vaug[:, b, :, 0:HD], bank[6 + b][0:NKV, 0:D].rearrange("p (h d) -> p h d", d=HD),
                             bv[0:NKV].rearrange("p (h d) -> p h d", d=HD), ALU.add)
                    if b == 0:
                        link(ins)
                    else:
                        ins.then_inc(s_kbz, 1)
                        own.done(s_kbz)

            def expand(v):
                return v.unsqueeze(2).broadcast_to((P, GRP, HALF))

            tq_, tp_ = tq, tp
            st3 = steps[:, :].unsqueeze(1).broadcast_to((P, GRP, HALF))

            def phases(g):
                tq, tp = tq_[g % 2], tp_[g % 2]
                ch = slice(GRP * g, GRP * g + GRP)
                link(tt(tq, expand(w[2][:, ch]), st3, ALU.mult))
                link(ts(trd, tq, cols[:, 0:1], MAGIC, ALU.add, ALU.add))
                stt(tq, trd, MAGIC, tq, ALU.subtract, ALU.subtract).then_inc(s_phase, 1)
                own.done(s_phase)
                link(tt(tp, expand(w[8][:, ch]), st3, ALU.mult))
                link(ts(trd, tp, MAGIC, None, ALU.add))
                stt(tp, trd, MAGIC, tp, ALU.subtract, ALU.subtract).then_inc(s_phase, 1)
                own.done(s_phase)

            def mode_weights():
                dve.wait_ge(s_small_act, 4)
                sb_, sh, th, ea = w[3], w[4], w[5], w[6]
                link(tt(sh, sh, sh, ALU.mult))
                link(tt(sh, sh, ea, ALU.mult))
                link(ts(w[10], th, -1.0, 1.0, ALU.mult, ALU.add))
                link(V.reciprocal(w[10], w[10]))
                link(tt(w[10], w[10], th, ALU.mult))
                link(tt(w[10], w[10], sh, ALU.subtract))
                link(ts(w[10], w[10], 2.0, None, ALU.mult))
                link(tt(w[11], sb_, ea, ALU.mult))
                link(tt(w[3], w[13], w[13], ALU.mult))
                link(tt(w[4], aim, aim, ALU.mult))
                link(tt(w[3], w[3], w[4], ALU.add))
                link(V.reciprocal(w[3], w[3]))
                link(tt(w[4], w[10], w[13], ALU.mult))
                link(tt(w[5], w[11], aim, ALU.mult))
                link(tt(w[4], w[4], w[5], ALU.add))
                link(tt(w[5], w[11], w[13], ALU.mult))
                link(tt(w[6], w[10], aim, ALU.mult))
                link(tt(w[5], w[5], w[6], ALU.subtract))
                link(tt(w[4], w[4], w[3], ALU.mult))
                link(tt(w[5], w[5], w[3], ALU.mult))
                link(tt(w[10], cre, w[4], ALU.mult))
                link(tt(w[11], cim, w[5], ALU.mult))
                link(tt(w[10], w[10], w[11], ALU.subtract))
                link(tt(w[11], cre, w[5], ALU.mult))
                link(tt(w[12], cim, w[4], ALU.mult))
                link(tt(w[11], w[11], w[12], ALU.add))
                link(ts(w[12], w[11], cols[:, 3:4], None, ALU.mult))
                link(stt(w[14], w[10], cols[:, 2:3], w[12], ALU.mult, ALU.add))
                link(ts(w[12], w[11], cols[:, 2:3], None, ALU.mult))
                stt(w[9], w[10], cols[:, 3:4], w[12], ALU.mult, ALU.subtract).then_inc(s_base, 1)
                own.done(s_base)

            def tables(g):
                d = g % 2
                dve.wait_ge(s_sin, g + 1)
                dve.wait_ge(s_dec, g + 1)
                link(tt(tqm[d], tqm[d], tq[d], ALU.mult))
                dve.wait_ge(s_wtd, 2 * g + 2)
                link(tt(tpc[d], tpc[d], tp[d], ALU.add))
                tt(tpm[d], tpm[d], tpc[d], ALU.mult).then_inc(s_tab, 1)
                own.done(s_tab)

            def spectra(hf, k1):
                m = FREQ * hf + k1
                dve.wait_ge(s_xfe, k1 + 1)
                dve.wait_ge(s_kfe, m + 1)
                if m == 0:
                    dve.wait_ge(s_ce, 4)
                r, i = slot_of(k1, 0), image_of(k1)
                xs = xS[:, r:i + 1:i - r, :].rearrange("p a (b n) -> p a b n", b=B)[:, :, :, HC * hf:HC * hf + HC]
                for out, pl in ((0, r), (1, i)):
                    for c in range(2):
                        ins = tt(prod[:, out, c], xs[:, c], kS[hf][:, pl, :].unsqueeze(1).broadcast_to((P, B, HC)),
                                 ALU.mult)
                link(ins)
                if m >= 2:
                    dve.wait_ge(s_z, m - 1)
                y = yf[:, m % 2].rearrange("p a (b n) -> p a b n", b=B)
                link(tt(y[:, 0], prod[:, 0, 0], prod[:, 1, 1], ALU.subtract))
                tt(y[:, 1], prod[:, 0, 1], prod[:, 1, 0], ALU.add).then_inc(s_yf, 1)
                own.done(s_yf)

            phases(0)
            mode_weights()
            context()
            for kind, n in order(HEAD, "dve"):
                if kind == "phases" and n:
                    phases(n)
                elif kind == "tables":
                    tables(n)
                elif kind == "spectra":
                    spectra(*divmod(n, FREQ))

            def statistics(k, tl, src, last):
                link(V.bn_stats(stats[:, tl % 2, :], src))
                ins = V.bn_aggr(mv[:, k, tl, :], stats[:, tl % 2, :])
                if last:
                    ins.then_inc(s_stat[k], 1)
                    own.done(s_stat[k])
                else:
                    link(ins)

            def normalise(k, tl, s_done, last=True):
                ins = ts(tok[:, tl, :], tok[:, tl, :], mv[:, k, tl, 0:1], rstd[:, k, tl:tl + 1], ALU.subtract, ALU.mult)
                if last:
                    ins.then_inc(s_done, 1)
                    own.done(s_done)
                else:
                    link(ins)

            def silu(key, half):
                dve.wait_ge(s_wact, W_FREE[W_AT[key + ("a",)]][1])
                stt(half, thb[:, SILU_AT[key] % 2, :], 1.0, half, ALU.add, ALU.mult).then_inc(s_silu, 1)
                own.done(s_silu)

            for step in order(SCHEDULE, "dve"):
                kind, n = step[0], step[1]
                if kind == "conv":
                    dve.wait_ge(s_r, n + 1)
                    for b in range(B):
                        statistics(0, 2 * n + b, bank[conv_bank(n)][:, D * b:D * b + D], b == 1)
                elif kind == "residual":
                    dve.wait_ge(s_rstd[0], n + 1)
                    dve.wait_ge(s_xbr, 2 * n + 2)
                    for b in range(B):
                        ins = stt(gtmp[:, b, :], bank[conv_bank(n)][:, D * b:D * b + D], mv[:, 0, 2 * n + b, 0:1], lnw,
                                  ALU.subtract, ALU.mult)
                        if b:
                            ins.then_inc(s_rfree, 1)
                            own.done(s_rfree)
                        else:
                            link(ins)
                    for b in range(B):
                        tl = 2 * n + b
                        link(stt(tok[:, tl, :], gtmp[:, b, :], rstd[:, 0, tl:tl + 1], tok[:, tl, :], ALU.mult, ALU.add))
                        statistics(1, tl, tok[:, tl, :], b == 1)
                elif kind == "norm1":
                    dve.wait_ge(s_rstd[1], n + 1)
                    for b in range(B):
                        normalise(1, 2 * n + b, s_x1, b == 1)
                elif kind == "score":
                    hh = step[2]
                    dve.wait_ge(s_smm, 2 * n + hh + 1)
                    if n >= 2:
                        dve.wait_ge(s_tmm, T_AT[("probs", n - 2, 2)] + 1)
                    m = smax[:, 0:8].rearrange("p (a h) -> p a h", a=2)
                    dst = prob[:, n % 2, 8 * NKV * hh:8 * NKV * (hh + 1)].rearrange("p (a h k) -> p a h k", a=2, k=NKV)
                    src = [bank[g][:, 0:GH * NKV].rearrange("p (h k) -> p h k", k=NKV) for g in range(2)]
                    for g in range(2):
                        link(V.tensor_reduce(m[:, g, :], src[g], AX_X, ALU.max))
                    link(tt(dst[:, 0], src[0], m[:, 0, :].unsqueeze(2).broadcast_to((P, GH, NKV)), ALU.subtract))
                    tt(dst[:, 1], src[1], m[:, 1, :].unsqueeze(2).broadcast_to((P, GH, NKV)),
                       ALU.subtract).then_inc(s_ssub, 1)
                    own.done(s_ssub)
                elif kind == "attend":
                    dve.wait_ge(s_pv, n + 1)
                    o3 = bank[4][:, 0:HEADS * (HD + 1)].rearrange("p (h d) -> p h d", d=HD + 1)
                    link(V.reciprocal(rec.unsqueeze(2), o3[:, :, HD:HD + 1]))
                    if n >= 2:
                        dve.wait_ge(s_tmm, T_AT[("turno", n - 2)] + 1)
                    tt(ob[:, n % 2, :].rearrange("p (h d) -> p h d", d=HD), o3[:, :, 0:HD],
                       rec.unsqueeze(2).broadcast_to((P, HEADS, HD)), ALU.mult).then_inc(s_on, 1)
                    own.done(s_on)
                elif kind == "project":
                    dve.wait_ge(s_wo, n + 1)
                    dve.wait_ge(s_bo, n + 1)
                    tt(tok[:, n, :], bank[4][:, 0:D], tok[:, n, :], ALU.add).then_inc(s_u[0], 1)
                    own.done(s_u[0])
                    statistics(2, n, tok[:, n, :], True)
                elif kind == "norm2":
                    dve.wait_ge(s_rstd[2], n + 1)
                    normalise(2, n, s_x2)
                elif kind == "best":
                    dve.wait_ge(s_wact, W_FREE[W_AT[("sim", n, "a")]][1])
                    tp_ = top[:, n % 2]
                    for m in range(2 * FH):
                        ins = V.max(best[:, m, :], sim[:, n % 2, m, :])
                    link(ins)
                    link(tt(pairs.rearrange("p h (a b) -> p h a b", a=TOPK),
                            best[:, 0:FH, :].unsqueeze(3).broadcast_to((P, FH, TOPK, TOPK)),
                            best[:, FH:2 * FH, :].unsqueeze(2).broadcast_to((P, FH, TOPK, TOPK)), ALU.add))
                    for h in range(FH):
                        ins = V.max(tp_[:, h, :], pairs[:, h, :])
                    link(ins)
                    ts(negm[:, n % 2, :], tp_[:, :, 0], -1.0, None, ALU.mult).then_inc(s_best, 1)
                    own.done(s_best)
                    tt(zexp, tp_, tp_[:, :, 0:1].broadcast_to((P, FH, TOPK)), ALU.subtract).then_inc(s_zarg, 1)
                    own.done(s_zarg)
                elif kind == "pair":
                    h, m = step[2], FH * n + step[2]
                    if h == 0:
                        dve.wait_ge(s_zexp, n + 1)
                        link(V.tensor_reduce(zinv, zexp, AX_X, ALU.add))
                        link(V.reciprocal(zinv, zinv))
                        if n >= SUPER:
                            dve.wait_ge(s_wmm, W_AT[("spread", n - SUPER, 1, "d")] + 1)
                    w_, e = rw[:, n % SUPER, :], ebuf[m % 2].rearrange("p a b -> p (a b)")
                    dve.wait_ge(s_e, m + 1)
                    link(stt(e, sxb[m % 2].rearrange("p a b -> p (a b)"), top[:, n % 2, h, TOPK - 1:TOPK], e,
                             ALU.is_ge, ALU.mult))
                    if h == 0:
                        ts(w_, e, zinv[:, h:h + 1], None, ALU.mult).then_inc(s_rfr, 1)
                    else:
                        stt(w_, e, zinv[:, h:h + 1], w_, ALU.mult, ALU.add,
                            accum_out=rsum[:, 0:1] if h == FH - 1 else None).then_inc(s_rfr, 1)
                    own.done(s_rfr)
                elif kind == "total":
                    w_ = rw[:, n % SUPER, NEXP - 1:NEXP]
                    link(ts(rsum[:, 1:2], rsum[:, 0:1], -1.0, float(FH), ALU.mult, ALU.add))
                    tt(w_, w_, rsum[:, 1:2], ALU.add).then_inc(s_rr, 1)
                    own.done(s_rr)
                elif kind == "expert":
                    silu(step, silg[:, step[2], :])
                elif kind == "inner":
                    c, m = step[2], FC * n + step[2]
                    silu(step, gate[:, m % 2, :])
                    dve.wait_ge(s_wact, W_FREE[W_AT[step + ("A",)]][1])
                    if n and c == 0:
                        dve.wait_ge(s_7mm, SUPER * n)
                    tt(hid[:, c, :], upb[:, m % 2, :], gate[:, m % 2, :], ALU.mult).then_inc(s_hid, 1)
                    own.done(s_hid)
                elif kind == "spread":
                    j, i, u = step[2], n % SUPER, W_AT[step + ("d",)]
                    dve.wait_ge(s_wmm, u + 1)
                    if n and j == 0:
                        dve.wait_ge(s_7mm, n)
                    tt(aT[:, 4 * j:4 * j + 4, :], bank[5 + u % 2][:, :].rearrange("p (c n) -> p c n", n=P),
                       silg[:, 4 * j:4 * j + 4, P * i:P * i + P], ALU.mult).then_inc(s_wdve, 1)
                    own.done(s_wdve)
                elif kind == "outer":
                    dve.wait_ge(s_7mm, n + 1)
                    dve.wait_ge(s_bd, n + 1)
                    tt(tok[:, n, :], bank[7][:, 0:D], tok[:, n, :], ALU.add).then_inc(s_7f, 1)
                    own.done(s_7f)
                    statistics(3, n, tok[:, n, :], True)
                elif kind == "norm3":
                    dve.wait_ge(s_rstd[3], n + 1)
                    normalise(3, n, s_out)


SHAPES = {}


def kernel(**inputs):
    import concourse.bacc as bacc
    from concourse.bass_utils import run_bass_kernel_spmd

    g = {k: np.asarray(v) for k, v in inputs.items()}

    def by_chunk(a):
        return np.ascontiguousarray(a.reshape(-1, P, a.shape[-1]).transpose(1, 0, 2))

    def both(a):
        return np.concatenate([a.T, a.T], axis=0)

    def every(a):
        return np.tile(a[None, :], (P, 1))

    fa, fai, fmat, imat = fourier_constants()
    cols, ident, head_mask, shift, steps = mask_constants()
    x = g["x"].reshape(B, NC, NQ, NS, D).transpose(1, 3, 2, 0, 4).reshape(P, TILES, D)
    ctx = g["ctx_1024"].reshape(B * NKV, D)
    keys = g["L0_ffn_keys"].transpose(3, 2, 0, 1).reshape(NKEYS, 2 * FH, NKEYS)
    arrays = {
        "ssm": np.stack([every(g["L0_attn_log_dt"]), both(g["L0_attn_log_A_real"]), both(g["L0_attn_A_imag"]),
                         both(g["L0_attn_C_re"]), both(g["L0_attn_C_im"])], axis=1),
        "skip": g["L0_attn_D"][None, :],
        "cols": cols, "steps": steps, "fa": fa, "fai": fai, "fmat": fmat, "imat": imat, "x": x,
        "ctxT": by_chunk(ctx.T), "wk": by_chunk(g["L0_xattn_Wk"].T), "wv": by_chunk(g["L0_xattn_Wv"].T),
        "wq": by_chunk(g["L0_xattn_Wq"].T), "wo": by_chunk(g["L0_xattn_Wo"].T),
        "pcol": np.concatenate([v.reshape(-1, P).T for v in (
            g["L0_xattn_bq"], g["L0_xattn_bk"], g["L0_ffn_bg"], g["L0_ffn_bu"])], axis=1),
        "rows": np.stack([every(g[n]) for n in (
            "L0_attn_ln_w", "L0_attn_ln_b", "L0_xattn_bo", "L0_ffn_bd", "L0_xattn_bv")], axis=1),
        "shift": shift, "head_mask": head_mask, "ident": ident,
        "wqf": g["L0_ffn_Wq"].T.reshape(2 * FH, NKEYS, D).transpose(1, 0, 2), "keysT": keys,
        "wg": by_chunk(g["L0_ffn_Wg"]), "wu": by_chunk(g["L0_ffn_Wu"]), "wd": by_chunk(g["L0_ffn_Wd"]),
        "dn": by_chunk(g["L0_ffn_down_embed"].T), "up": by_chunk(g["L0_ffn_up_embed"]),
    }
    arrays = {f"in_{k}": np.ascontiguousarray(v) for k, v in arrays.items()}
    nc = bacc.Bacc("TRN2", target_bir_lowering=False, num_devices=1)
    t = {k[3:]: nc.dram_tensor(k, v.shape, F32, kind="ExternalInput").ap() for k, v in arrays.items()}
    for name, shape in (("scr_x", (NQ, NSLOT, NS, B * D)), ("scr_k", (2, NQ, NSLOT, NS, HC)),
                        ("scr_t", (2, HALF, HALF, HC)), ("scr_z", (2, NSLOT, P, B * HC))):
        t[name] = nc.dram_tensor(name, shape, F32, kind="Internal").ap()
    t["out"] = nc.dram_tensor("out", (P, TILES, D), F32, kind="ExternalOutput").ap()
    build(nc, t)
    r = run_bass_kernel_spmd(nc, [arrays], core_ids=[0])
    out = r.results[0]["out"].reshape(NC, NS, NQ, B, D)
    return np.ascontiguousarray(out.transpose(3, 0, 2, 1, 4).reshape(B, L, D))
```

```python
from contextlib import ExitStack

import numpy as np

import concourse.bass as bass
from concourse import mybir

ALU = mybir.AluOpType
ACT = mybir.ActivationFunctionType
AX_X = mybir.AxisListType.X
F32 = mybir.dt.float32
I32 = mybir.dt.int32

P = 128
B, L, D = 2, 1024, 256
NST = 64
NFFT = 2 * L
NC, NQ, NS = 8, 8, 16
KC = D // P
TILES = B * L // P
SUPER = 4
NSUP = TILES // SUPER
W = SUPER * P
NSLOT = 16
FREQ = 9
NKV, HEADS, HD = 77, 16, 16
GH = 4
FLAT = HEADS * NKV
PCH = (FLAT + P - 1) // P
FF = 1024
NEXP, NKEYS, FH, TOPK = 1024, 64, 4, 8
XR = NEXP // NKEYS
FC, EC = FF // P, NEXP // P
MAGIC = 1.5 * 2.0**23
TWO_PI = 6.283185
EPS = 1e-5
GRP = 32
NGRP = D // GRP
HC = D // 2
HALF_GROUPS = NGRP // 2
ZRING = 4
HALF = 32


def slot_of(k1, part):
    if k1 in (0, 8):
        return k1 // 8
    return 2 * k1 + part


def mat_of(k1, kind):
    if k1 == 0:
        return {0: 0, 2: 1}[kind]
    if k1 == 8:
        return {0: 2, 2: 3}[kind]
    return 4 + 3 * (k1 - 1) + kind


NMAT = 4 + 3 * 7


PLACE = {"probs": (0.018, 0.036, 0.325), "score": (0.273, 0.65), "attend": (0.517,), "turno": (0.772,),
         "project": (1.238,), "project_last": (0.95,), "turn1": (0.02, 0.05), "query": (0.2, 0.109),
         "turn2": (-0.001, 0.064), "sim": (0.292,), "sim_first": (0.082,), "best": (0.418,),
         "best_first": (0.119,), "pair": (0.245, 0.35, 0.731, 0.8), "total": (0.96,), "first": (0.324,),
         "sums": (-0.348,), "exps": (-0.041,), "late": (-0.027, 0.048, 0.423),
         "conv": (-2.185, -1.728, -1.313, -1.535, -1.35, -1.358, -1.515, -1.19),
         "ln": (-1.794, -1.527, 0.191, 1.196, 1.775, 2.155, 2.893, 3.011),
         "ln_steps": (-0.127, -0.272, 0.142, 0.24, 0.3), "phases": (-1.53,), "exponents": (-1.983,),
         "sines": (-1.64,), "decays": (-1.246, -1.43), "weigh": (-1.215,), "tables": (0.141,), "taps": (-0.168,),
         "x_second": (1.298, 0.531), "skip": (0.233,), "k_first": (5.415, 8.342), "simw": (-0.619,),
         "x_bias": (7.405, 0.885), "values": (1.689, 0.302), "diagonal": (-0.694,),
         "k_second": (7.144, 0.031, 9.66, 0.124), "spectra": (7.681, 0.064, 10.038, 0.549),
         "inverse": (8.005, 0.183, 10.332, 0.12), "products": (0.0, 1.0, 0.0, 0.996, 0.0, 1.011, 0.0, 0.975),
         "probs_alone": (-0.017, 0.065, 0.304), "score_alone": (0.367, 0.686), "attend_alone": (0.473,),
         "turno_alone": (0.782,), "project_alone": (1.191,), "dev2": (0.051,), "norm2": (0.08,), "dev3": (0.05,),
         "norm3": (0.3,)}
LAG = {("act", "x_second"): 0.187, ("act", "taps"): 0.28, ("act", "k_first"): 0.087, ("act", "k_second"): 0.108,
       ("act", "inverse"): 0.088, ("dve", "score"): 0.096, ("act", "score"): 0.164, ("act", "best"): 0.083,
       ("dve", "attend"): 0.086, ("dve", "expert"): 0.161, ("dve", "inner"): 0.051, ("dve", "outer"): 0.05,
       ("dve", "spread"): 0.016, ("dve", "project"): 0.018, ("act", "norm1"): 0.049, ("act", "norm3"): 0.02,
       ("dve", "phases"): 0.132, ("dve", "tables"): -0.062, ("dve", "spectra"): 0.522, ("dve", "pair"): 0.069,
       ("dve", "ln"): -0.027, ("dve", "residual"): -0.025, ("pool", "turn1"): 0.273, ("pool", "turn2"): 0.008,
       ("pool", "dev1"): 0.035, ("pool", "spectra"): -0.081, ("pool", "weigh"): -0.151,
       ("pool", "exponents"): 0.034}


def image_of(k1):
    return NSLOT + k1 // 8 if k1 in (0, 8) else slot_of(k1, 1)


def heads_of(chunk):
    return chunk * P // NKV, min((chunk * P + P - 1) // NKV, HEADS - 1)


def plan():
    steps = []

    def put(start, kind, n, *rest, key=None, j=0):
        steps.append((start + PLACE[key or kind][j], (kind, n) + rest))
        return steps[-1][0]

    def queries(start, s):
        for kind in ("turn1", "query"):
            for j in range(2):
                put(start, kind, s, j, j=j)

    def normed(at, tl, k):
        put(at, f"dev{k}", tl)
        put(at, f"norm{k}", tl)

    def products(f, i):
        r = SUPER * f
        if i == 0:
            return [("expert", f, c) for c in range(6)]
        if i == 1:
            return [("expert", f, 6), ("expert", f, 7)] + [("inner", f, c) for c in range(4)]
        if i == 2:
            return [("inner", f, c) for c in range(4, 8)] + [("spread", r, 0), ("spread", r, 1)]
        return [("outer", r), ("spread", r + 1, 0), ("spread", r + 1, 1), ("outer", r + 1),
                ("spread", r + 2, 0), ("spread", r + 2, 1), ("outer", r + 2)]

    for q in range(NQ):
        steps.append((PLACE["conv"][q], ("conv", q)))
        for k, kind in enumerate(("ln", "dev0", "residual", "dev1", "norm1")):
            steps.append((PLACE["ln"][q] + PLACE["ln_steps"][k], (kind, q)))
    queries(-1, 0)
    for h in range(2):
        put(-1, "score", 0, h, j=h)
    for tl in range(TILES):
        s, i = divmod(tl, SUPER)
        start = tl
        alone = "_alone" if tl < SUPER - 1 else ""
        for j in range(3):
            put(start, "probs", tl, j, key="probs" + alone, j=j)
        put(start, "attend", tl, key="attend" + alone)
        put(start, "turno", tl, key="turno" + alone)
        normed(put(start, "project", tl, key="project_last" if i == SUPER - 1 else "project" + alone), tl, 2)
        if i == SUPER - 1 and s + 1 < NSUP:
            queries(start, s + 1)
        if tl + 1 < TILES:
            for h in range(2):
                put(start, "score", tl + 1, h, key="score" + alone, j=h)
        start = tl + SUPER
        if i == 0:
            for j in range(2):
                put(start, "turn2", s, j, j=j)
            put(start, "sim", tl, key="sim_first")
            put(start, "best", tl, key="best_first")
        work = products(s, i)
        for k, y in enumerate(work):
            lo, hi = PLACE["products"][2 * i:2 * i + 2]
            at = start + lo + (hi - lo) * (k + 0.5) / len(work)
            steps.append((at, y))
            if y[0] == "outer":
                normed(at, y[1], 3)
        for h in range(FH):
            at = put(start, "pair", tl, h, j=h)
            for kind in ("sums", "exps"):
                steps.append((max(at + PLACE[kind][0], start + PLACE["best_first"][0] + 0.01 if i == 0 else at - 1.0),
                              (kind, tl, h)))
        put(start, "first", tl)
        put(start, "total", tl)
        if i < SUPER - 1:
            put(start, "sim", tl + 1)
            put(start, "best", tl + 1)
        else:
            for j in range(2):
                put(start + 1, "spread", tl, j, key="late", j=j)
            normed(put(start + 1, "outer", tl, key="late", j=2), tl, 3)
    return steps


def head():
    steps = []
    steps += [(PLACE["simw"][0], ("simw", 0)), (PLACE["diagonal"][0], ("diagonal", 0))]
    steps += [(PLACE["values"][0] + PLACE["values"][1] * n, ("values", n)) for n in range(PCH)]
    for g in range(NGRP):
        for kind in ("phases", "exponents", "sines", "weigh", "tables", "taps"):
            steps.append((g + PLACE[kind][0], (kind, g)))
        steps.append((g + PLACE["decays"][g % 2], ("decays", g)))
    for tl in range(TILES):
        steps.append((PLACE["x_bias"][0] + PLACE["x_bias"][1] * tl, ("x_bias", tl)))
    for k in range(FREQ):
        steps.append((PLACE["x_second"][0] + PLACE["x_second"][1] * k, ("x_second", k)))
    for hf in range(2):
        steps.append((HALF_GROUPS * (hf + 1) - 1 + PLACE["skip"][0], ("skip", hf)))
        steps.append((PLACE["k_first"][hf], ("k_first", hf)))
        for kind in ("k_second", "spectra", "inverse"):
            for k in range(FREQ):
                steps.append((PLACE[kind][2 * hf] + PLACE[kind][2 * hf + 1] * k, (kind, FREQ * hf + k)))
    return steps


def order(steps, engine):
    return [y for _, y in sorted(steps, key=lambda v: v[0] + LAG.get((engine, v[1][0]), 0.0))]


def fourier_constants():
    c, s = np.divmod(np.arange(P), NS)
    fwd = np.zeros((P, NSLOT, NS))
    inv = np.zeros((NSLOT, NS, P))
    for k1 in range(FREQ):
        ang = 2 * np.pi * k1 * c / NSLOT
        own = 1.0 if k1 in (0, 8) else 2.0
        fwd[np.arange(P), slot_of(k1, 0), s] = np.cos(ang)
        inv[slot_of(k1, 0), s, np.arange(P)] = own * np.cos(ang) / NFFT
        if k1 not in (0, 8):
            fwd[np.arange(P), slot_of(k1, 1), s] = -np.sin(ang)
            inv[slot_of(k1, 1), s, np.arange(P)] = -own * np.sin(ang) / NFFT
    fmat, imat = np.zeros((P, NMAT, P)), np.zeros((P, NMAT, P))
    pp, kk = np.meshgrid(np.arange(P), np.arange(P), indexing="ij")
    for k1 in range(FREQ):
        ang = 2 * np.pi * ((pp * (k1 + 16 * kk)) % NFFT) / NFFT
        for kind, m in ((0, np.cos(ang)), (1, np.sin(ang)), (2, -np.sin(ang))):
            if kind == 1 and k1 in (0, 8):
                continue
            fmat[:, mat_of(k1, kind)] = m
            imat[:, mat_of(k1, kind)] = m.T
    inv = inv.reshape(2, P, P).transpose(1, 0, 2)
    return [np.ascontiguousarray(a, dtype=np.float32) for a in (fwd.reshape(P, 2, P), inv, fmat, imat)]


def mask_constants():
    cols = np.zeros((P, 8), np.float32)
    cols[:64, 0] = -0.25
    cols[:64, 1] = np.pi / 2
    cols[:64, 2] = 2.0
    cols[64:, 3] = -2.0
    cols[:, 4] = np.pi / 2
    cols[:, 5] = -0.5
    ident = np.eye(P, dtype=np.float32)
    head_mask = np.zeros((P, P // HD), np.float32)
    head_mask[np.arange(P), np.arange(P) // HD] = 1.0
    shift = np.zeros((NKV, 3 * P), np.float32)
    shift[np.arange(NKV), np.arange(NKV) + P] = 1.0
    steps = np.tile(np.arange(HALF, dtype=np.float32), (P, 1))
    return [cols, ident, head_mask, shift, steps]


def build(nc, t):
    with ExitStack() as ctx:
        def sb(name, shape, dt=F32):
            return ctx.enter_context(nc.sbuf_tensor(name, shape, dt))

        def sem(name):
            return ctx.enter_context(nc.semaphore(name))

        bank = [ctx.enter_context(nc.psum_tensor(f"bank{i}", [P, 512], F32)) for i in range(8)]

        tok = sb("tok", [P, TILES, D])
        wq = sb("wq", [P, KC, D])
        wo = sb("wo", [P, KC, D])
        wsim = sb("wsim", [P, KC, 2 * FH * NKEYS])
        rows = sb("rows", [P, 5, D])
        lnw, lnb, bo, bd, bv = (rows[:, i, :] for i in range(5))
        pcol = sb("pcol", [P, 4 + 2 * FC])
        ident = sb("ident", [P, P])
        cols = sb("cols", [P, 8])
        head_mask = sb("head_mask", [P, P // HD])
        steps = sb("steps", [P, HALF])
        kbd = sb("kbd", [P, B, KC, 8 * NKV])
        vbd = sb("vbd", [P, B, PCH, 51])
        stats = sb("stats", [P, 2, 6])
        mv = sb("mv", [P, 4, TILES, 2])
        rstd = sb("rstd", [P, 4, TILES])
        skip = sb("skip", [1, D])

        WORDS = 41600
        arena = sb("arena", [P, WORDS])
        place = {}

        def part(name, start, *dims, rows_=P):
            n = int(np.prod(dims))
            assert start + n <= WORDS, (name, start, n)
            place[name] = (start, start + n)
            v = arena[0:rows_, start:start + n]
            if len(dims) == 1:
                return v
            names = "abcde"[:len(dims)]
            return v.rearrange(f"p ({' '.join(names)}) -> p {' '.join(names)}",
                               **{k: d for k, d in zip(names, dims)})

        o_a, o_b, o_tab, o_par, o_mat, o_u = 0, 8192, 17408, 28672, 33792, 37504
        cA = part("cA", o_a, 2, NQ, 512)
        ktime = part("ktime", o_a, HALF, HC, rows_=HALF)
        kQ = part("kQ", o_a + 4096, NQ, HC)
        kS = [part("kS0", o_a + 5120, NSLOT + 2, HC), part("kS1", o_tab + 8192, NSLOT + 2, HC)]
        kA = [part("kA0", o_a + 5120, 2, NQ, HC), part("kA1", o_tab + 8192, 2, NQ, HC)]
        xS = part("xS", o_b, NSLOT + 2, 512)
        prod = part("prod", o_a + 7424, 1, 2, B, HC)
        shiftn = part("shiftn", o_a + 7936, 4, TILES)
        pim = part("pim", o_u, 2, 2, B, HC)
        yf = part("yf", o_u + 1024, 2, 2, 2 * HC)
        zring = part("zring", o_u + 2048, ZRING, 2, 2 * HC)
        zB = part("zB", o_tab, 2, 2, NQ, 2 * HC)
        tq, tqm, tp, tpm, tpc = ([part(f"tab{i}{d}", o_tab + 2048 * i + 1024 * d, GRP, HALF) for d in range(2)]
                                 for i in range(5))
        trd = part("trd", o_tab + 10240, GRP, HALF)
        wqf = part("wqf", o_u, 2 * FH, D, rows_=NKEYS)
        keysT = part("keysT", o_u + 2048, 2 * FH, NKEYS, rows_=NKEYS)
        wk = part("wk", o_b, KC, D)
        wv = part("wv", o_b + 512, KC, D)
        ctxT = part("ctxT", o_b + 1024, KC, B * NKV)
        kT = part("kT", o_u + 2560, KC, B * NKV)
        vaug = part("vaug", o_u + 2868, B, HEADS, HD + 1, rows_=NKV)
        shift = part("shift", o_u + 3412, 3 * P, rows_=NKV)
        wk_ = [None] * 15
        for j, i in enumerate((1, 2, 7, 8, 9, 14, 0, 3, 4, 5, 6, 10, 11, 12, 13)):
            wk_[i] = part(f"w{i}", o_par + D * j, D)
        ssm = part("ssm", o_par + 15 * D, 5, D)
        imat = part("imat", o_par + 6 * D, NMAT, P)
        fmat = part("fmat", o_mat, NMAT, P)
        fa = part("fa", o_mat + 3200, 2, P)
        fai = part("fai", o_mat + 3456, 2, P)

        o_wt = 16384
        wg, wu, dn = (part(n, o_wt + 2048 * i, KC, FF) for i, n in ((0, "wg"), (1, "wu"), (3, "dn")))
        wd, up = (part(n, o_wt + 2048 * i, FC, D) for i, n in ((2, "wd"), (4, "up")))
        o_w = o_wt + 10240
        silg = part("silg", o_w, EC, W)
        hid = part("hid", o_w + 4096, FC, W)
        rconv = part("rconv", o_w + 4096, TILES, D)
        x2T = part("x2T", o_w + 8192, KC, W)
        sim = part("sim", o_w + 9216, 2, 2 * FH, NKEYS)
        ebuf = [part("ebuf0", o_w + 10240, XR, NKEYS)]
        o_l = o_w + 11264
        ebuf.append(part("ebuf1", o_l, XR, NKEYS))
        sxb = [part("sx0", o_l + 1024, XR, NKEYS)]
        best = part("best", o_l + 2048, 2 * FH, TOPK)
        pairs = part("pairs", o_l + 2112, FH, TOPK * TOPK)
        top = part("top", o_l + 2368, 2, FH, TOPK)
        zexp = part("zexp", o_l + 2432, FH, TOPK)
        zinv = part("zinv", o_l + 2464, FH)
        negm = part("negm", o_l + 2468, 2, FH)
        rsum = part("rsum", o_l + 2476, 2)
        smax = part("smax", o_l + 2488, 8)
        rec = part("rec", o_l + 2496, HEADS)
        vare = part("vare", o_l + 2512, 4)
        gtmp = part("gtmp", o_l + 2516, B, D)
        x1T = part("x1T", o_a, KC, W)
        qT = part("qT", o_a + 1024, KC, W)
        prob = part("prob", o_a + 2048, 2, FLAT)
        pT = part("pT", o_a + 4512, PCH, P)
        ob = part("ob", o_a + 5792, 2, D)
        oT = part("oT", o_a + 6304, 2, KC, P)
        sxb.append(part("sx1", o_a + 6816, XR, NKEYS))
        rw = part("rw", o_b, SUPER, NEXP)
        aT = part("aT", o_b + 4096, EC, P)
        gate = part("gate", o_b + 5120, 3, W)
        thb = part("thb", o_b + 6656, 3, W)
        upb = part("upb", o_l + 2516, 2, W)

        s_ssm, s_cst, s_ctx, s_wsim_in, s_ffn_in = (sem(n) for n in (
            "ssm_loaded", "const_loaded", "ctx_loaded", "simw_loaded", "ffn_loaded"))
        s_x = [sem(f"x{q}_loaded") for q in range(NQ)]
        s_mat = sem("mat_loaded")
        s_dve, s_pool, s_actc = sem("dve_steps"), sem("pool_steps"), sem("act_steps")
        s_small_ready = sem("small_ready")
        s_small_act = sem("small_act")
        s_base = sem("table_base_ready")
        s_outer = sem("decay_outer_ready")
        s_phase = sem("table_phase_ready")
        s_sin = sem("table_sines_ready")
        s_dec = sem("table_decays_ready")
        s_wtd = sem("table_sines_weighted")
        s_tab = sem("table_ready")
        s_ktm = sem("ktime_mm")
        s_kev = sem("ktime_evac")
        s_kdone = sem("ktime_done")
        s_kw, s_kq, s_kaw, s_kb, s_zr = ([sem(f"{n}{h}") for h in range(2)] for n in (
            "taps_written", "taps_moved", "ka_written", "kb_loaded", "z_loaded"))
        s_xa, s_xae, s_xaw, s_xb = sem("xa_mm"), sem("xa_evac"), sem("xa_written"), sem("xb_loaded")
        s_imat = sem("imat_loaded")
        s_ka, s_kae = sem("ka_mm"), sem("ka_evac")
        s_kfm, s_kfe = sem("kf_mm"), sem("kf_evac")
        s_xf, s_xfe, s_yf = sem("xf_mm"), sem("xf_evac"), sem("y_ready")
        s_im = sem("xk_imaginary")
        s_z, s_ze = sem("z_mm"), sem("z_evac")
        s_zw = [sem(f"z_written{d}") for d in range(ZRING)]
        s_cm, s_kt, s_ce = sem("ctx_mm"), sem("ctx_keys"), sem("ctx_evac")
        s_kbd = sem("kbd_ready")
        s_kbz = sem("vaug_ready")

        s_xbr = sem("x_plus_bias")
        s_x1, s_x2, s_out = sem("x1_ready"), sem("x2_ready"), sem("out_ready")
        s_outw = sem("out_written")
        s_stat = [sem(f"norm{n}_stats") for n in range(4)]
        s_rstd = [sem(f"norm{n}_rstd") for n in range(4)]
        s_u = [sem("attn_residual")]
        s_bo, s_bd = sem("bo_added"), sem("bd_added")
        s_tmm, s_tev = sem("turned_mm"), sem("turned_evac")
        s_wmm, s_wact, s_wdve = sem("wide_mm"), sem("wide_read_act"), sem("wide_read_dve")
        s_smm, s_ssub, s_exp = sem("score_mm"), sem("score_shifted"), sem("score_exp")
        s_pv, s_on, s_wo = sem("pv_mm"), sem("attn_normed"), sem("wo_mm")
        s_best, s_zarg, s_zexp = sem("pair_top"), sem("pair_args"), sem("pair_exp")
        s_sx, s_e, s_rfr, s_rr = sem("pair_sums"), sem("pair_exps"), sem("pair_used"), sem("weights_ready")
        s_7mm, s_7f = sem("outer_mm"), sem("outer_read")
        s_w0 = sem("first_weights")
        s_half = sem("gate_bias_halved")
        s_hid = sem("hidden_ready")
        s_silu = sem("silu_ready")

        HEAD = head()
        SCHEDULE = plan()
        PLAN = order(SCHEDULE, "pe")
        T_AT = {step: u for u, step in enumerate(y for y in PLAN if y[0] in ("turn1", "turn2", "probs", "turno"))}
        W_AT, W_DONE, W_FREE, count = {}, [], [], {"a": 0, "d": 0, "w": 0}
        SILU_AT = {step: u for u, step in enumerate(y for y in PLAN if y[0] in ("expert", "inner"))}
        READER = {"query": "a", "sim": "a", "expert": "a", "inner": "aA", "spread": "d", "outer": "o", "conv": "a"}
        for step in PLAN:
            for part_ in READER.get(step[0], ""):
                W_AT[step + (part_,)] = len(W_FREE)
                if part_ == "o":
                    W_DONE.append((s_7mm, step[1] + 1))
                    W_FREE.append((s_7f, step[1] + 1))
                else:
                    eng = part_.lower()
                    count[eng] += 1
                    count["w"] += 1
                    W_DONE.append((s_wmm, count["w"]))
                    W_FREE.append((s_wdve if eng == "d" else s_wact, count[eng]))

        def w_bank(u):
            return bank[5 + u % 3]

        scr_x = t["scr_x"]
        scr_k = t["scr_k"]
        scr_t = t["scr_t"]
        scr_z = t["scr_z"]

        def spectrum_of_x(k1, hf):
            r, i = slot_of(k1, 0), image_of(k1)
            xs = xS[:, r:i + 1:i - r, :].rearrange("p a (b n) -> p a b n", b=B)
            return xs[:, :, :, HC * hf:HC * hf + HC], (r, i)

        def z_writes(upto, d):
            return len(range(d, upto, ZRING))

        class Steps:

            def __init__(self, eng, s):
                self.eng, self.s, self.n = eng, s, 0
                self.counts = {}

            def mark(self, ins):
                self.n += 1
                ins.then_inc(self.s, 1)
                return self.n

            def need(self, k):
                self.eng.wait_ge(self.s, k)

            def link(self, ins):
                self.need(self.mark(ins))

            def done(self, s):
                self.counts[id(s)] = self.counts.get(id(s), 0) + 1
                self.eng.wait_ge(s, self.counts[id(s)])

        block = ctx.enter_context(nc.Block())

        @block.sync
        def _(sp):
            sp.dma_start(ssm, t["ssm"]).then_inc(s_ssm, 16)
            sp.dma_start(cols[:, :], t["cols"]).then_inc(s_ssm, 16)
            sp.dma_start(steps[:, :], t["steps"]).then_inc(s_ssm, 16)
            sp.dma_start(skip[:, :], t["skip"]).then_inc(s_ssm, 16)
            sp.dma_start(fa, t["fa"]).then_inc(s_cst, 16)
            for q in range(NQ):
                sp.dma_start(tok[:, 2 * q:2 * q + 2, :], t["x"][:, 2 * q:2 * q + 2, :]).then_inc(s_x[q], 16)
            for dst, n in ((ctxT, "ctxT"), (wk, "wk"), (wv, "wv"), (pcol[:, :], "pcol"), (shift, "shift"),
                           (head_mask[:, :], "head_mask"), (rows[:, :, :], "rows")):
                sp.dma_start(dst, t[n]).then_inc(s_ctx, 16)
            sp.dma_start(wqf, t["wqf"]).then_inc(s_wsim_in, 16)
            sp.dma_start(keysT, t["keysT"]).then_inc(s_wsim_in, 16)
            for dst, n in ((fmat, "fmat"), (fai, "fai"), (wq[:, :, :], "wq"), (wo[:, :, :], "wo"),
                           (ident[:, :], "ident")):
                sp.dma_start(dst, t[n]).then_inc(s_mat, 16)
            for q in range(NQ):
                sp.wait_ge(s_xae, 2 * (q + 1))
                for h in range(2):
                    sp.dma_start(scr_x[q, 8 * h:8 * h + 8].rearrange("r s n -> (r s) n"),
                                 cA[:, h, q, :]).then_inc(s_xaw, 16)
            sp.wait_ge(s_base, 2)
            sp.dma_start(imat, t["imat"]).then_inc(s_imat, 16)
            sp.wait_ge(s_xaw, 16 * 2 * NQ)
            sp.wait_ge(s_cm, 4)
            for q in range(NQ):
                sp.dma_start(xS[16 * q:16 * q + 16, 0:NSLOT, :],
                             scr_x[q].rearrange("r s n -> s r n")).then_inc(s_xb, 16)
            for hf in range(2):
                sp.wait_ge(s_kdone, hf + 1)
                sp.dma_start(scr_t[hf], ktime).then_inc(s_kw[hf], 16)
                sp.wait_ge(s_kw[hf], 16)
                taps = scr_t[hf].rearrange("i j n -> (i j) n").rearrange("(c q s) n -> c s q n", c=NC, q=NQ)
                if hf:
                    sp.wait_ge(s_ka, 4)
                for c in range(NC):
                    sp.dma_start(kQ[16 * c:16 * c + 16, :, :], taps[c]).then_inc(s_kq[hf], 16)
                for h in range(2):
                    sp.wait_ge(s_kae, 4 * hf + 2 * h + 2)
                    sp.dma_start(scr_k[hf, :, 8 * h:8 * h + 8].rearrange("q r s n -> (r s) q n"),
                                 kA[hf][:, h]).then_inc(s_kaw[hf], 16)
                sp.wait_ge(s_kaw[hf], 16 * 2)
                for q in range(NQ):
                    sp.dma_start(kS[hf][16 * q:16 * q + 16, 0:NSLOT, :],
                                 scr_k[hf, q].rearrange("r s n -> s r n")).then_inc(s_kb[hf], 16)
            sp.wait_ge(s_ktm, 2 * NGRP)
            for n in range(2 * FREQ):
                hf, k = divmod(n, FREQ)
                sp.wait_ge(s_zw[n % ZRING], 16 * z_writes(n + 1, n % ZRING))
                for r in range(slot_of(k, 0), slot_of(k, 0) + (1 if k in (0, 8) else 2)):
                    h, rr = divmod(r, 8)
                    sp.dma_start(zB[16 * rr:16 * rr + 16, hf, h, :, :],
                                 scr_z[hf, r].rearrange("(q s) n -> s q n", s=NS)).then_inc(s_zr[hf], 16)
            sp.wait_ge(*W_DONE[W_AT[("conv", NQ - 1, "a")]])
            for dst, n in ((dn, "dn"), (wg, "wg"), (wu, "wu"), (wd, "wd"), (up, "up")):
                sp.dma_start(dst, t[n]).then_inc(s_ffn_in, 16)
            for tl in range(TILES):
                sp.wait_ge(s_out, tl + 1)
                sp.dma_start(t["out"][:, tl, :], tok[:, tl, :]).then_inc(s_outw, 16)
            sp.wait_ge(s_outw, 16 * TILES)

        @block.tensor
        def _(pe):
            mm = nc.tensor.matmul
            pe.wait_ge(s_cst, 16)
            for q in range(NQ):
                pe.wait_ge(s_x[q], 16)
                for h in range(2):
                    i = 2 * q + h
                    if i >= 4:
                        pe.wait_ge(s_xae, i - 3)
                    mm(bank[i % 4][:, :], fa[:, h, :],
                       tok[:, 2 * q:2 * q + 2, :].rearrange("p a b -> p (a b)"),
                       start=True, stop=True).then_inc(s_xa, 1)
            pe.wait_ge(s_ctx, 16 * 7)
            for oc in range(KC):
                for ic in range(KC):
                    ins = mm(bank[4 + oc][:, 0:B * NKV], wk[:, ic, P * oc:P * oc + P], ctxT[:, ic, :],
                             start=(ic == 0), stop=(ic == KC - 1))
                ins.then_inc(s_cm, 1)
            for b in range(B):
                for ic in range(KC):
                    ins = mm(bank[6 + b][0:NKV, 0:D], ctxT[:, ic, NKV * b:NKV * b + NKV], wv[:, ic, :],
                             start=(ic == 0), stop=(ic == KC - 1))
                ins.then_inc(s_cm, 1)
            pe.wait_ge(s_wsim_in, 32)
            pe.wait_ge(s_kt, 2)
            for oc in range(KC):
                for m in range(2 * FH):
                    ins = mm(bank[4 + oc][:, NKEYS * m:NKEYS * m + NKEYS], wqf[:, m, P * oc:P * oc + P],
                             keysT[:, m, :], start=True, stop=True, skip_group_check=True)
                ins.then_inc(s_cm, 1)
            def spread_values(b, chunks):
                pe.wait_ge(s_kbz, 1)
                for ch in chunks:
                    h0, h1 = heads_of(ch)
                    for h in range(h0, h1 + 1):
                        at = P + P * ch - NKV * h
                        ins = mm(bank[6 + b][:, 51 * ch + 17 * (h - h0):51 * ch + 17 * (h - h0) + 17],
                                 shift[:, at:at + P], vaug[:, b, h, :], start=True, stop=True,
                                 skip_group_check=True)
                if chunks[-1] == PCH - 1:
                    ins.then_inc(s_cm, 1)

            def taps(g):
                pe.wait_ge(s_tab, g + 1)
                for m in range(2):
                    i = 2 * g + m
                    if i >= 2:
                        pe.wait_ge(s_kev, i - 1)
                    for hh in range(16):
                        ch = 16 * m + hh
                        ins = mm(bank[4 + i % 2][0:HALF, HALF * hh:HALF * hh + HALF], tpm[g % 2][:, ch, :],
                                 tqm[g % 2][:, ch, :], start=True, stop=True, skip_group_check=True)
                    ins.then_inc(s_ktm, 1)

            def second_stage(k1, re, im, src):
                r, i = slot_of(k1, 0), slot_of(k1, 1)
                two = k1 not in (0, 8)
                mm(re, fmat[:, mat_of(k1, 0), :], src(r), start=True, stop=not two, skip_group_check=True)
                if two:
                    mm(re, fmat[:, mat_of(k1, 1), :], src(i), start=False, stop=True, skip_group_check=True)
                ins = mm(im, fmat[:, mat_of(k1, 2), :], src(r), start=True, stop=not two, skip_group_check=True)
                if two:
                    ins = mm(im, fmat[:, mat_of(k1, 0), :], src(i), start=False, stop=True, skip_group_check=True)
                return ins

            def x_second(k1):
                pe.wait_ge(s_mat, 16 * 5)
                pe.wait_ge(s_xb, 16 * NQ)
                if k1 >= 2:
                    pe.wait_ge(s_xfe, k1 - 1)
                bb = 2 * (k1 % 2)
                second_stage(k1, bank[bb][:, :], bank[bb + 1][:, :], lambda r: xS[:, r, :]).then_inc(s_xf, 1)

            def k_first(hf):
                pe.wait_ge(s_kq[hf], 16 * NC)
                if hf:
                    pe.wait_ge(s_kfe, FREQ)
                else:
                    pe.wait_ge(s_ce, 4)
                for i in range(4):
                    h, qh = divmod(i, 2)
                    if i >= 2 or hf:
                        pe.wait_ge(s_kae, 4 * hf + max(i - 1, 0))
                    mm(bank[6 + i % 2][:, :], fa[:, h, :], kQ[:, 4 * qh:4 * qh + 4, :].rearrange("p a b -> p (a b)"),
                       start=True, stop=True).then_inc(s_ka, 1)

            def k_second(hf, k1):
                pe.wait_ge(s_kb[hf], 16 * NQ)
                if k1 >= 2:
                    pe.wait_ge(s_kfe, FREQ * hf + k1 - 1)
                else:
                    pe.wait_ge(s_kae, 4 * hf + 4)
                bk = bank[6 + k1 % 2]
                second_stage(k1, bk[:, 0:HC], bk[:, HC:2 * HC], lambda r: kS[hf][:, r, :]).then_inc(s_kfm, 1)

            def inverse(hf, k):
                m = FREQ * hf + k
                pe.wait_ge(s_imat, 16)
                pe.wait_ge(s_xfe, FREQ)
                pe.wait_ge(s_yf, m + 1)
                if m >= 4:
                    pe.wait_ge(s_ze, m - 3)
                bk, y = bank[m % 4], yf[:, m % 2]
                mm(bk[:, 0:2 * HC], imat[:, mat_of(k, 0), :], y[:, 0, :], start=True, stop=False, skip_group_check=True)
                ins = mm(bk[:, 0:2 * HC], imat[:, mat_of(k, 2), :], y[:, 1, :], start=False, stop=True,
                         skip_group_check=True)
                if k not in (0, 8):
                    mm(bk[:, 2 * HC:4 * HC], imat[:, mat_of(k, 1), :], y[:, 0, :], start=True, stop=False,
                       skip_group_check=True)
                    ins = mm(bk[:, 2 * HC:4 * HC], imat[:, mat_of(k, 0), :], y[:, 1, :], start=False, stop=True,
                             skip_group_check=True)
                ins.then_inc(s_z, 1)

            for kind, n in order(HEAD, "pe"):
                if kind == "taps":
                    if n == 0:
                        pe.wait_ge(s_ce, 2)
                    taps(n)
                elif kind == "values":
                    b, j = divmod(n, PCH // 2)
                    spread_values(b, (2 * j, 2 * j + 1))
                elif kind == "x_second":
                    x_second(n)
                elif kind == "k_first":
                    k_first(n)
                elif kind == "k_second":
                    k_second(*divmod(n, FREQ))
                elif kind == "inverse":
                    inverse(*divmod(n, FREQ))

            def t_unit(key):
                u = T_AT[key]
                if u >= 2:
                    pe.wait_ge(s_tev, u - 1)
                return bank[2 + u % 2]

            def w_unit(key):
                u = W_AT[key]
                if u >= 3:
                    pe.wait_ge(*W_FREE[u - 3])
                return w_bank(u)

            def conv(q):
                for hf in range(2):
                    pe.wait_ge(s_zr[hf], 16 * NSLOT)
                pe.wait_ge(s_kev, 2 * NGRP)
                pe.wait_ge(s_kfe, 2 * FREQ)
                bk = w_unit(("conv", q, "a"))[:, :].rearrange("p (b f n) -> p f b n", b=B, f=2)
                for hf in range(2):
                    for h in range(2):
                        ins = mm(bk[:, hf], fai[:, h, :], zB[:, hf, h, q, :].rearrange("p (b n) -> p b n", b=B),
                                 start=(h == 0), stop=(h == 1), skip_group_check=True)
                ins.then_inc(s_wmm, 1)

            def turn_tokens(key, s, j):
                bk = t_unit(key)
                for i in range(2):
                    for k in range(KC):
                        ins = nc.tensor.transpose(bk[:, P * (2 * i + k):P * (2 * i + k) + P],
                                                  tok[:, SUPER * s + 2 * j + i, P * k:P * k + P], ident[:, :])
                ins.then_inc(s_tmm, 1)

            def wide(key, w, m, src):
                bk = w_unit(key)
                for k in range(KC):
                    ins = mm(bk[:, :], w[:, k, P * m:P * m + P], src[:, k, :], start=(k == 0), stop=(k == KC - 1))
                ins.then_inc(s_wmm, 1)

            for step in order(SCHEDULE, "pe"):
                kind, n = step[0], step[1]
                if kind == "conv":
                    conv(n)
                elif kind == "turn1":
                    pe.wait_ge(s_x1, 2 * n + step[2] + 1)
                    turn_tokens(step, n, step[2])
                elif kind == "query":
                    pe.wait_ge(s_tev, T_AT[("turn1", n, 1)] + 1)
                    wide(step + ("a",), wq, step[2], x1T)
                elif kind == "score":
                    hh, i, b = step[2], n % SUPER, n % B
                    pe.wait_ge(s_wact, W_FREE[W_AT[("query", n // SUPER, hh, "a")]][1])
                    if n == 0:
                        pe.wait_ge(s_kbd, 1)
                    if n or hh:
                        pe.wait_ge(s_ssub, 2 * n + hh)
                    for g in range(2):
                        ins = mm(bank[g][:, 0:GH * NKV], qT[:, hh, P * i:P * i + P],
                                 kbd[:, b, hh, GH * NKV * g:GH * NKV * (g + 1)], start=True, stop=True)
                    ins.then_inc(s_smm, 1)
                elif kind == "probs":
                    j = step[2]
                    pe.wait_ge(s_exp, 2 * n + 2)
                    bk = t_unit(step)
                    for c in range(4 * j, min(4 * j + 4, PCH)):
                        m = min(P, FLAT - P * c)
                        ins = nc.tensor.transpose(bk[0:m, P * (c % 4):P * (c % 4) + P],
                                                  prob[:, n % 2, P * c:P * c + m], ident[:, :])
                    ins.then_inc(s_tmm, 1)
                elif kind == "attend":
                    if n:
                        pe.wait_ge(s_u[0], n)
                    for c in range(PCH):
                        if c % 4 == 0:
                            pe.wait_ge(s_tev, T_AT[("probs", n, c // 4)] + 1)
                        h0, h1 = heads_of(c)
                        m = min(P, FLAT - P * c)
                        k = (HD + 1) * (h1 - h0 + 1)
                        ins = mm(bank[4][:, (HD + 1) * h0:(HD + 1) * h0 + k], pT[0:m, c, :], vbd[0:m, n % B, c, 0:k],
                                 start=(c == 0), stop=(c == PCH - 1), skip_group_check=True)
                    ins.then_inc(s_pv, 1)
                elif kind == "turno":
                    pe.wait_ge(s_on, n + 1)
                    bk = t_unit(step)
                    for k in range(KC):
                        ins = nc.tensor.transpose(bk[:, P * k:P * k + P], ob[:, n % 2, P * k:P * k + P], ident[:, :])
                    ins.then_inc(s_tmm, 1)
                elif kind == "project":
                    pe.wait_ge(s_tev, T_AT[("turno", n)] + 1)
                    for k in range(KC):
                        ins = mm(bank[4][:, 0:D], oT[:, n % 2, k, :], wo[:, k, :], start=(k == 0), stop=(k == KC - 1))
                    ins.then_inc(s_wo, 1)
                elif kind == "turn2":
                    pe.wait_ge(s_x2, SUPER * n + 2 * step[2] + 2)
                    turn_tokens(step, n, step[2])
                elif kind == "sim":
                    f, i = divmod(n, SUPER)
                    pe.wait_ge(s_tev, T_AT[("turn2", f, i // 2)] + 1)
                    bk = w_unit(step + ("a",))
                    for k in range(KC):
                        ins = mm(bk[:, :], x2T[:, k, P * i:P * i + P], wsim[:, k, :], start=(k == 0), stop=(k == KC - 1))
                    ins.then_inc(s_wmm, 1)
                elif kind == "expert":
                    if step[2] == 0:
                        pe.wait_ge(s_ffn_in, 16 * 5)
                        pe.wait_ge(s_tev, T_AT[("turn2", n, 1)] + 1)
                    wide(step + ("a",), dn, step[2], x2T)
                elif kind == "inner":
                    wide(step + ("a",), wg, step[2], x2T)
                    wide(step + ("A",), wu, step[2], x2T)
                elif kind == "spread":
                    j = step[2]
                    pe.wait_ge(s_rr, n + 1)
                    bk = w_unit(step + ("d",))
                    for c in range(4):
                        ins = nc.tensor.transpose(bk[:, P * c:P * c + P],
                                                  rw[:, n % SUPER, P * (4 * j + c):P * (4 * j + c) + P], ident[:, :])
                    ins.then_inc(s_wmm, 1)
                elif kind == "outer":
                    i = n % SUPER
                    pe.wait_ge(s_hid, FC * (n // SUPER + 1))
                    bk = w_unit(step + ("o",))
                    for c in range(FC):
                        mm(bk[:, 0:D], hid[:, c, P * i:P * i + P], wd[:, c, :], start=(c == 0), stop=False)
                    pe.wait_ge(s_wdve, W_FREE[W_AT[("spread", n, 1, "d")]][1])
                    for c in range(EC):
                        ins = mm(bk[:, 0:D], aT[:, c, :], up[:, c, :], start=False, stop=(c == EC - 1))
                    ins.then_inc(s_7mm, 1)

        def evac_taps(act, own, i):
            if i == 0:
                act.wait_ge(s_xaw, 16 * 2 * NQ)
            act.wait_ge(s_ktm, i + 1)
            if i == NGRP:
                act.wait_ge(s_kw[0], 16)
            src = bank[4 + i % 2][0:HALF, :].rearrange("p (h j) -> p j h", j=HALF)
            i = i % NGRP
            nc.scalar.copy(ktime[:, :, 16 * i:16 * i + 16], src).then_inc(s_kev, 1)
            own.done(s_kev)

        @block.scalar
        def _(act):
            fn = nc.scalar.activation
            own = Steps(act, s_actc)
            for i in range(2 * NQ):
                act.wait_ge(s_xa, i + 1)
                nc.scalar.copy(cA[:, i % 2, i // 2, :], bank[i % 4][:, :]).then_inc(s_xae, 1)
                own.done(s_xae)
                if i == 3:
                    act.wait_ge(s_small_ready, 1)
                    fn(wk_[3], wk_[2], ACT.Sin, scale=-TWO_PI).then_inc(s_small_act, 1)
                    own.done(s_small_act)
                    fn(wk_[4], wk_[2], ACT.Sin, scale=-TWO_PI / 2).then_inc(s_small_act, 1)
                    own.done(s_small_act)
                    act.wait_ge(s_small_ready, 2)
                    fn(wk_[5], wk_[1], ACT.Tanh, scale=0.5).then_inc(s_small_act, 1)
                    own.done(s_small_act)
                    fn(wk_[6], wk_[1], ACT.Exp).then_inc(s_small_act, 1)
                    own.done(s_small_act)
            def sines(g):
                d = g % 2
                act.wait_ge(s_phase, 2 * g + 1)
                own.link(fn(tq[d], tq[d], ACT.Sin, scale=TWO_PI, bias=cols[:, 1:2]))
                act.wait_ge(s_phase, 2 * g + 2)
                own.link(fn(tpc[d], tp[d], ACT.Abs))
                own.link(fn(tpc[d], tpc[d], ACT.Sin, scale=-TWO_PI, bias=cols[:, 4:5]))
                fn(tp[d], tp[d], ACT.Sin, scale=-TWO_PI).then_inc(s_sin, 1)
                own.done(s_sin)

            def decays(g):
                d = g % 2
                act.wait_ge(s_outer, 2 * g + 2)
                own.link(fn(tqm[d], tqm[d], ACT.Exp))
                fn(tpm[d], tpm[d], ACT.Exp).then_inc(s_dec, 1)
                own.done(s_dec)

            for kind, n in order(HEAD, "act"):
                if kind == "simw":
                    for k in range(KC):
                        act.wait_ge(s_cm, 5 + k)
                        nc.scalar.copy(wsim[:, k, :], bank[4 + k][:, :]).then_inc(s_ce, 1)
                        own.done(s_ce)
                elif kind == "values":
                    b, j = divmod(n, PCH // 2)
                    if j == PCH // 2 - 1:
                        act.wait_ge(s_cm, 7 + b)
                        for ch in range(PCH):
                            h0, h1 = heads_of(ch)
                            k = 17 * (h1 - h0 + 1)
                            ins = nc.scalar.copy(vbd[:, b, ch, 0:k], bank[6 + b][:, 51 * ch:51 * ch + k])
                        ins.then_inc(s_ce, 1)
                        own.done(s_ce)
                elif kind == "sines":
                    sines(n)
                elif kind == "decays":
                    decays(n)
                elif kind == "taps":
                    for i in (2 * n, 2 * n + 1):
                        evac_taps(act, own, i)
                elif kind == "x_second":
                    act.wait_ge(s_xf, n + 1)
                    r = slot_of(n, 0)
                    own.link(nc.scalar.copy(xS[:, r, :], bank[2 * (n % 2)][:, :]))
                    nc.scalar.copy(xS[:, image_of(n), :], bank[2 * (n % 2) + 1][:, :]).then_inc(s_xfe, 1)
                    own.done(s_xfe)
                elif kind == "k_first":
                    for i in range(4):
                        h, qh = divmod(i, 2)
                        act.wait_ge(s_ka, 4 * n + i + 1)
                        nc.scalar.copy(kA[n][:, h, 4 * qh:4 * qh + 4, :].rearrange("p a b -> p (a b)"),
                                       bank[6 + i % 2][:, :]).then_inc(s_kae, 1)
                        own.done(s_kae)
                elif kind == "k_second":
                    hf, k1 = divmod(n, FREQ)
                    act.wait_ge(s_kfm, n + 1)
                    r, m = slot_of(k1, 0), image_of(k1)
                    nc.scalar.copy(kS[hf][:, r:m + 1:m - r, :],
                                   bank[6 + k1 % 2][:, 0:2 * HC].rearrange("p (a b) -> p a b", a=2)).then_inc(s_kfe, 1)
                    own.done(s_kfe)
                elif kind == "inverse":
                    hf, k = divmod(n, FREQ)
                    d, planes = n % ZRING, 1 if k in (0, 8) else 2
                    act.wait_ge(s_z, n + 1)
                    if n >= ZRING:
                        act.wait_ge(s_zw[d], 16 * z_writes(n, d))
                    nc.scalar.copy(zring[:, d, 0:planes].rearrange("p a b -> p (a b)"),
                                   bank[n % 4][:, 0:2 * HC * planes]).then_inc(s_ze, 1)
                    own.done(s_ze)
                    r = slot_of(k, 0)
                    act.dma_start(scr_z[hf, r:r + planes].rearrange("r p n -> p r n"),
                                  zring[:, d, 0:planes]).then_inc(s_zw[d], 16)

            def turned(key, out, view):
                u = T_AT[key]
                act.wait_ge(s_tmm, u + 1)
                nc.scalar.copy(out, view(bank[2 + u % 2])).then_inc(s_tev, 1)
                own.done(s_tev)

            def turned_tokens(key, j, dst):
                turned(key, dst[:, :, 2 * P * j:2 * P * j + 2 * P].rearrange("p k (i n) -> p k i n", n=P),
                       lambda bk: bk[:, :].rearrange("p (i k n) -> p k i n", i=2, k=KC))

            def wide_ready(key):
                u = W_AT[key]
                act.wait_ge(*W_DONE[u])
                return w_bank(u)[:, :]

            def normalise(k, tl, s_done, last=True):
                ins = fn(tok[:, tl, :], tok[:, tl, :], ACT.Identity, scale=rstd[:, k, tl:tl + 1],
                         bias=shiftn[:, k, tl:tl + 1])
                if last:
                    ins.then_inc(s_done, 1)
                    own.done(s_done)

            def silu(key, half, src, **bias):
                u = SILU_AT[key]
                if u == 0:
                    act.wait_ge(s_half, 1)
                if u >= 3:
                    act.wait_ge(s_silu, u - 2)
                fn(half, src, ACT.Identity, scale=0.5, **bias)
                fn(thb[:, u % 3, :], src, ACT.Tanh, scale=0.5, **bias).then_inc(s_wact, 1)
                own.done(s_wact)

            for step in order(SCHEDULE, "act"):
                kind, n = step[0], step[1]
                if kind == "conv":
                    src = wide_ready(step + ("a",))
                    nc.scalar.copy(rconv[:, 2 * n:2 * n + 2, :].rearrange("p a b -> p (a b)"), src).then_inc(s_wact, 1)
                    own.done(s_wact)
                elif kind == "turn1":
                    if n:
                        act.wait_ge(*W_DONE[W_AT[("query", n - 1, KC - 1, "a")]])
                    turned_tokens(step, step[2], x1T)
                elif kind == "query":
                    j = step[2]
                    src = wide_ready(step + ("a",))
                    if n:
                        act.wait_ge(s_smm, 2 * SUPER * n)
                    fn(qT[:, j, :], src, ACT.Identity, bias=pcol[:, j:j + 1]).then_inc(s_wact, 1)
                    own.done(s_wact)
                elif kind == "score":
                    act.wait_ge(s_ssub, 2 * n + step[2] + 1)
                    half = prob[:, n % 2, 8 * NKV * step[2]:8 * NKV * (step[2] + 1)]
                    fn(half, half, ACT.Exp).then_inc(s_exp, 1)
                    own.done(s_exp)
                elif kind == "probs":
                    j, u = step[2], T_AT[step]
                    if n:
                        act.wait_ge(s_pv, n)
                    if j < 2:
                        turned(step, pT[:, 4 * j:4 * j + 4, :], lambda bk: bk[:, :].rearrange("p (c n) -> p c n", n=P))
                    else:
                        act.wait_ge(s_tmm, u + 1)
                        own.link(nc.scalar.copy(pT[:, 8, :], bank[2 + u % 2][:, 0:P]))
                        m = FLAT - 9 * P
                        nc.scalar.copy(pT[0:m, 9, :], bank[2 + u % 2][0:m, P:2 * P]).then_inc(s_tev, 1)
                        own.done(s_tev)
                elif kind == "turno":
                    if n >= 2:
                        act.wait_ge(s_wo, n - 1)
                    turned(step, oT[:, n % 2], lambda bk: bk[:, 0:D].rearrange("p (k n) -> p k n", n=P))
                elif kind == "turn2":
                    if n:
                        act.wait_ge(*W_DONE[max(W_AT[("inner", n - 1, FC - 1, "A")], W_AT[("sim", SUPER * n - 1, "a")])])
                    turned_tokens(step, step[2], x2T)
                elif kind == "sim":
                    src = wide_ready(step + ("a",))
                    if n >= 2:
                        act.wait_ge(s_sx, FH * (n - 1))
                        act.wait_ge(s_best, n - 1)
                    nc.scalar.copy(sim[:, n % 2].rearrange("p a b -> p (a b)"), src).then_inc(s_wact, 1)
                    own.done(s_wact)
                elif kind == "expert":
                    c = step[2]
                    src = wide_ready(step + ("a",))
                    if n:
                        act.wait_ge(s_wdve, W_FREE[W_AT[("spread", SUPER * n - 1, 1, "d")]][1])
                    silu(step, silg[:, c, :], src)
                elif kind == "inner":
                    c, m = step[2], FC * n + step[2]
                    src = wide_ready(step + ("a",))
                    if m >= 3:
                        act.wait_ge(s_hid, m - 2)
                    silu(step, gate[:, m % 3, :], src, bias=pcol[:, 4 + c:5 + c])
                    src = wide_ready(step + ("A",))
                    if m >= 2:
                        act.wait_ge(s_hid, m - 1)
                    fn(upb[:, m % 2, :], src, ACT.Identity, bias=pcol[:, 4 + FC + c:5 + FC + c]).then_inc(s_wact, 1)
                    own.done(s_wact)
                elif kind == "best":
                    act.wait_ge(s_zarg, n + 1)
                    fn(zexp, zexp, ACT.Exp).then_inc(s_zexp, 1)
                    own.done(s_zexp)
                elif kind == "norm1":
                    act.wait_ge(s_rstd[1], n + 1)
                    for b in range(B):
                        normalise(1, 2 * n + b, s_x1, b == 1)
                elif kind in ("norm2", "norm3"):
                    k = int(kind[-1])
                    act.wait_ge(s_rstd[k], n + 1)
                    normalise(k, n, s_x2 if k == 2 else s_out)
                elif kind == "first":
                    act.wait_ge(s_rfr, FH * n + 1)
                    if n >= SUPER:
                        act.wait_ge(*W_DONE[W_AT[("spread", n - SUPER, 1, "d")]])
                    nc.scalar.mul(rw[:, n % SUPER, :], ebuf[FH * n % 2].rearrange("p a b -> p (a b)"),
                                  zinv[:, 0:1]).then_inc(s_w0, 1)
                    own.done(s_w0)
                elif kind == "exps":
                    m = FH * n + step[2]
                    act.wait_ge(s_best, n + 1)
                    act.wait_ge(s_sx, m + 1)
                    if m >= 2:
                        act.wait_ge(s_rfr, m - 1)
                    fn(ebuf[m % 2], sxb[m % 2], ACT.Exp, bias=negm[:, n % 2, step[2]:step[2] + 1]).then_inc(s_e, 1)
                    own.done(s_e)

        @block.gpsimd
        def _(pool):
            own = Steps(pool, s_pool)
            tt = nc.gpsimd.tensor_tensor
            pool.wait_ge(s_base, 1)

            def exponents(g):
                d, ch = g % 2, slice(GRP * g, GRP * g + GRP)
                if g >= 2:
                    pool.wait_ge(s_ktm, 2 * (g - 1))
                for dst, a in ((tqm[d], wk_[1]), (tpm[d], wk_[7])):
                    tt(dst, a[:, ch].unsqueeze(2).broadcast_to((P, GRP, HALF)),
                       steps[:, :].unsqueeze(1).broadcast_to((P, GRP, HALF)), ALU.mult).then_inc(s_outer, 1)
                    own.done(s_outer)

            def weigh(g):
                d, ch = g % 2, slice(GRP * g, GRP * g + GRP)
                pool.wait_ge(s_sin, g + 1)
                pool.wait_ge(s_base, 2)
                for dst, a in ((tpc[d], wk_[14]), (tp[d], wk_[9])):
                    tt(dst, dst, a[:, ch].unsqueeze(2).broadcast_to((P, GRP, HALF)), ALU.mult).then_inc(s_wtd, 1)
                    own.done(s_wtd)

            def skip_terms(hf):
                pool.wait_ge(s_kev, NGRP * (hf + 1))
                tt(ktime[0:1, 0, :], skip[0:1, HC * hf:HC * hf + HC], ktime[0:1, 0, :], ALU.add).then_inc(s_kdone, 1)
                own.done(s_kdone)

            def spectra_im(hf, k1):
                m = FREQ * hf + k1
                if hf == 0:
                    pool.wait_ge(s_xfe, k1 + 1)
                pool.wait_ge(s_kfe, m + 1)
                if m == 0:
                    pool.wait_ge(s_ce, 4)
                if m >= 2:
                    pool.wait_ge(s_yf, m - 1)
                xs, planes = spectrum_of_x(k1, hf)
                for c in range(2):
                    ins = tt(pim[:, m % 2, c], xs[:, c],
                             kS[hf][:, planes[1], :].unsqueeze(1).broadcast_to((P, B, HC)), ALU.mult)
                ins.then_inc(s_im, 1)
                own.done(s_im)

            def keys_diagonal():
                pool.wait_ge(s_kt, 2)
                for b in range(B):
                    for oc in range(KC):
                        ins = tt(kbd[:, b, oc, :].rearrange("p (h k) -> p h k", k=NKV),
                                 kT[:, oc, NKV * b:NKV * b + NKV].unsqueeze(1).broadcast_to((P, 8, NKV)),
                                 head_mask[:, :].unsqueeze(2).broadcast_to((P, 8, NKV)), ALU.mult)
                        if (b, oc) == (B - 1, KC - 1):
                            ins.then_inc(s_kbd, 1)
                            own.done(s_kbd)
                        else:
                            own.link(ins)

            for kind, n in order(HEAD, "pool"):
                if kind == "exponents":
                    exponents(n)
                elif kind == "weigh":
                    weigh(n)
                elif kind == "diagonal":
                    own.link(nc.gpsimd.tensor_scalar(skip[:, :], skip[:, :], 1.0, None, ALU.add))
                    keys_diagonal()
                elif kind == "skip":
                    skip_terms(n)
                elif kind == "spectra":
                    spectra_im(*divmod(n, FREQ))
                elif kind == "x_bias":
                    if n == 0:
                        pool.wait_ge(s_xa, 2 * NQ)
                        pool.wait_ge(s_ctx, 16 * 7)
                        nc.gpsimd.tensor_scalar(pcol[:, 4:4 + FC], pcol[:, 4:4 + FC], 0.5, None,
                                                ALU.mult).then_inc(s_half, 1)
                    tt(tok[:, n, :], tok[:, n, :], lnb, ALU.add).then_inc(s_xbr, 1)
                    own.done(s_xbr)

            def deviation(k, tl, n):
                if k:
                    nc.gpsimd.tensor_scalar(shiftn[:, k, tl:tl + n], mv[:, k, tl:tl + n, 0], -1.0, None, ALU.mult)
                own.link(nc.gpsimd.tensor_scalar(vare[:, 0:n], mv[:, k, tl:tl + n, 1], EPS, None, ALU.add))
                ins = tt(rstd[:, k, tl:tl + n], vare[:, 0:n], cols[:, 5:6].broadcast_to((P, n)), ALU.pow)
                if k:
                    own.link(ins)
                    ins = tt(shiftn[:, k, tl:tl + n], shiftn[:, k, tl:tl + n], rstd[:, k, tl:tl + n], ALU.mult)
                ins.then_inc(s_rstd[k], 1)
                own.done(s_rstd[k])

            for step in order(SCHEDULE, "pool"):
                kind, n = step[0], step[1]
                if kind in ("turn1", "turn2"):
                    pool.wait_ge(s_tmm, T_AT[step] + 1)
                    bias, s_added = (bo, s_bo) if kind == "turn1" else (bd, s_bd)
                    for i in range(2):
                        tl = SUPER * n + 2 * step[2] + i
                        tt(tok[:, tl, :], tok[:, tl, :], bias, ALU.add).then_inc(s_added, 1)
                        own.done(s_added)
                elif kind == "sums":
                    h, m = step[2], FH * n + step[2]
                    pool.wait_ge(s_wact, W_FREE[W_AT[("sim", n, "a")]][1])
                    if m >= 2:
                        pool.wait_ge(s_rfr, m - 1)
                    tt(sxb[m % 2], sim[:, n % 2, h, 0:XR].unsqueeze(2).broadcast_to((P, XR, NKEYS)),
                       sim[:, n % 2, FH + h, :].unsqueeze(1).broadcast_to((P, XR, NKEYS)), ALU.add).then_inc(s_sx, 1)
                    own.done(s_sx)
                elif kind in ("dev0", "dev1"):
                    k = int(kind[-1])
                    pool.wait_ge(s_stat[k], n + 1)
                    deviation(k, 2 * n, 2)
                elif kind in ("dev2", "dev3"):
                    k = int(kind[-1])
                    pool.wait_ge(s_stat[k], n + 1)
                    deviation(k, n, 1)

        @block.vector
        def _(dve):
            own = Steps(dve, s_dve)
            link, mark, need = own.link, own.mark, own.need
            V = nc.vector
            tt, ts, stt = V.tensor_tensor, V.tensor_scalar, V.scalar_tensor_tensor
            w = wk_

            def exact_exp(out, x, a, b, c):
                link(ts(a, x, 1.4426950408889634, MAGIC, ALU.mult, ALU.add))
                link(ts(a, a, MAGIC, None, ALU.subtract))
                link(stt(b, a, -0.693359375, x, ALU.mult, ALU.add))
                link(stt(b, a, 2.12194440e-4, b, ALU.mult, ALU.add))
                link(ts(c, b, 1.0 / 40320, None, ALU.mult))
                for k in (5040, 720, 120, 24, 6, 2, 1):
                    link(stt(c, c, 1.0 / k, b, ALU.add, ALU.mult))
                link(ts(a.bitcast(I32), a, 127.0, 8388608.0, ALU.add, ALU.mult))
                link(stt(out, c, 1.0, a, ALU.add, ALU.mult))

            dve.wait_ge(s_ssm, 64)
            logdt, loga, aim, cre, cim = (ssm[:, i, :] for i in range(5))
            exact_exp(w[0], logdt, w[10], w[11], w[12])
            link(tt(w[2], w[0], aim, ALU.mult))
            link(ts(w[2], w[2], 0.15915494309189535, None, ALU.mult))
            link(ts(w[10], w[2], MAGIC, None, ALU.add))
            stt(w[2], w[10], MAGIC, w[2], ALU.subtract, ALU.subtract).then_inc(s_small_ready, 1)
            own.done(s_small_ready)
            exact_exp(w[13], loga, w[10], w[11], w[12])
            link(ts(w[13], w[13], -1.0, None, ALU.mult))
            tt(w[1], w[13], w[0], ALU.mult).then_inc(s_small_ready, 1)
            own.done(s_small_ready)
            link(ts(w[7], w[1], float(HALF), None, ALU.mult))
            link(ts(w[8], w[2], float(HALF), None, ALU.mult))
            link(ts(w[10], w[8], MAGIC, None, ALU.add))
            stt(w[8], w[10], MAGIC, w[8], ALU.subtract, ALU.subtract).then_inc(s_base, 1)
            own.done(s_base)

            def context():
                for oc in range(KC):
                    dve.wait_ge(s_cm, oc + 1)
                    dve.wait_ge(s_ctx, 16 * 7)
                    ts(kT[:, oc, :], bank[4 + oc][:, 0:B * NKV], pcol[:, 2 + oc:3 + oc], HD ** -0.5,
                       ALU.add, ALU.mult).then_inc(s_kt, 1)
                    own.done(s_kt)
                link(V.memset(vaug, 1.0))
                for b in range(B):
                    dve.wait_ge(s_cm, 3 + b)
                    ins = tt(vaug[:, b, :, 0:HD], bank[6 + b][0:NKV, 0:D].rearrange("p (h d) -> p h d", d=HD),
                             bv[0:NKV].rearrange("p (h d) -> p h d", d=HD), ALU.add)
                    if b == 0:
                        link(ins)
                    else:
                        ins.then_inc(s_kbz, 1)
                        own.done(s_kbz)

            def expand(v):
                return v.unsqueeze(2).broadcast_to((P, GRP, HALF))

            tq_, tp_ = tq, tp
            st3 = steps[:, :].unsqueeze(1).broadcast_to((P, GRP, HALF))

            def phases(g):
                tq, tp = tq_[g % 2], tp_[g % 2]
                ch = slice(GRP * g, GRP * g + GRP)
                link(tt(tq, expand(w[2][:, ch]), st3, ALU.mult))
                link(ts(trd, tq, cols[:, 0:1], MAGIC, ALU.add, ALU.add))
                stt(tq, trd, MAGIC, tq, ALU.subtract, ALU.subtract).then_inc(s_phase, 1)
                own.done(s_phase)
                link(tt(tp, expand(w[8][:, ch]), st3, ALU.mult))
                link(ts(trd, tp, MAGIC, None, ALU.add))
                stt(tp, trd, MAGIC, tp, ALU.subtract, ALU.subtract).then_inc(s_phase, 1)
                own.done(s_phase)

            def mode_weights():
                dve.wait_ge(s_small_act, 4)
                sb_, sh, th, ea = w[3], w[4], w[5], w[6]
                link(tt(sh, sh, sh, ALU.mult))
                link(tt(sh, sh, ea, ALU.mult))
                link(ts(w[10], th, -1.0, 1.0, ALU.mult, ALU.add))
                link(V.reciprocal(w[10], w[10]))
                link(tt(w[10], w[10], th, ALU.mult))
                link(tt(w[10], w[10], sh, ALU.subtract))
                link(ts(w[10], w[10], 2.0, None, ALU.mult))
                link(tt(w[11], sb_, ea, ALU.mult))
                link(tt(w[3], w[13], w[13], ALU.mult))
                link(tt(w[4], aim, aim, ALU.mult))
                link(tt(w[3], w[3], w[4], ALU.add))
                link(V.reciprocal(w[3], w[3]))
                link(tt(w[4], w[10], w[13], ALU.mult))
                link(tt(w[5], w[11], aim, ALU.mult))
                link(tt(w[4], w[4], w[5], ALU.add))
                link(tt(w[5], w[11], w[13], ALU.mult))
                link(tt(w[6], w[10], aim, ALU.mult))
                link(tt(w[5], w[5], w[6], ALU.subtract))
                link(tt(w[4], w[4], w[3], ALU.mult))
                link(tt(w[5], w[5], w[3], ALU.mult))
                link(tt(w[10], cre, w[4], ALU.mult))
                link(tt(w[11], cim, w[5], ALU.mult))
                link(tt(w[10], w[10], w[11], ALU.subtract))
                link(tt(w[11], cre, w[5], ALU.mult))
                link(tt(w[12], cim, w[4], ALU.mult))
                link(tt(w[11], w[11], w[12], ALU.add))
                link(ts(w[12], w[11], cols[:, 3:4], None, ALU.mult))
                link(stt(w[14], w[10], cols[:, 2:3], w[12], ALU.mult, ALU.add))
                link(ts(w[12], w[11], cols[:, 2:3], None, ALU.mult))
                stt(w[9], w[10], cols[:, 3:4], w[12], ALU.mult, ALU.subtract).then_inc(s_base, 1)
                own.done(s_base)

            def tables(g):
                d = g % 2
                dve.wait_ge(s_sin, g + 1)
                dve.wait_ge(s_dec, g + 1)
                link(tt(tqm[d], tqm[d], tq[d], ALU.mult))
                dve.wait_ge(s_wtd, 2 * g + 2)
                link(tt(tpc[d], tpc[d], tp[d], ALU.add))
                tt(tpm[d], tpm[d], tpc[d], ALU.mult).then_inc(s_tab, 1)
                own.done(s_tab)

            def spectra(hf, k1):
                m = FREQ * hf + k1
                if hf == 0:
                    dve.wait_ge(s_xfe, k1 + 1)
                dve.wait_ge(s_kfe, m + 1)
                if m == 0:
                    dve.wait_ge(s_ce, 4)
                xs, planes = spectrum_of_x(k1, hf)
                for c in range(2):
                    link(tt(prod[:, 0, c], xs[:, c], kS[hf][:, planes[0], :].unsqueeze(1).broadcast_to((P, B, HC)),
                            ALU.mult))
                dve.wait_ge(s_im, m + 1)
                if m >= 2:
                    dve.wait_ge(s_z, m - 1)
                y = yf[:, m % 2].rearrange("p a (b n) -> p a b n", b=B)
                link(tt(y[:, 0], prod[:, 0, 0], pim[:, m % 2, 1], ALU.subtract))
                tt(y[:, 1], prod[:, 0, 1], pim[:, m % 2, 0], ALU.add).then_inc(s_yf, 1)
                own.done(s_yf)

            phases(0)
            mode_weights()
            context()
            for kind, n in order(HEAD, "dve"):
                if kind == "phases" and n:
                    phases(n)
                elif kind == "tables":
                    tables(n)
                elif kind == "spectra":
                    spectra(*divmod(n, FREQ))

            def statistics(k, tl, src, last):
                link(V.bn_stats(stats[:, tl % 2, :], src))
                ins = V.bn_aggr(mv[:, k, tl, :], stats[:, tl % 2, :])
                if last:
                    ins.then_inc(s_stat[k], 1)
                    own.done(s_stat[k])
                else:
                    link(ins)

            def silu(key, half):
                dve.wait_ge(s_wact, W_FREE[W_AT[key + ("a",)]][1])
                stt(half, thb[:, SILU_AT[key] % 3, :], 1.0, half, ALU.add, ALU.mult).then_inc(s_silu, 1)
                own.done(s_silu)

            for step in order(SCHEDULE, "dve"):
                kind, n = step[0], step[1]
                if kind == "ln":
                    dve.wait_ge(s_wact, W_FREE[W_AT[("conv", n, "a")]][1])
                    for b in range(B):
                        statistics(0, 2 * n + b, rconv[:, 2 * n + b, :], b == 1)
                elif kind == "residual":
                    dve.wait_ge(s_rstd[0], n + 1)
                    dve.wait_ge(s_xbr, 2 * n + 2)
                    for b in range(B):
                        link(stt(gtmp[:, b, :], rconv[:, 2 * n + b, :], mv[:, 0, 2 * n + b, 0:1], lnw,
                                 ALU.subtract, ALU.mult))
                    for b in range(B):
                        tl = 2 * n + b
                        link(stt(tok[:, tl, :], gtmp[:, b, :], rstd[:, 0, tl:tl + 1], tok[:, tl, :], ALU.mult, ALU.add))
                        statistics(1, tl, tok[:, tl, :], b == 1)
                elif kind == "score":
                    hh = step[2]
                    dve.wait_ge(s_smm, 2 * n + hh + 1)
                    if n >= 2:
                        dve.wait_ge(s_tmm, T_AT[("probs", n - 2, 2)] + 1)
                    m = smax[:, 0:8].rearrange("p (a h) -> p a h", a=2)
                    dst = prob[:, n % 2, 8 * NKV * hh:8 * NKV * (hh + 1)].rearrange("p (a h k) -> p a h k", a=2, k=NKV)
                    src = [bank[g][:, 0:GH * NKV].rearrange("p (h k) -> p h k", k=NKV) for g in range(2)]
                    for g in range(2):
                        link(V.tensor_reduce(m[:, g, :], src[g], AX_X, ALU.max))
                    link(tt(dst[:, 0], src[0], m[:, 0, :].unsqueeze(2).broadcast_to((P, GH, NKV)), ALU.subtract))
                    tt(dst[:, 1], src[1], m[:, 1, :].unsqueeze(2).broadcast_to((P, GH, NKV)),
                       ALU.subtract).then_inc(s_ssub, 1)
                    own.done(s_ssub)
                elif kind == "attend":
                    dve.wait_ge(s_pv, n + 1)
                    o3 = bank[4][:, 0:HEADS * (HD + 1)].rearrange("p (h d) -> p h d", d=HD + 1)
                    link(V.reciprocal(rec.unsqueeze(2), o3[:, :, HD:HD + 1]))
                    if n >= 2:
                        dve.wait_ge(s_tmm, T_AT[("turno", n - 2)] + 1)
                    tt(ob[:, n % 2, :].rearrange("p (h d) -> p h d", d=HD), o3[:, :, 0:HD],
                       rec.unsqueeze(2).broadcast_to((P, HEADS, HD)), ALU.mult).then_inc(s_on, 1)
                    own.done(s_on)
                elif kind == "project":
                    dve.wait_ge(s_wo, n + 1)
                    dve.wait_ge(s_bo, n + 1)
                    tt(tok[:, n, :], bank[4][:, 0:D], tok[:, n, :], ALU.add).then_inc(s_u[0], 1)
                    own.done(s_u[0])
                    statistics(2, n, tok[:, n, :], True)
                elif kind == "best":
                    dve.wait_ge(s_wact, W_FREE[W_AT[("sim", n, "a")]][1])
                    tp_ = top[:, n % 2]
                    for m in range(2 * FH):
                        ins = V.max(best[:, m, :], sim[:, n % 2, m, :])
                    link(ins)
                    link(tt(pairs.rearrange("p h (a b) -> p h a b", a=TOPK),
                            best[:, 0:FH, :].unsqueeze(3).broadcast_to((P, FH, TOPK, TOPK)),
                            best[:, FH:2 * FH, :].unsqueeze(2).broadcast_to((P, FH, TOPK, TOPK)), ALU.add))
                    for h in range(FH):
                        ins = V.max(tp_[:, h, :], pairs[:, h, :])
                    link(ins)
                    ts(negm[:, n % 2, :], tp_[:, :, 0], -1.0, None, ALU.mult).then_inc(s_best, 1)
                    own.done(s_best)
                    tt(zexp, tp_, tp_[:, :, 0:1].broadcast_to((P, FH, TOPK)), ALU.subtract).then_inc(s_zarg, 1)
                    own.done(s_zarg)
                elif kind == "pair":
                    h, m = step[2], FH * n + step[2]
                    if h == 0:
                        dve.wait_ge(s_zexp, n + 1)
                        link(V.tensor_reduce(zinv, zexp, AX_X, ALU.add))
                        link(V.reciprocal(zinv, zinv))
                    w_, e = rw[:, n % SUPER, :], ebuf[m % 2].rearrange("p a b -> p (a b)")
                    dve.wait_ge(s_e, m + 1)
                    ins = stt(e, sxb[m % 2].rearrange("p a b -> p (a b)"), top[:, n % 2, h, TOPK - 1:TOPK], e,
                              ALU.is_ge, ALU.mult)
                    if h == 0:
                        ins.then_inc(s_rfr, 1)
                    else:
                        link(ins)
                        if h == 1:
                            dve.wait_ge(s_w0, n + 1)
                        stt(w_, e, zinv[:, h:h + 1], w_, ALU.mult, ALU.add,
                            accum_out=rsum[:, 0:1] if h == FH - 1 else None).then_inc(s_rfr, 1)
                    own.done(s_rfr)
                elif kind == "total":
                    w_ = rw[:, n % SUPER, NEXP - 1:NEXP]
                    link(ts(rsum[:, 1:2], rsum[:, 0:1], -1.0, float(FH), ALU.mult, ALU.add))
                    tt(w_, w_, rsum[:, 1:2], ALU.add).then_inc(s_rr, 1)
                    own.done(s_rr)
                elif kind == "expert":
                    silu(step, silg[:, step[2], :])
                elif kind == "inner":
                    c, m = step[2], FC * n + step[2]
                    silu(step, gate[:, m % 3, :])
                    dve.wait_ge(s_wact, W_FREE[W_AT[step + ("A",)]][1])
                    if n and c == 0:
                        dve.wait_ge(s_7mm, SUPER * n)
                    tt(hid[:, c, :], upb[:, m % 2, :], gate[:, m % 3, :], ALU.mult).then_inc(s_hid, 1)
                    own.done(s_hid)
                elif kind == "spread":
                    j, i, u = step[2], n % SUPER, W_AT[step + ("d",)]
                    dve.wait_ge(*W_DONE[u])
                    if n and j == 0:
                        dve.wait_ge(s_7mm, n)
                    tt(aT[:, 4 * j:4 * j + 4, :], w_bank(u)[:, :].rearrange("p (c n) -> p c n", n=P),
                       silg[:, 4 * j:4 * j + 4, P * i:P * i + P], ALU.mult).then_inc(s_wdve, 1)
                    own.done(s_wdve)
                elif kind == "outer":
                    dve.wait_ge(s_7mm, n + 1)
                    dve.wait_ge(s_bd, n + 1)
                    tt(tok[:, n, :], w_bank(W_AT[step + ("o",)])[:, 0:D], tok[:, n, :], ALU.add).then_inc(s_7f, 1)
                    own.done(s_7f)
                    statistics(3, n, tok[:, n, :], True)


SHAPES = {}


def kernel(**inputs):
    import concourse.bacc as bacc
    from concourse.bass_utils import run_bass_kernel_spmd

    g = {k: np.asarray(v) for k, v in inputs.items()}

    def by_chunk(a):
        return np.ascontiguousarray(a.reshape(-1, P, a.shape[-1]).transpose(1, 0, 2))

    def both(a):
        return np.concatenate([a.T, a.T], axis=0)

    def every(a):
        return np.tile(a[None, :], (P, 1))

    fa, fai, fmat, imat = fourier_constants()
    cols, ident, head_mask, shift, steps = mask_constants()
    x = g["x"].reshape(B, NC, NQ, NS, D).transpose(1, 3, 2, 0, 4).reshape(P, TILES, D)
    ctx = g["ctx_1024"].reshape(B * NKV, D)
    keys = g["L0_ffn_keys"].transpose(3, 2, 0, 1).reshape(NKEYS, 2 * FH, NKEYS)
    arrays = {
        "ssm": np.stack([every(g["L0_attn_log_dt"]), both(g["L0_attn_log_A_real"]), both(g["L0_attn_A_imag"]),
                         both(g["L0_attn_C_re"]), both(g["L0_attn_C_im"])], axis=1),
        "skip": g["L0_attn_D"][None, :],
        "cols": cols, "steps": steps, "fa": fa, "fai": fai, "fmat": fmat, "imat": imat, "x": x,
        "ctxT": by_chunk(ctx.T), "wk": by_chunk(g["L0_xattn_Wk"].T), "wv": by_chunk(g["L0_xattn_Wv"].T),
        "wq": by_chunk(g["L0_xattn_Wq"].T), "wo": by_chunk(g["L0_xattn_Wo"].T),
        "pcol": np.concatenate([v.reshape(-1, P).T for v in (
            g["L0_xattn_bq"], g["L0_xattn_bk"], g["L0_ffn_bg"], g["L0_ffn_bu"])], axis=1),
        "rows": np.stack([every(g[n]) for n in (
            "L0_attn_ln_w", "L0_attn_ln_b", "L0_xattn_bo", "L0_ffn_bd", "L0_xattn_bv")], axis=1),
        "shift": shift, "head_mask": head_mask, "ident": ident,
        "wqf": g["L0_ffn_Wq"].T.reshape(2 * FH, NKEYS, D).transpose(1, 0, 2), "keysT": keys,
        "wg": by_chunk(g["L0_ffn_Wg"]), "wu": by_chunk(g["L0_ffn_Wu"]), "wd": by_chunk(g["L0_ffn_Wd"]),
        "dn": by_chunk(g["L0_ffn_down_embed"].T), "up": by_chunk(g["L0_ffn_up_embed"]),
    }
    arrays = {f"in_{k}": np.ascontiguousarray(v) for k, v in arrays.items()}
    nc = bacc.Bacc("TRN2", target_bir_lowering=False, num_devices=1)
    t = {k[3:]: nc.dram_tensor(k, v.shape, F32, kind="ExternalInput").ap() for k, v in arrays.items()}
    for name, shape in (("scr_x", (NQ, NSLOT, NS, B * D)), ("scr_k", (2, NQ, NSLOT, NS, HC)),
                        ("scr_t", (2, HALF, HALF, HC)), ("scr_z", (2, NSLOT, P, B * HC))):
        t[name] = nc.dram_tensor(name, shape, F32, kind="Internal").ap()
    t["out"] = nc.dram_tensor("out", (P, TILES, D), F32, kind="ExternalOutput").ap()
    build(nc, t)
    r = run_bass_kernel_spmd(nc, [arrays], core_ids=[0])
    out = r.results[0]["out"].reshape(NC, NS, NQ, B, D)
    return np.ascontiguousarray(out.transpose(3, 0, 2, 1, 4).reshape(B, L, D))
```
